# Optimizing a Trainium2 kernel written in Bass

```python
import numpy as np
import jax
import jax.numpy as jnp

def _softmax(x, axis=-1):
    return jax.nn.softmax(x, axis=axis)

def _gelu(x):
    return jax.nn.gelu(x, approximate=True)

def _silu(x):
    return jax.nn.silu(x)

def _sigmoid(x):
    return jax.nn.sigmoid(x)

def _layernorm(x, axis=-1, eps=1e-05):
    m = jnp.mean(x, axis=axis, keepdims=True)
    v = jnp.var(x, axis=axis, keepdims=True)
    return (x - m) / jnp.sqrt(v + eps)

def _scatter_add(tgt, idx, src, axis=0):
    return tgt.at[idx].add(src)

def _segment_sum(src, seg, n):
    return jax.ops.segment_sum(src, seg, n)
kernel_name = 'mk_perceiver_d2_seqx_r8_123c5b'

def setup_inputs(seed: int=0):
    np.random.seed(seed)
    _w = jnp.asarray

    def _rec_inputs():
        import jax
        import jax.numpy as jnp
        _rk = jax.random.key(seed)
        x = -0.0005146 + 1 * jax.random.normal(jax.random.fold_in(_rk, 1), (64, 64, 128), jnp.float32)
        _lenS = 64 - jax.random.randint(jax.random.fold_in(_rk, 7), (64,), 0, max(1, 64 // 4) + 1, jnp.int32)
        _lenS2 = 128 - jax.random.randint(jax.random.fold_in(_rk, 8), (64,), 0, max(1, 128 // 4) + 1, jnp.int32)
        _ctx_768P = jax.random.normal(jax.random.fold_in(_rk, 11), (64, 16, 96), jnp.float32)
        _ctx_768c = jax.random.dirichlet(jax.random.fold_in(_rk, 511), 0.3 * jnp.ones((16,), jnp.float32), (64, 128))
        _ctx_768t = jnp.einsum('bsk,bkd->bsd', _ctx_768c, _ctx_768P)
        _ctx_768t = _ctx_768t * jax.lax.rsqrt(jnp.mean(jnp.square(_ctx_768t)) + 1e-12) * 0.953939
        ctx_768 = -0.00040386 + 0.999972 * (_ctx_768t + 0.3 * jax.random.normal(jax.random.fold_in(_rk, 611), (64, 128, 96), jnp.float32))
        _validS = jnp.arange(64)[None, :] < _lenS[:, None]
        _validS2 = jnp.arange(128)[None, :] < _lenS2[:, None]
        _causal = jnp.tril(jnp.ones((64, 64), dtype=bool))
        mask_BxS2_bk0 = jnp.logical_not(jnp.broadcast_to(_validS2[:, :], (64, 128)))
        return (x, ctx_768, mask_BxS2_bk0)
    x, ctx_768, mask_BxS2_bk0 = _rec_inputs()

    def _L0_xattn_setup():
        import jax, jax.numpy as jnp
        import numpy as np
        DIM_IN, DIM_LAT, DIM_HEAD = (96, 128, 64)
        INNER = max(DIM_LAT, DIM_IN)
        HEADS = INNER // DIM_HEAD
        SCALE = DIM_HEAD ** (-0.5)
        RMS_EPS = 1e-08
        LN_EPS = 1e-05

        def layernorm(x, g, b):
            mu = jnp.mean(x, axis=-1, keepdims=True)
            var = jnp.mean((x - mu) ** 2, axis=-1, keepdims=True)
            return (x - mu) * jax.lax.rsqrt(var + LN_EPS) * g + b

        def rmsnorm(x, gamma):
            norm = jnp.sqrt(jnp.sum(x * x, axis=-1, keepdims=True)) * x.shape[-1] ** (-0.5)
            return x / jnp.maximum(norm, RMS_EPS) * gamma
        key = jax.random.key(seed)
        ks = jax.random.split(key, 12)
        b, n, m = (4, 512, 64)
        x = jax.random.normal(ks[0], (b, n, DIM_IN), jnp.float32)
        latents = jax.random.normal(ks[1], (b, m, DIM_LAT), jnp.float32)
        mask = jax.random.randint(ks[2], (b, n), 0, 2).astype(bool)
        s = lambda k, sh, fan: jax.random.normal(k, sh, jnp.float32) * fan ** (-0.5)
        return {'x': x, 'latents': latents, 'mask': mask, 'ln_x_g': jnp.ones((DIM_IN,), jnp.float32), 'ln_x_b': jnp.zeros((DIM_IN,), jnp.float32), 'ln_l_g': jnp.ones((DIM_LAT,), jnp.float32), 'ln_l_b': jnp.zeros((DIM_LAT,), jnp.float32), 'qn_g': jnp.ones((DIM_HEAD,), jnp.float32), 'kn_g': jnp.ones((DIM_HEAD,), jnp.float32), 'Wq': s(ks[3], (INNER, DIM_LAT), DIM_LAT), 'Wkv': s(ks[4], (2 * INNER, DIM_IN), DIM_IN), 'Wlkv': s(ks[5], (2 * INNER, DIM_LAT), DIM_LAT), 'Wo': s(ks[6], (DIM_LAT, INNER), INNER), 'bo': jnp.zeros((DIM_LAT,), jnp.float32)}
    _L0_xattn_all = _L0_xattn_setup()
    _L0_xattn_in = {k: v for k, v in _L0_xattn_all.items() if k in ('ln_x_g', 'ln_x_b', 'ln_l_g', 'ln_l_b', 'qn_g', 'kn_g', 'Wq', 'Wkv', 'Wlkv', 'Wo', 'bo')}
    del _L0_xattn_all

    def _L0_attn_setup():
        import jax, jax.numpy as jnp
        import numpy as np
        DIM = 128
        key = jax.random.key(seed)
        kx, kw = jax.random.split(key)
        x = jax.random.normal(kx, (4, 256, DIM), dtype=jnp.float32)
        W_qkv = jax.random.normal(kw, (3 * DIM, DIM), dtype=jnp.float32) * DIM ** (-0.5)
        return {'x': x, 'W_qkv': W_qkv}
    _L0_attn_all = _L0_attn_setup()
    _L0_attn_in = {k: v for k, v in _L0_attn_all.items() if k in ('W_qkv',)}
    del _L0_attn_all

    def _L0_ffn_setup():
        import jax, jax.numpy as jnp
        import numpy as np
        B, S, D, H, E = (64, 128, 128, 64, 8)
        EPS = 1e-05
        key = jax.random.key(seed)
        ks = jax.random.split(key, 8)
        x = jax.random.normal(ks[0], (B, S, D), jnp.float32)
        return {'x': x, 'ln_g': jnp.ones((D,), jnp.float32), 'ln_b': jnp.zeros((D,), jnp.float32), 'bn_g': jnp.ones((D,), jnp.float32), 'bn_b': jnp.zeros((D,), jnp.float32), 'bn_mean': jax.random.normal(ks[1], (D,), jnp.float32) * 0.01, 'bn_var': jnp.ones((D,), jnp.float32), 'Wr': jax.random.normal(ks[2], (D, E), jnp.float32) * 0.02, 'br': jnp.zeros((E,), jnp.float32), 'W_down': jax.random.normal(ks[3], (E, D, H), jnp.float32) * 0.02, 'b_down': jnp.zeros((E, H), jnp.float32), 'W_up': jax.random.normal(ks[4], (E, H, D), jnp.float32) * 0.02, 'b_up': jnp.zeros((E, D), jnp.float32)}
    _L0_ffn_all = _L0_ffn_setup()
    _L0_ffn_in = {k: v for k, v in _L0_ffn_all.items() if k in ('ln_g', 'ln_b', 'bn_g', 'bn_b', 'bn_mean', 'bn_var', 'Wr', 'br', 'W_down', 'b_down', 'W_up', 'b_up')}
    del _L0_ffn_all

    def _L1_xattn_setup():
        import jax, jax.numpy as jnp
        import numpy as np
        EMBED_DIM = 128
        Q_DIM = 128
        KV_DIM = 96
        NUM_HEADS = 16
        HEAD_DIM = EMBED_DIM // NUM_HEADS
        SCALE = NUM_HEADS ** (-0.5)

        def _linear_params(key, in_dim, out_dim):
            kw, kb = jax.random.split(key)
            bound = 1.0 / np.sqrt(in_dim)
            W = jax.random.uniform(kw, (in_dim, out_dim), minval=-bound, maxval=bound, dtype=jnp.float32)
            b = jax.random.uniform(kb, (out_dim,), minval=-bound, maxval=bound, dtype=jnp.float32)
            return (W, b)
        key = jax.random.key(seed)
        ks = jax.random.split(key, 8)
        B, N1, N2 = (2, 256, 256)
        query = jax.random.normal(ks[0], (B, N1, Q_DIM), dtype=jnp.float32)
        k_in = jax.random.normal(ks[1], (B, N2, KV_DIM), dtype=jnp.float32)
        v_in = jax.random.normal(ks[2], (B, N2, KV_DIM), dtype=jnp.float32)
        Wq, bq = _linear_params(ks[3], Q_DIM, EMBED_DIM)
        Wk, bk = _linear_params(ks[4], KV_DIM, EMBED_DIM)
        Wv, bv = _linear_params(ks[5], KV_DIM, EMBED_DIM)
        Wo, bo = _linear_params(ks[6], EMBED_DIM, EMBED_DIM)
        return {'query': query, 'key': k_in, 'value': v_in, 'Wq': Wq, 'bq': bq, 'Wk': Wk, 'bk': bk, 'Wv': Wv, 'bv': bv, 'Wo': Wo, 'bo': bo}
    _L1_xattn_all = _L1_xattn_setup()
    _L1_xattn_in = {k: v for k, v in _L1_xattn_all.items() if k in ('Wq', 'bq', 'Wk', 'bk', 'Wv', 'bv', 'Wo', 'bo')}
    del _L1_xattn_all

    def _L1_attn_setup():
        import jax, jax.numpy as jnp
        import numpy as np
        NUM_HEADS = 16
        BLOCK_SIZE = 64
        key = jax.random.key(seed)
        ks = jax.random.split(key, 5)
        B, S, C = (2, 2047, 128)
        return {'x': jax.random.normal(ks[0], (B, S, C), dtype=jnp.float32), 'global_token': jax.random.normal(ks[1], (1, 1, C), dtype=jnp.float32), 'qkv_w': jax.random.normal(ks[2], (3 * C, C), dtype=jnp.float32) * 0.02, 'proj_w': jax.random.normal(ks[3], (C, C), dtype=jnp.float32) * 0.02, 'proj_b': jax.random.normal(ks[4], (C,), dtype=jnp.float32) * 0.02}
    _L1_attn_all = _L1_attn_setup()
    _L1_attn_in = {k: v for k, v in _L1_attn_all.items() if k in ('global_token', 'qkv_w', 'proj_w', 'proj_b')}
    del _L1_attn_all

    def _L1_ffn_setup():
        import jax, jax.numpy as jnp
        import numpy as np
        D_MODEL, D_FF, N_EXPERTS, TOP_K = (128, 256, 8, 2)
        B, S = (2, 256)
        key = jax.random.key(seed)
        ks = jax.random.split(key, 6)
        sd = 1.0 / np.sqrt(D_MODEL)
        sf = 1.0 / np.sqrt(D_FF)
        return {'x': jax.random.normal(ks[0], (B, S, D_MODEL), jnp.float32), 'router_w': jax.random.normal(ks[1], (N_EXPERTS, D_MODEL), jnp.float32) * sd, 'gate_w': jax.random.normal(ks[2], (N_EXPERTS, D_MODEL, D_FF), jnp.float32) * sd, 'gate_b': jnp.zeros((N_EXPERTS, D_FF), jnp.float32), 'up_w': jax.random.normal(ks[3], (N_EXPERTS, D_MODEL, D_FF), jnp.float32) * sd, 'up_b': jnp.zeros((N_EXPERTS, D_FF), jnp.float32), 'down_w': jax.random.normal(ks[4], (N_EXPERTS, D_FF, D_MODEL), jnp.float32) * sf, 'down_b': jnp.zeros((N_EXPERTS, D_MODEL), jnp.float32)}
    _L1_ffn_all = _L1_ffn_setup()
    _L1_ffn_in = {k: v for k, v in _L1_ffn_all.items() if k in ('router_w', 'gate_w', 'gate_b', 'up_w', 'up_b', 'down_w', 'down_b')}
    del _L1_ffn_all
    return {'x': x, 'ctx_768': ctx_768, 'mask_BxS2_bk0': mask_BxS2_bk0, 'L0_xattn_ln_x_g': _L0_xattn_in['ln_x_g'], 'L0_xattn_ln_x_b': _L0_xattn_in['ln_x_b'], 'L0_xattn_ln_l_g': _L0_xattn_in['ln_l_g'], 'L0_xattn_ln_l_b': _L0_xattn_in['ln_l_b'], 'L0_xattn_qn_g': _L0_xattn_in['qn_g'], 'L0_xattn_kn_g': _L0_xattn_in['kn_g'], 'L0_xattn_Wq': _L0_xattn_in['Wq'], 'L0_xattn_Wkv': _L0_xattn_in['Wkv'], 'L0_xattn_Wlkv': _L0_xattn_in['Wlkv'], 'L0_xattn_Wo': _L0_xattn_in['Wo'], 'L0_xattn_bo': _L0_xattn_in['bo'], 'L0_attn_W_qkv': _L0_attn_in['W_qkv'], 'L0_ffn_ln_g': _L0_ffn_in['ln_g'], 'L0_ffn_ln_b': _L0_ffn_in['ln_b'], 'L0_ffn_bn_g': _L0_ffn_in['bn_g'], 'L0_ffn_bn_b': _L0_ffn_in['bn_b'], 'L0_ffn_bn_mean': _L0_ffn_in['bn_mean'], 'L0_ffn_bn_var': _L0_ffn_in['bn_var'], 'L0_ffn_Wr': _L0_ffn_in['Wr'], 'L0_ffn_br': _L0_ffn_in['br'], 'L0_ffn_W_down': _L0_ffn_in['W_down'], 'L0_ffn_b_down': _L0_ffn_in['b_down'], 'L0_ffn_W_up': _L0_ffn_in['W_up'], 'L0_ffn_b_up': _L0_ffn_in['b_up'], 'L1_xattn_Wq': _L1_xattn_in['Wq'], 'L1_xattn_bq': _L1_xattn_in['bq'], 'L1_xattn_Wk': _L1_xattn_in['Wk'], 'L1_xattn_bk': _L1_xattn_in['bk'], 'L1_xattn_Wv': _L1_xattn_in['Wv'], 'L1_xattn_bv': _L1_xattn_in['bv'], 'L1_xattn_Wo': _L1_xattn_in['Wo'], 'L1_xattn_bo': _L1_xattn_in['bo'], 'L1_attn_global_token': _L1_attn_in['global_token'], 'L1_attn_qkv_w': _L1_attn_in['qkv_w'], 'L1_attn_proj_w': _L1_attn_in['proj_w'], 'L1_attn_proj_b': _L1_attn_in['proj_b'], 'L1_ffn_router_w': _L1_ffn_in['router_w'], 'L1_ffn_gate_w': _L1_ffn_in['gate_w'], 'L1_ffn_gate_b': _L1_ffn_in['gate_b'], 'L1_ffn_up_w': _L1_ffn_in['up_w'], 'L1_ffn_up_b': _L1_ffn_in['up_b'], 'L1_ffn_down_w': _L1_ffn_in['down_w'], 'L1_ffn_down_b': _L1_ffn_in['down_b']}

def reference(x, ctx_768, mask_BxS2_bk0, L0_xattn_ln_x_g, L0_xattn_ln_x_b, L0_xattn_ln_l_g, L0_xattn_ln_l_b, L0_xattn_qn_g, L0_xattn_kn_g, L0_xattn_Wq, L0_xattn_Wkv, L0_xattn_Wlkv, L0_xattn_Wo, L0_xattn_bo, L0_attn_W_qkv, L0_ffn_ln_g, L0_ffn_ln_b, L0_ffn_bn_g, L0_ffn_bn_b, L0_ffn_bn_mean, L0_ffn_bn_var, L0_ffn_Wr, L0_ffn_br, L0_ffn_W_down, L0_ffn_b_down, L0_ffn_W_up, L0_ffn_b_up, L1_xattn_Wq, L1_xattn_bq, L1_xattn_Wk, L1_xattn_bk, L1_xattn_Wv, L1_xattn_bv, L1_xattn_Wo, L1_xattn_bo, L1_attn_global_token, L1_attn_qkv_w, L1_attn_proj_w, L1_attn_proj_b, L1_ffn_router_w, L1_ffn_gate_w, L1_ffn_gate_b, L1_ffn_up_w, L1_ffn_up_b, L1_ffn_down_w, L1_ffn_down_b):
    import jax
    import jax.numpy as jnp

    def _L0_xattn_ref(x, latents, mask, ln_x_g, ln_x_b, ln_l_g, ln_l_b, qn_g, kn_g, Wq, Wkv, Wlkv, Wo, bo):
        import jax, jax.numpy as jnp
        import numpy as np
        DIM_IN, DIM_LAT, DIM_HEAD = (96, 128, 64)
        INNER = max(DIM_LAT, DIM_IN)
        HEADS = INNER // DIM_HEAD
        SCALE = DIM_HEAD ** (-0.5)
        RMS_EPS = 1e-08
        LN_EPS = 1e-05

        def layernorm(x, g, b):
            mu = jnp.mean(x, axis=-1, keepdims=True)
            var = jnp.mean((x - mu) ** 2, axis=-1, keepdims=True)
            return (x - mu) * jax.lax.rsqrt(var + LN_EPS) * g + b

        def rmsnorm(x, gamma):
            norm = jnp.sqrt(jnp.sum(x * x, axis=-1, keepdims=True)) * x.shape[-1] ** (-0.5)
            return x / jnp.maximum(norm, RMS_EPS) * gamma
        b, n, _ = x.shape
        m = latents.shape[1]
        xn = layernorm(x, ln_x_g, ln_x_b)
        ln = layernorm(latents, ln_l_g, ln_l_b)
        q = ln @ Wq.T
        kv = jnp.concatenate([xn @ Wkv.T, ln @ Wlkv.T], axis=1)
        k, v = (kv[..., :INNER], kv[..., INNER:])
        split_heads = lambda t: t.reshape(t.shape[0], t.shape[1], HEADS, DIM_HEAD).transpose(0, 2, 1, 3)
        q, k, v = (split_heads(q), split_heads(k), split_heads(v))
        qn = rmsnorm(q, qn_g) * SCALE
        kn = rmsnorm(k, kn_g)
        attn = jnp.einsum('bhid,bhjd->bhij', qn, kn)
        full_mask = jnp.pad(mask, ((0, 0), (0, m)), constant_values=True)
        attn = jnp.where(full_mask[:, None, None, :], attn, -jnp.finfo(attn.dtype).max)
        attn = jax.nn.softmax(attn, axis=-1)
        out = jnp.einsum('bhij,bhjd->bhid', attn, v)
        out = out.transpose(0, 2, 1, 3).reshape(b, m, INNER)
        return out @ Wo.T + bo

    def _L0_attn_ref(x, W_qkv):
        import jax, jax.numpy as jnp
        import numpy as np
        DIM = 128
        qkv = jnp.einsum('bnd,ed->bne', x, W_qkv)
        B, N, _ = qkv.shape
        qkv = qkv.reshape(B, N, 3, DIM).transpose(2, 0, 1, 3)
        q, k, v = (qkv[0], qkv[1], qkv[2])
        scale = DIM ** (-0.5)
        attn = jnp.einsum('bnd,bmd->bnm', q * scale, k)
        attn = jax.nn.softmax(attn, axis=-1)
        out = jnp.einsum('bnm,bmd->bnd', attn, v)
        return out

    def _L0_ffn_ref(x, ln_g, ln_b, bn_g, bn_b, bn_mean, bn_var, Wr, br, W_down, b_down, W_up, b_up):
        import jax, jax.numpy as jnp
        import numpy as np
        B, S, D, H, E = (64, 128, 128, 64, 8)
        EPS = 1e-05
        mu = jnp.mean(x, axis=-1, keepdims=True)
        var = jnp.var(x, axis=-1, keepdims=True)
        z = (x - mu) * jax.lax.rsqrt(var + EPS) * ln_g + ln_b
        z_sent = jnp.mean(z, axis=1)
        z_bn = (z_sent - bn_mean) * jax.lax.rsqrt(bn_var + EPS) * bn_g + bn_b
        probs = jax.nn.softmax(z_bn @ Wr + br, axis=-1)
        idx = jnp.argmax(probs, axis=-1)
        gate = jnp.take_along_axis(probs, idx[:, None], axis=1)[:, 0]
        h = jax.nn.relu(jnp.einsum('bsd,bdh->bsh', z, W_down[idx]) + b_down[idx][:, None, :])
        y = jnp.einsum('bsh,bhd->bsd', h, W_up[idx]) + b_up[idx][:, None, :]
        return y * gate[:, None, None]

    def _L1_xattn_ref(query, key, value, Wq, bq, Wk, bk, Wv, bv, Wo, bo):
        import jax, jax.numpy as jnp
        import numpy as np
        EMBED_DIM = 128
        Q_DIM = 128
        KV_DIM = 96
        NUM_HEADS = 16
        HEAD_DIM = EMBED_DIM // NUM_HEADS
        SCALE = NUM_HEADS ** (-0.5)

        def _linear_params(key, in_dim, out_dim):
            kw, kb = jax.random.split(key)
            bound = 1.0 / np.sqrt(in_dim)
            W = jax.random.uniform(kw, (in_dim, out_dim), minval=-bound, maxval=bound, dtype=jnp.float32)
            b = jax.random.uniform(kb, (out_dim,), minval=-bound, maxval=bound, dtype=jnp.float32)
            return (W, b)
        B, N1, _ = query.shape
        N2 = key.shape[1]
        Q = (query @ Wq + bq).reshape(B, N1, NUM_HEADS, HEAD_DIM).transpose(0, 2, 1, 3)
        K = (key @ Wk + bk).reshape(B, N2, NUM_HEADS, HEAD_DIM).transpose(0, 2, 1, 3)
        V = (value @ Wv + bv).reshape(B, N2, NUM_HEADS, HEAD_DIM).transpose(0, 2, 1, 3)
        att = jnp.einsum('bhqd,bhkd->bhqk', Q, K) * SCALE
        att = jax.nn.softmax(att, axis=-1)
        out = jnp.einsum('bhqk,bhkd->bhqd', att, V)
        out = out.transpose(0, 2, 1, 3).reshape(B, N1, EMBED_DIM)
        return out @ Wo + bo

    def _L1_attn_ref(x, global_token, qkv_w, proj_w, proj_b):
        import jax, jax.numpy as jnp
        import numpy as np
        NUM_HEADS = 16
        BLOCK_SIZE = 64
        B, S, C = x.shape
        H = NUM_HEADS
        D = C // H
        scale = D ** (-0.5)
        g = jnp.broadcast_to(global_token, (B, 1, C))
        xg = jnp.concatenate([g, x], axis=1)
        N = S + 1
        qkv = (xg @ qkv_w.T).reshape(B, N, 3, H, D)
        qkv = jnp.transpose(qkv, (2, 0, 3, 1, 4))
        q, k, v = (qkv[0], qkv[1], qkv[2])
        blk = jnp.arange(N) // BLOCK_SIZE
        mask = blk[:, None] >= blk[None, :]
        attn = jnp.einsum('bhqd,bhkd->bhqk', q, k) * scale
        attn = jnp.where(mask[None, None], attn, -jnp.inf)
        attn = jax.nn.softmax(attn, axis=-1)
        out = jnp.einsum('bhqk,bhkd->bhqd', attn, v)
        out = jnp.transpose(out, (0, 2, 1, 3)).reshape(B, N, C)
        out = out[:, 1:, :]
        return out @ proj_w.T + proj_b

    def _L1_ffn_ref(x, router_w, gate_w, gate_b, up_w, up_b, down_w, down_b):
        import jax, jax.numpy as jnp
        import numpy as np
        D_MODEL, D_FF, N_EXPERTS, TOP_K = (128, 256, 8, 2)
        B, S = (2, 256)
        b, s, d = x.shape
        xf = x.reshape(b * s, d)
        n = xf.shape[0]
        router_logits = xf @ router_w.T
        probs = jax.nn.softmax(router_logits, axis=-1)
        topv, topi = jax.lax.top_k(probs, TOP_K)
        mask = jnp.zeros_like(probs).at[jnp.arange(n)[:, None], topi].set(1.0)
        probs = probs * mask
        probs = probs / (probs.sum(axis=-1, keepdims=True) + 1e-09)
        g = jnp.einsum('nd,edf->nef', xf, gate_w) + gate_b
        u = jnp.einsum('nd,edf->nef', xf, up_w) + up_b
        h = jax.nn.silu(g) * u
        expert_out = jnp.einsum('nef,efd->ned', h, down_w) + down_b
        y = jnp.einsum('ne,ned->nd', probs, expert_out)
        return y.reshape(b, s, d)
    x = x + _L0_xattn_ref(ctx_768, _layernorm(x, axis=-1), mask_BxS2_bk0, L0_xattn_ln_x_g, L0_xattn_ln_x_b, L0_xattn_ln_l_g, L0_xattn_ln_l_b, L0_xattn_qn_g, L0_xattn_kn_g, L0_xattn_Wq, L0_xattn_Wkv, L0_xattn_Wlkv, L0_xattn_Wo, L0_xattn_bo)
    x = x + _L0_attn_ref(_layernorm(x, axis=-1), L0_attn_W_qkv)
    x = x + _L0_ffn_ref(_layernorm(x, axis=-1), L0_ffn_ln_g, L0_ffn_ln_b, L0_ffn_bn_g, L0_ffn_bn_b, L0_ffn_bn_mean, L0_ffn_bn_var, L0_ffn_Wr, L0_ffn_br, L0_ffn_W_down, L0_ffn_b_down, L0_ffn_W_up, L0_ffn_b_up)
    x = x + _L1_xattn_ref(_layernorm(x, axis=-1), ctx_768, ctx_768, L1_xattn_Wq, L1_xattn_bq, L1_xattn_Wk, L1_xattn_bk, L1_xattn_Wv, L1_xattn_bv, L1_xattn_Wo, L1_xattn_bo)
    x = x + _L1_attn_ref(_layernorm(x, axis=-1), L1_attn_global_token, L1_attn_qkv_w, L1_attn_proj_w, L1_attn_proj_b)
    x = x + _L1_ffn_ref(_layernorm(x, axis=-1), L1_ffn_router_w, L1_ffn_gate_w, L1_ffn_gate_b, L1_ffn_up_w, L1_ffn_up_b, L1_ffn_down_w, L1_ffn_down_b)
    return x

_drawn_inputs = setup_inputs


def setup_inputs(seed=0):
    import zlib

    import numpy as np

    out = dict(_drawn_inputs(seed))
    spreads = {'L0_xattn_ln_x_g': (1.0, 0.2),
     'L0_xattn_ln_x_b': (0.0, 0.1),
     'L0_xattn_ln_l_g': (1.0, 0.2),
     'L0_xattn_ln_l_b': (0.0, 0.1),
     'L0_xattn_qn_g': (1.0, 0.2),
     'L0_xattn_kn_g': (1.0, 0.2),
     'L0_xattn_bo': (0.0, 0.1),
     'L0_ffn_ln_g': (1.0, 0.6),
     'L0_ffn_ln_b': (0.0, 0.733),
     'L0_ffn_bn_g': (1.0, 0.6),
     'L0_ffn_bn_b': (0.0, 0.701),
     'L0_ffn_bn_var': (1.0, 0.6),
     'L0_ffn_br': (0.0, 0.1),
     'L0_ffn_b_down': (0.0, 0.64),
     'L0_ffn_b_up': (0.0, 0.1),
     'L1_ffn_gate_b': (0.0, 0.1),
     'L1_ffn_up_b': (0.0, 0.1),
     'L1_ffn_down_b': (0.0, 0.1)}
    factors = {'L0_ffn_bn_mean': 8.0,
     'L0_ffn_W_down': 3.95,
     'L0_ffn_W_up': 3.403,
     'L1_xattn_bq': 15.717,
     'L1_xattn_bk': 64.0,
     'L1_attn_global_token': 8.0}
    for name, (base, spread) in spreads.items():
        noise = np.random.default_rng([zlib.crc32(name.encode()), seed]).standard_normal(out[name].shape)
        drawn = base * np.exp(spread * noise) if base else spread * noise
        out[name] = jnp.asarray(drawn.astype(out[name].dtype))
    for name, factor in factors.items():
        out[name] = (out[name] * factor).astype(out[name].dtype)
    return out
```

```python
from contextlib import ExitStack

import concourse.bass as bass
from concourse import mybir

ALU = mybir.AluOpType
ACT = mybir.ActivationFunctionType
F32 = mybir.dt.float32
BF16 = mybir.dt.bfloat16
U8 = mybir.dt.uint8
AX_X = mybir.AxisListType.X

P = 128
B, S, C = 64, 64, 128
TILES = B * S // P
M, CC = 128, 96
G = 4
GW = G * P
GROUPS = TILES // G
EPS = 1e-5
RMS_EPS = 1e-8
NEG = -1e30
HD0 = 64
NK0 = M + S
HP, HD = 8, 8
SC0 = HD0 ** -0.5
SC1 = C ** -0.5
SC4 = 16 ** -0.5
SC5 = HD ** -0.5
E = 8
H0 = 64
CH0 = E * H0 // P
FC = 2
PAIR_TURNS = TILES // 2
GROUP_TURNS = GROUPS // 2

LNX_G, LNX_B, LNL_G, LNL_B, QN_G, KN_G, FLN_G, FLN_B, BN_G, BN_B, BN_M, BN_V, BQ4, BK4, GTOK = range(15)
BDOWN = 15
GATE_B = BDOWN + CH0
UP_B = GATE_B + E * FC
NCOLS = UP_B + E * FC
BO0, BV4, BO4, BO5 = range(4)


def perceiver_kernel(nc, x, ctx, ctxT, mask, cols, rows, br, iota8, ident, headmask, sel2, qneg, e64, esel,
                     w_kv0, w_qkv0, w_o0, w_qkv1, w_r2, w_down2, w_up2, b_up2,
                     w_q4, w_k4, w_v4, w_o4, w_qkv5, w_o5, w_r6, w_gate6, w_up6, w_down6, b_down6, out):
    with ExitStack() as stack:
        def sb(name, shape, dt=F32):
            return stack.enter_context(nc.sbuf_tensor(name, shape, dt))

        def sem(name):
            return stack.enter_context(nc.semaphore(name))

        def two(name):
            return [sem(f"{name}_{s}") for s in range(2)]

        bank = [[stack.enter_context(nc.psum_tensor(f"bank{s}{i}", [P, 512], F32)) for i in range(2)] for s in range(2)]
        wide = [stack.enter_context(nc.psum_tensor(f"wide{s}", [P, 2, 512], F32)) for s in range(2)]

        x_sb = sb("x_sb", [P, TILES * C])
        ctx_sb = sb("ctx_sb", [P, B * CC])
        feat_T = sb("feat_T", [P, TILES * P])
        stats = sb("stats", [P, TILES * 6])
        cstats = sb("cstats", [P, B * 6])
        mean = sb("mean", [P, TILES])
        rstd = sb("rstd", [P, TILES])
        cmean = sb("cmean", [P, B])
        crstd = sb("crstd", [P, B])
        st_a = sb("st_a", [P, B])
        st_b = sb("st_b", [P, B])
        st_c = sb("st_c", [P, B])
        st_d = sb("st_d", [P, B])
        st_v = sb("st_v", [P, B])
        neg_half = sb("neg_half", [P, B])
        cols_sb = sb("cols_sb", [P, NCOLS])
        rows_sb = sb("rows_sb", [P, 4, C])
        br_sb = sb("br_sb", [B, E])
        iota_sb = sb("iota_sb", [P, E])
        id_sb = sb("id_sb", [P, P])
        hm_sb = sb("hm_sb", [P, 2 * HP])
        sel2_sb = sb("sel2_sb", [2, P], BF16)
        qneg_sb = sb("qneg_sb", [1, P], BF16)
        e64_sb = sb("e64_sb", [1, 4 * (S + 1)], BF16)
        esel_sb = sb("esel_sb", [E, E * H0])
        mask_sb = sb("mask_sb", [2, TILES * M], U8)
        mneg = sb("mneg", [2, TILES * M], BF16)
        wkv0 = sb("wkv0", [CC, 2 * C])
        wqkv0 = sb("wqkv0", [P, 3 * C])
        wo0 = sb("wo0", [P, C])
        wqkv1 = sb("wqkv1", [P, 3 * C])
        wr2 = sb("wr2", [P, E])
        wdown2 = sb("wdown2", [P, E * H0])
        wup2 = sb("wup2", [P, CH0, C])
        bup2 = sb("bup2", [E, C])
        wq4 = sb("wq4", [P, C])
        wk4 = sb("wk4", [CC, C])
        wv4 = sb("wv4", [CC, C])
        wo4 = sb("wo4", [P, 2, C])
        wqkv5 = sb("wqkv5", [P, 3 * C])
        wo5 = sb("wo5", [P, 2, C])
        wr6 = sb("wr6", [P, E])
        wgate6 = sb("wgate6", [P, E * FC, P])
        wup6 = sb("wup6", [P, E * FC, P])
        wdown6 = sb("wdown6", [P, E * FC, C])
        bdown6 = sb("bdown6", [E, C])
        gq0 = sb("gq0", [P, 1])
        bq4s = sb("bq4s", [P, 1])

        def col(i):
            return cols_sb[:, i:i + 1]

        def pairs(name, shape, dt=F32):
            return [sb(f"{name}{s}", shape, dt) for s in range(2)]

        xn = pairs("xn", [P, G, C])
        xT = pairs("xT", [P, GW])
        xb = pairs("xb", [P, C])
        probs = pairs("probs", [P, HP, P])
        probsT = pairs("probsT", [P, HP, P])
        big = pairs("big", [P, 2, 2 * HP, S])
        sm = pairs("sm", [P, 64])
        sm2 = pairs("sm2", [P, 64])
        sm3 = pairs("sm3", [P, 64])

        loaded = sem("loaded")
        consts = sem("consts")
        vec = sem("vec")
        stat_var = sem("stat_var")
        stat_rstd = sem("stat_rstd")
        x_done = sem("x_done")
        block = stack.enter_context(nc.Block())

        loads = [(x_sb[:, :].rearrange("p (t c) -> p t c", c=C), x), (ctx_sb[:, :].rearrange("p (b c) -> p b c", c=CC), ctx),
                 (cols_sb[:, :], cols), (rows_sb[:, :, :], rows), (br_sb[:, :], br), (iota_sb[:, :], iota8),
                 (id_sb[:, :], ident), (hm_sb[:, :], headmask), (sel2_sb[:, :], sel2), (qneg_sb[:, :], qneg),
                 (e64_sb[:, :], e64), (esel_sb[:, :], esel), (mask_sb[:, :], mask), (wkv0[:, :], w_kv0),
                 (wqkv0[:, :], w_qkv0), (wo0[:, :], w_o0)]
        later = [(wqkv1[:, :], w_qkv1), (wr2[:, :], w_r2), (wdown2[:, :], w_down2), (wup2[:, :, :], w_up2),
                 (bup2[:, :], b_up2), (wq4[:, :], w_q4), (wk4[:, :], w_k4), (wv4[:, :], w_v4), (wo4[:, :, :], w_o4),
                 (wqkv5[:, :], w_qkv5), (wo5[:, :, :], w_o5), (wr6[:, :], w_r6), (wgate6[:, :, :], w_gate6),
                 (wup6[:, :, :], w_up6), (wdown6[:, :, :], w_down6), (bdown6[:, :], b_down6)]
        LOADED = 16 * len(loads)
        loaded_later = sem("loaded_later")
        LATER = 16 * len(later)

        lnT = [xT[s][:, 0:P] for s in range(2)]
        cnT = [xT[s][:, P:3 * P] for s in range(2)]
        qT0 = [xT[s][:, 3 * P:4 * P] for s in range(2)]
        flat = [[t[s][:, :, :].rearrange("p a b -> p (a b)") for s in range(2)] for t in (probs, probsT)]
        bigf = [big[s][:, :, :, :].rearrange("p a b c -> p (a b c)") for s in range(2)]
        p0 = [flat[0][s][:, 0:2 * NK0].rearrange("p (h k) -> p h k", h=2) for s in range(2)]
        kT0 = [flat[0][s][:, 512:896] for s in range(2)]
        oT0 = [flat[0][s][:, 896:1024] for s in range(2)]
        pT0 = [flat[1][s][:, 0:512] for s in range(2)]
        vc = [flat[1][s][:, 512:768] for s in range(2)]
        vl = [flat[1][s][:, 768:1024] for s in range(2)]
        qk0 = [bigf[s][:, 0:512] for s in range(2)]
        sq = [bigf[s][:, 512:1024] for s in range(2)]
        bq = [flat[0][s][:, 0:512] for s in range(2)]
        bk = [flat[0][s][:, 512:1024] for s in range(2)]
        bv = [flat[1][s][:, 0:512] for s in range(2)]
        bpT = [flat[1][s][:, 512:1024] for s in range(2)]
        pbd = [bigf[s][:, 0:512] for s in range(2)]
        bsub = [bigf[s][:, 512:768] for s in range(2)]
        zsum = sb("zsum", [P, B])
        zbn = sb("zbn", [P, B])
        rt = sb("rt", [P, 8])
        rt64 = sb("rt64", [B, 4])
        lg = sb("lg", [B, E])
        lg2 = sb("lg2", [B, E])
        ex = sb("ex", [B, E])
        pick = sb("pick", [B, E])
        coef = sb("coef", [B, E])
        coefT = sb("coefT", [E, B])
        cspr = sb("cspr", [P, CH0 * B])
        hr = [bigf[s].rearrange("p (c n) -> p c n", c=CH0) for s in range(2)]
        ctok = [flat[0][s][0:E, 0:GW] for s in range(2)]
        ctxT_s = pairs("ctxT_s", [CC, 2 * M])
        kT4 = pairs("kT4", [P, 2 * M])
        vaug = pairs("vaug", [P, 2, HP, 17])
        on4 = pairs("on4", [P, P])
        oT4 = pairs("oT4", [P, 2, P])
        mst = pairs("mst", [2, M], BF16)
        xg = pairs("xg", [P, 2, S + 1])
        rl_all = sb("rl_all", [P, TILES * E])
        route = [sb(f"route{i}", [P, TILES * E]) for i in range(5)]
        r_l0 = rl_all[:, :].rearrange("p (t e) -> p t e", e=E)
        r_1, r_2, r_3, r_e, r_l = [r[:, :].rearrange("p (t e) -> p t e", e=E) for r in route]
        r_3f = route[2]
        wst = sb("wst", [P, G * E])
        wTs = flat[1][0][0:E, 0:GW]
        sg = [flat[0][0][:, 0:512], flat[0][0][:, 512:1024]]
        hf = [flat[0][1][:, 0:512], flat[0][1][:, 512:1024]]
        yacc = xn[0]

        a_normed, a_turned, a_lnT, a_proj, a_sq = sem("a_normed"), sem("a_turned"), sem("a_lnT"), sem("a_proj"), sem("a_sq")
        a_ss, a_ssm, a_rk, a_qkn, a_qkT = sem("a_ss"), sem("a_ssm"), sem("a_rk"), sem("a_qkn"), sem("a_qkT")
        a_qTs, a_scores, a_nmx, a_exp = sem("a_qTs"), sem("a_scores"), sem("a_nmx"), sem("a_exp")
        a_rden, a_pn, a_pT, a_pTs = sem("a_rden"), sem("a_pn"), sem("a_pT"), sem("a_pTs")
        a_oT, a_oTs, a_y, a_xb, a_upd = sem("a_oT"), sem("a_oTs"), sem("a_y"), sem("a_xb"), sem("a_upd")
        b_normed, b_turned, b_xT, b_qk, b_v = sem("b_normed"), sem("b_turned"), sem("b_xT"), sem("b_qk"), sem("b_v")
        b_q, b_kv, b_scores, b_nmx, b_sub = sem("b_q"), sem("b_kv"), sem("b_scores"), sem("b_nmx"), sem("b_sub")
        b_exp, b_den, b_rden, b_pT, b_pTs, b_o, b_upd = (sem("b_exp"), sem("b_den"), sem("b_rden"), sem("b_pT"),
                                                         sem("b_pTs"), sem("b_o"), sem("b_upd"))
        b_zero = sem("b_zero")
        c_normed, c_turned, c_z = sem("c_normed"), sem("c_turned"), sem("c_z")
        c_zsum, c_route, c_logits, c_exp, c_coef = sem("c_zsum"), sem("c_route"), sem("c_logits"), sem("c_exp"), sem("c_coef")
        c_coefT, c_spread, c_spread_s = sem("c_coefT"), sem("c_spread"), sem("c_spread_s")
        c_tok, c_h, c_relu, c_hm, c_y, c_upd = sem("c_tok"), sem("c_h"), sem("c_relu"), sem("c_hm"), sem("c_y"), sem("c_upd")
        d_ctx, d_normed, d_turned, d_xT, d_proj, d_qk = (two("d_ctx"), sem("d_normed"), sem("d_turned"), sem("d_xT"),
                                                         sem("d_proj"), sem("d_qk"))
        d_v, d_qm, d_scores, d_nmx, d_sub, d_exp = (sem("d_v"), sem("d_qm"), sem("d_scores"), sem("d_nmx"),
                                                    sem("d_sub"), sem("d_exp"))
        d_pT, d_pTs, d_o, d_rden, d_on, d_oT, d_oTs = (sem("d_pT"), sem("d_pTs"), sem("d_o"), sem("d_rden"),
                                                       sem("d_on"), sem("d_oT"), sem("d_oTs"))
        d_y, d_xb, d_upd = sem("d_y"), sem("d_xb"), sem("d_upd")
        d_ones, d_gtok, d_bq = sem("d_ones"), sem("d_gtok"), sem("d_bq")
        f_normed, f_turned, f_xT, f_logits = sem("f_normed"), sem("f_turned"), sem("f_xT"), sem("f_logits")
        f_logits_s, f_vec, f_exp, f_w = sem("f_logits_s"), sem("f_vec"), sem("f_exp"), sem("f_w")
        f_wst, f_wT, f_wTs, f_yb, f_acc0 = sem("f_wst"), sem("f_wT"), sem("f_wTs"), sem("f_yb"), sem("f_acc0")
        f_gu, f_silu, f_h, f_down, f_acc, f_upd = (sem("f_gu"), sem("f_silu"), sem("f_h"), sem("f_down"), sem("f_acc"),
                                                   sem("f_upd"))
        stored = sem("stored")

        st = stats[:, :].rearrange("p (t k) -> p t k", k=6)
        cst = cstats[:, :].rearrange("p (t k) -> p t k", k=6)
        KX = S + 1

        def xt(tile, n=1):
            return x_sb[:, bass.ds(tile * C, n * C)]

        def spread(ap, n):
            return ap.unsqueeze(len(ap.shape)).to_broadcast(list(ap.shape) + [n])

        @block.sync
        def _(sp):
            for dst, src in loads:
                sp.dma_start(dst, src).then_inc(loaded, 16)
            for dst, src in later:
                sp.dma_start(dst, src).then_inc(loaded_later, 16)
            for s in range(2):
                sp.dma_start(ctxT_s[s][:, :], ctxT[:, s * 2 * M:(s + 1) * 2 * M]).then_inc(d_ctx[s], 16)
            with sp.Fori(1, PAIR_TURNS) as t:
                for s in range(2):
                    sp.wait_ge(d_proj, 2 * t + s - 1)
                    sp.dma_start(ctxT_s[s][:, :], ctxT[:, bass.ds((2 * t + s) * 2 * M, 2 * M)]).then_inc(d_ctx[s], 16)
            with sp.Fori(0, GROUPS) as g:
                sp.wait_ge(f_upd, g + 1)
                sp.dma_start(out[:, bass.ds(g * G, G), :],
                             xt(g * G, G).rearrange("p (t c) -> p t c", c=C)).then_inc(stored, 16)
            sp.wait_ge(stored, 16 * GROUPS)

        @block.gpsimd
        def _(pool):
            nc.gpsimd.memset(neg_half[:, :], -0.5).then_inc(consts, 1)
            pool.wait_ge(consts, 1)

            def power(n, dst, width):
                pool.wait_ge(stat_var, n)
                nc.gpsimd.tensor_tensor(dst, st_v[:, 0:width], neg_half[:, 0:width], ALU.pow).then_inc(stat_rstd, 1)

            pool.wait_ge(loaded_later, LATER)
            power(1, rstd[:, :], TILES)
            power(2, crstd[:, :], B)

            with pool.Fori(0, PAIR_TURNS) as t:
                for s in range(2):
                    tile = 2 * t + s
                    pool.wait_ge(a_normed, 2 * t + s + 1)
                    nc.gpsimd.tensor_tensor(xb[s][:, :], xt(tile), rows_sb[:, BO0, :], ALU.add).then_inc(a_xb, 1)
                for s in range(2):
                    pool.wait_ge(a_ssm, 2 * t + s + 1)
                    nc.gpsimd.tensor_tensor(sm[s][:, 16:24], sm[s][:, 8:16], neg_half[:, 0:8],
                                            ALU.pow).then_inc(a_rk, 1)
            power(3, rstd[:, :], TILES)
            for s in range(2):
                nc.gpsimd.memset(pbd[s], 0.0).then_inc(b_zero, 1)
            power(4, rstd[:, :], TILES)
            pool.wait_ge(c_route, 1)
            nc.gpsimd.tensor_tensor(rt[:, 1:2], rt[:, 0:1], neg_half[:, 0:1], ALU.pow).then_inc(c_exp, 1)
            pool.wait_ge(c_spread_s, 1)
            with pool.Fori(0, GROUP_TURNS) as t:
                for s in range(2):
                    g = 2 * t + s
                    pool.wait_ge(c_h, 2 * CH0 * t + s + 1)
                    nc.gpsimd.tensor_copy(ctok[s].rearrange("p (b q) -> p b q", q=S),
                                          spread(coefT[:, bass.ds(g * 2 * G, 2 * G)], S)).then_inc(c_tok, 1)

            for k, bo, n in ((0, BO4, 5), (1, BO5, 6)):
                power(n, rstd[:, :], TILES)
                if k == 0:
                    for s in range(2):
                        nc.gpsimd.memset(vaug[s][:, :, :, 16:17], 1.0).then_inc(d_ones, 1)
                        nc.gpsimd.memset(on4[s][:, HP * HD:P], 0.0).then_inc(d_ones, 1)
                with pool.Fori(k * PAIR_TURNS, (k + 1) * PAIR_TURNS) as t:
                    for s in range(2):
                        tile = 2 * (t - k * PAIR_TURNS) + s
                        pool.wait_ge(d_normed, 2 * t + s + 1)
                        nc.gpsimd.tensor_tensor(xb[s][:, :], xt(tile), rows_sb[:, bo, :], ALU.add).then_inc(d_xb, 1)
                    for b in range(2):
                        for s in range(2):
                            pool.wait_ge(d_qk, 4 * t + 2 * s + 1)
                            nc.gpsimd.tensor_tensor(
                                big[s][:, b, :, :],
                                xT[s][:, 256 + b * S:256 + (b + 1) * S].unsqueeze(1).to_broadcast([P, 2 * HP, S]),
                                spread(hm_sb[:, :], S), ALU.mult).then_inc(d_qm, 1)
            power(7, rstd[:, :], TILES)

        @block.scalar
        def _(act):
            ID, SQ, EXP = ACT.Identity, ACT.Square, ACT.Exp
            act.wait_ge(loaded, LOADED)
            act.wait_ge(loaded_later, LATER)
            act.wait_ge(vec, 2)
            with act.Fori(0, PAIR_TURNS) as t:
                for s in range(2):
                    T = bank[s][0]
                    act.wait_ge(a_turned, 2 * t + s + 1)
                    nc.scalar.activation(lnT[s], T[:, 0:P], ID, bias=col(LNL_B), scale=col(LNL_G))
                    nc.scalar.activation(cnT[s][0:CC, :], T[0:CC, P:3 * P], ID, bias=cols_sb[0:CC, LNX_B:LNX_B + 1],
                                         scale=cols_sb[0:CC, LNX_G:LNX_G + 1]).then_inc(a_lnT, 1)
                for s in range(2):
                    act.wait_ge(a_proj, 2 * t + s + 1)
                    nc.scalar.activation(sq[s][:, 0:256], wide[s][:, 1, 0:256], SQ)
                    nc.scalar.activation(sq[s][:, 256:512].rearrange("p (b k) -> p b k", b=2),
                                         wide[s][:, 0, :].rearrange("p (b k) -> p b k", b=2)[:, :, 0:P],
                                         SQ).then_inc(a_sq, 1)
                for s in range(2):
                    act.wait_ge(a_qkT, 2 * t + s + 1)
                    nc.scalar.activation(qT0[s], bank[s][0][:, 0:P], ID, scale=gq0[:, 0:1])
                    nc.scalar.activation(kT0[s], bank[s][0][:, P:4 * P], ID).then_inc(a_qTs, 1)
                for s in range(2):
                    act.wait_ge(a_nmx, 2 * t + s + 1)
                    for h in range(2):
                        ins = nc.scalar.activation(p0[s][:, h, :], (bank[s][1], wide[s][:, 0, :])[h][:, 0:NK0], EXP,
                                                   bias=sm[s][:, 24 + h:25 + h], scale=1.0,
                                                   accum_out=sm[s][:, 26 + h:27 + h])
                    ins.then_inc(a_exp, 1)
                for s in range(2):
                    act.wait_ge(a_pT, 2 * t + s + 1)
                    nc.scalar.activation(pT0[s][:, 0:2 * P], bank[s][0][:, 0:2 * P], ID)
                    nc.scalar.activation(pT0[s][0:S, 2 * P:4 * P], bank[s][0][0:S, 2 * P:4 * P], ID).then_inc(a_pTs, 1)
                for s in range(2):
                    act.wait_ge(a_oT, 2 * t + s + 1)
                    nc.scalar.activation(oT0[s], wide[s][:, 0, 0:P], ID).then_inc(a_oTs, 1)

            act.wait_ge(b_zero, 2)
            with act.Fori(0, GROUP_TURNS) as t:
                for s in range(2):
                    act.wait_ge(b_turned, 2 * t + s + 1)
                    nc.scalar.activation(xT[s][:, :], bank[s][0][:, :], ID).then_inc(b_xT, 1)
                for s in range(2):
                    act.wait_ge(b_qk, 2 * t + s + 1)
                    nc.scalar.activation(bq[s], wide[s][:, 0, :], ID, scale=SC1).then_inc(b_q, 1)
                for s in range(2):
                    act.wait_ge(b_sub, 2 * t + s + 1)
                    for b in range(2):
                        half = slice(b * S, (b + 1) * S)
                        ins = nc.scalar.activation(pbd[s].rearrange("p (j k) -> p j k", k=P)[half, :, half],
                                                   bsub[s].rearrange("p (j k) -> p j k", k=S)[half, :, :], EXP)
                    ins.then_inc(b_exp, 1)
                for s in range(2):
                    act.wait_ge(b_pT, 2 * t + s + 1)
                    nc.scalar.activation(bpT[s], wide[s][:, 1, :], ID).then_inc(b_pTs, 1)

            with act.Fori(0, GROUP_TURNS) as t:
                for s in range(2):
                    act.wait_ge(c_turned, 2 * t + s + 1)
                    nc.scalar.activation(feat_T[:, bass.ds((2 * t + s) * GW, GW)], bank[s][0][:, :], ID,
                                         bias=col(FLN_B), scale=col(FLN_G)).then_inc(c_z, 1)
            act.wait_ge(c_route, 2)
            nc.scalar.activation(ex[:, :], lg2[:, :], EXP, accum_out=rt64[:, 2:3]).then_inc(c_exp, 1)
            with act.Fori(0, GROUP_TURNS) as t:
                for c in range(CH0):
                    for s in range(2):
                        act.wait_ge(c_h, 2 * (CH0 * t + c) + s + 1)
                        nc.scalar.activation(hr[s][:, c, :], bank[s][c % 2][:, :], ACT.Relu,
                                             bias=col(BDOWN + c)).then_inc(c_relu, 1)

            act.wait_ge(d_bq, 1)
            act.wait_ge(d_gtok, 2)
            for k in range(2):
                keys = (M, KX)[k]
                with act.Fori(k * PAIR_TURNS, (k + 1) * PAIR_TURNS) as t:
                    for s in range(2):
                        act.wait_ge(d_turned, 2 * t + s + 1)
                        if k == 0:
                            nc.scalar.activation(xT[s][:, 0:P], bank[s][0][:, 0:P], ID).then_inc(d_xT, 1)
                        else:
                            nc.scalar.activation(xg[s][:, :, 1:KX],
                                                 bank[s][0][:, 0:P].rearrange("p (b q) -> p b q", b=2),
                                                 ID).then_inc(d_xT, 1)
                    for s in range(2):
                        act.wait_ge(d_proj, 2 * t + s + 1)
                        if k == 0:
                            nc.scalar.activation(xT[s][:, 256:384], bank[s][1][:, 0:P], ID, bias=bq4s[:, 0:1],
                                                 scale=SC4).then_inc(d_qk, 1)
                            nc.scalar.activation(kT4[s][:, 0:2 * keys], bank[s][1][:, P:P + 2 * keys], ID,
                                                 bias=col(BK4)).then_inc(d_qk, 1)
                        else:
                            nc.scalar.activation(xT[s][:, 256:384], bank[s][1][:, 0:P], ID, scale=SC5).then_inc(d_qk, 1)
                            nc.scalar.activation(kT4[s][:, 0:2 * keys], bank[s][1][:, P:P + 2 * keys],
                                                 ID).then_inc(d_qk, 1)
                    for b in range(2):
                        for s in range(2):
                            act.wait_ge(d_sub, 4 * t + 2 * b + s + 1)
                            nc.scalar.activation(probs[s][:, :, 0:keys], probs[s][:, :, 0:keys], EXP).then_inc(d_exp, 1)
                        for s in range(2):
                            for half in range(2):
                                act.wait_ge(d_pT, 8 * t + 4 * b + 2 * s + half + 1)
                                nc.scalar.activation(
                                    probsT[s][0:keys, 4 * half:4 * half + 4, :],
                                    bank[s][half][0:keys, :].rearrange("p (h q) -> p h q", q=P),
                                    ID).then_inc(d_pTs, 1)
                        for s in range(2):
                            act.wait_ge(d_oT, 4 * t + 2 * b + s + 1)
                            nc.scalar.activation(oT4[s][:, b, :], bank[s][0][:, 0:P], ID).then_inc(d_oTs, 1)

            with act.Fori(0, GROUP_TURNS) as t:
                for s in range(2):
                    act.wait_ge(f_turned, 2 * t + s + 1)
                    nc.scalar.activation(xT[s][:, :], bank[s][0][:, :], ID).then_inc(f_xT, 1)
                    nc.scalar.activation(feat_T[:, bass.ds((2 * t + s) * GW, GW)], bank[s][0][:, :],
                                         ID).then_inc(f_xT, 1)
            act.wait_ge(f_vec, 2)
            nc.scalar.activation(r_e, r_l, EXP).then_inc(f_exp, 1)
            with act.Fori(0, GROUPS) as g:
                act.wait_ge(f_wT, g + 1)
                nc.scalar.activation(wTs, wide[1][0:E, 0, :], ID).then_inc(f_wTs, 1)
                for k in range(E * FC):
                    act.wait_ge(f_gu, E * FC * g + k + 1)
                    nc.scalar.activation(sg[k % 2], bank[k % 2][0][:, :], ACT.Silu,
                                         bias=col(GATE_B + k)).then_inc(f_silu, 1)

        @block.vector
        def _(dve):
            SUB, MUL, ADD, MAX = ALU.subtract, ALU.mult, ALU.add, ALU.max
            v = nc.vector
            done = [0]

            def link(ins):
                done[0] += 1
                ins.then_inc(vec, 1)
                dve.wait_ge(vec, done[0])

            def variance(src, mean_dst, n, a, b):
                link(v.tensor_tensor(st_a[:, 0:n], src[:, :, 1], src[:, :, 4], ADD))
                link(v.tensor_scalar(mean_dst, st_a[:, 0:n], 0.5, None, MUL))
                link(v.tensor_tensor(st_b[:, 0:n], src[:, :, 1], src[:, :, 4], SUB))
                link(v.tensor_tensor(st_c[:, 0:n], src[:, :, 2], src[:, :, 5], ADD))
                link(v.scalar_tensor_tensor(st_d[:, 0:n], st_b[:, 0:n], 0.25, st_b[:, 0:n], MUL, MUL))
                width = C if n == TILES else CC
                link(v.scalar_tensor_tensor(st_a[:, 0:n], st_c[:, 0:n], 1.0 / width, st_d[:, 0:n], MUL, ADD))
                done[0] += 1
                v.tensor_scalar(st_v[:, 0:n], st_a[:, 0:n], a, b, MUL, ADD).then_inc(vec, 1)
                dve.wait_ge(vec, done[0])
                v.tensor_scalar(st_a[:, 0:1], st_v[:, 0:1], 1.0, None, MUL).then_inc(stat_var, 1)

            TWICE = (1.0 + EPS, EPS * EPS)
            ONCE = (1.0, EPS)

            def normalise(dst, tile, n, normed):
                for j in range(n):
                    ins = v.tensor_scalar(dst[:, j, :], xt(tile + j), mean[:, bass.ds(tile + j, 1)],
                                          rstd[:, bass.ds(tile + j, 1)], SUB, MUL)
                ins.then_inc(normed, 1)

            dve.wait_ge(loaded, LOADED)
            dve.wait_ge(loaded_later, LATER)
            link(v.tensor_scalar(mneg[:, :], mask_sb[:, :], -1.0, -NEG, ADD, MUL))
            done[0] += 1
            v.scalar_tensor_tensor(gq0[:, :], col(QN_G), SC0, col(KN_G), MUL, MUL).then_inc(vec, 1)
            dve.wait_ge(vec, done[0])
            v.tensor_scalar(bq4s[:, :], col(BQ4), SC4, None, MUL).then_inc(d_bq, 1)
            for s in range(2):
                v.tensor_copy(xg[s][:, :, 0:1], spread(col(GTOK), 2).rearrange("p a b -> p b a")).then_inc(d_gtok, 1)
            for i in range(TILES):
                link(v.bn_stats(st[:, i, :], xt(i)))
            variance(st, mean[:, :], TILES, *TWICE)
            for i in range(B):
                link(v.bn_stats(cst[:, i, :], ctx_sb[:, i * CC:(i + 1) * CC]))
            dve.wait_ge(stat_rstd, 1)
            variance(cst, cmean[:, :], B, *ONCE)
            dve.wait_ge(stat_rstd, 2)

            with dve.Fori(0, PAIR_TURNS) as t:
                for s in range(2):
                    tile = 2 * t + s
                    for b in range(2):
                        v.tensor_scalar(xn[s][:, 1 + b, 0:CC], ctx_sb[:, bass.ds((2 * tile + b) * CC, CC)],
                                        cmean[:, bass.ds(2 * tile + b, 1)], crstd[:, bass.ds(2 * tile + b, 1)], SUB, MUL)
                    v.tensor_copy(mst[s][:, :], mneg[:, bass.ds(tile * M, M)])
                    normalise(xn[s], tile, 1, a_normed)
                for s in range(2):
                    dve.wait_ge(a_sq, 2 * t + s + 1)
                    v.tensor_reduce(sm[s][:, 0:8], sq[s].rearrange("p (h d) -> p h d", d=HD0), AX_X, ADD).then_inc(a_ss, 1)
                for s in range(2):
                    kv, ql = wide[s][:, 0, :].rearrange("p (b k) -> p b k", b=2), wide[s][:, 1, :]
                    v.tensor_copy(vc[s].rearrange("p (b k) -> p b k", b=2), kv[:, :, P:2 * P])
                    v.tensor_copy(vl[s][0:S, :], ql[0:S, 256:512])
                for s in range(2):
                    dve.wait_ge(a_ss, 2 * t + s + 1)
                    v.tensor_scalar(sm[s][:, 8:16], sm[s][:, 0:8], 1.0 / HD0, RMS_EPS * RMS_EPS, MUL, MAX).then_inc(a_ssm, 1)
                for s in range(2):
                    kv, ql = wide[s][:, 0, :].rearrange("p (b k) -> p b k", b=2), wide[s][:, 1, :]
                    dve.wait_ge(a_rk, 2 * t + s + 1)
                    v.tensor_tensor(qk0[s][:, 0:256].rearrange("p (h d) -> p h d", d=HD0),
                                    ql[:, 0:256].rearrange("p (h d) -> p h d", d=HD0),
                                    spread(sm[s][:, 16:20], HD0), MUL)
                    for b in range(2):
                        ins = v.tensor_tensor(qk0[s][:, 256 + b * P:256 + (b + 1) * P].rearrange("p (h d) -> p h d", d=HD0),
                                              kv[:, b, 0:P].rearrange("p (h d) -> p h d", d=HD0),
                                              spread(sm[s][:, 20 + 2 * b:22 + 2 * b], HD0), MUL)
                    ins.then_inc(a_qkn, 1)
                for s in range(2):
                    dve.wait_ge(a_scores, 2 * t + s + 1)
                    v.tensor_reduce(sm[s][:, 24:25], bank[s][1][:, 0:NK0], AX_X, MAX, negate=True)
                    v.tensor_reduce(sm[s][:, 25:26], wide[s][:, 0, 0:NK0], AX_X, MAX, negate=True).then_inc(a_nmx, 1)
                for s in range(2):
                    dve.wait_ge(a_exp, 2 * t + s + 1)
                    v.reciprocal(sm[s][:, 28:30], sm[s][:, 26:28]).then_inc(a_rden, 1)
                for s in range(2):
                    dve.wait_ge(a_rden, 2 * t + s + 1)
                    for h in range(2):
                        ins = v.tensor_scalar(p0[s][:, h, :], p0[s][:, h, :], sm[s][:, 28 + h:29 + h], None, MUL)
                    ins.then_inc(a_pn, 1)
                for s in range(2):
                    tile = 2 * t + s
                    dve.wait_ge(a_y, 2 * t + s + 1)
                    dve.wait_ge(a_xb, 2 * t + s + 1)
                    v.tensor_tensor(xt(tile), wide[s][:, 1, 0:C], xb[s][:, :], ADD).then_inc(a_upd, 1)
                for s in range(2):
                    dve.wait_ge(a_upd, 2 * t + s + 1)
                    ins = v.bn_stats(stats[:, bass.ds((2 * t + s) * 6, 6)], xt(2 * t + s))
            link(v.memset(st_a[:, 0:1], 0.0))
            variance(st, mean[:, :], TILES, *ONCE)
            dve.wait_ge(stat_rstd, 3)

            with dve.Fori(0, GROUP_TURNS) as t:
                for s in range(2):
                    normalise(xn[s], (2 * t + s) * G, G, b_normed)
                for s in range(2):
                    dve.wait_ge(b_qk, 2 * t + s + 1)
                    v.tensor_copy(bk[s], wide[s][:, 1, :])
                    dve.wait_ge(b_v, 2 * t + s + 1)
                    v.tensor_copy(bv[s], bank[s][0][:, :]).then_inc(b_kv, 1)
                for s in range(2):
                    sc = bank[s][1][:, 0:G * S].rearrange("p (j k) -> p j k", k=S)
                    dve.wait_ge(b_scores, 2 * t + s + 1)
                    v.tensor_reduce(sm[s][:, 0:G], sc, AX_X, MAX).then_inc(b_nmx, 1)
                for s in range(2):
                    sc = bank[s][1][:, 0:G * S].rearrange("p (j k) -> p j k", k=S)
                    dve.wait_ge(b_nmx, 2 * t + s + 1)
                    v.tensor_tensor(bsub[s].rearrange("p (j k) -> p j k", k=S), sc, spread(sm[s][:, 0:G], S),
                                    SUB).then_inc(b_sub, 1)
                for s in range(2):
                    dve.wait_ge(b_exp, 2 * t + s + 1)
                    v.tensor_reduce(sm[s][:, 4:4 + G], pbd[s].rearrange("p (j k) -> p j k", k=P), AX_X,
                                    ADD).then_inc(b_den, 1)
                for s in range(2):
                    dve.wait_ge(b_den, 2 * t + s + 1)
                    v.reciprocal(sm[s][:, 8:8 + G], sm[s][:, 4:4 + G]).then_inc(b_rden, 1)
                for s in range(2):
                    g = 2 * t + s
                    dve.wait_ge(b_rden, 2 * t + s + 1)
                    dve.wait_ge(b_o, 2 * t + s + 1)
                    for j in range(G):
                        ins = v.scalar_tensor_tensor(xt(g * G + j), bank[s][1][:, j * C:(j + 1) * C],
                                                     sm[s][:, 8 + j:9 + j], xt(g * G + j), MUL, ADD)
                    ins.then_inc(b_upd, 1)
                for s in range(2):
                    g = 2 * t + s
                    dve.wait_ge(b_upd, 2 * t + s + 1)
                    for j in range(G):
                        v.bn_stats(stats[:, bass.ds((g * G + j) * 6, 6)], xt(g * G + j))
            link(v.memset(st_a[:, 0:1], 0.0))
            variance(st, mean[:, :], TILES, *TWICE)
            dve.wait_ge(stat_rstd, 4)

            with dve.Fori(0, GROUP_TURNS) as t:
                for s in range(2):
                    normalise(xn[s], (2 * t + s) * G, G, c_normed)
                for s in range(2):
                    g = 2 * t + s
                    dve.wait_ge(c_z, 2 * t + s + 1)
                    v.tensor_reduce(zsum[:, bass.ds(g * 2 * G, 2 * G)],
                                    feat_T[:, bass.ds(g * GW, GW)].rearrange("p (b q) -> p b q", q=S), AX_X, ADD)
            v.tensor_scalar(rt[:, 0:1], col(BN_V), EPS, None, ADD).then_inc(c_route, 1)
            dve.wait_ge(c_exp, 1)
            link(v.tensor_scalar(rt[:, 2:3], col(BN_G), rt[:, 1:2], None, MUL))
            link(v.scalar_tensor_tensor(rt[:, 3:4], col(BN_M), rt[:, 2:3], col(BN_B), MUL, SUB))
            link(v.tensor_scalar(rt[:, 4:5], rt[:, 2:3], 1.0 / S, None, MUL))
            v.tensor_scalar(zbn[:, :], zsum[:, :], rt[:, 4:5], rt[:, 3:4], MUL, SUB).then_inc(c_zsum, 1)
            dve.wait_ge(c_logits, 1)
            link(v.tensor_tensor(lg[:, :], bank[0][0][0:B, 0:E], br_sb[:, :], ADD))
            link(v.tensor_reduce(rt64[:, 0:1], lg[:, :], AX_X, MAX))
            v.tensor_scalar(lg2[:, :], lg[:, :], rt64[:, 0:1], None, SUB).then_inc(c_route, 1)
            link(v.tensor_scalar(pick[:, :], lg[:, :], rt64[:, 0:1], None, ALU.is_ge))
            link(v.tensor_tensor(pick[:, :], pick[:, :], iota_sb[0:B, :], MUL))
            link(v.tensor_reduce(rt64[:, 1:2], pick[:, :], AX_X, MAX))
            dve.wait_ge(c_exp, 2)
            link(v.reciprocal(rt64[:, 3:4], rt64[:, 2:3]))
            v.tensor_scalar(coef[:, :], pick[:, :], rt64[:, 1:2], rt64[:, 3:4], ALU.is_equal, MUL).then_inc(c_coef, 1)
            dve.wait_ge(c_coefT, 1)
            v.tensor_copy(coefT[:, :], bank[0][1][0:E, 0:B]).then_inc(c_coef, 1)
            dve.wait_ge(c_spread, 1)
            v.tensor_copy(cspr[:, :], bank[1][0][:, 0:CH0 * B]).then_inc(c_spread_s, 1)
            dve.wait_ge(c_spread_s, 1)
            with dve.Fori(0, GROUP_TURNS) as t:
                for c in range(CH0):
                    for s in range(2):
                        g = 2 * t + s
                        dve.wait_ge(c_relu, 2 * (CH0 * t + c) + s + 1)
                        v.tensor_tensor(hr[s][:, c, :].rearrange("p (b q) -> p b q", q=S),
                                        hr[s][:, c, :].rearrange("p (b q) -> p b q", q=S),
                                        spread(cspr[:, bass.ds(c * B + g * 2 * G, 2 * G)], S), MUL).then_inc(c_hm, 1)
                for s in range(2):
                    g = 2 * t + s
                    dve.wait_ge(c_y, 2 * t + s + 1)
                    v.tensor_tensor(xt(g * G, G), wide[s][:, 0, :], xt(g * G, G), ADD).then_inc(c_upd, 1)
                for s in range(2):
                    g = 2 * t + s
                    dve.wait_ge(c_upd, 2 * t + s + 1)
                    for j in range(G):
                        v.bn_stats(stats[:, bass.ds((g * G + j) * 6, 6)], xt(g * G + j))
            link(v.memset(st_a[:, 0:1], 0.0))
            variance(st, mean[:, :], TILES, *ONCE)
            dve.wait_ge(stat_rstd, 5)

            dve.wait_ge(d_ones, 4)
            for k in range(2):
                keys = (M, KX)[k]
                with dve.Fori(k * PAIR_TURNS, (k + 1) * PAIR_TURNS) as t:
                    for s in range(2):
                        normalise(xn[s], 2 * (t - k * PAIR_TURNS) + s, 1, d_normed)
                    for s in range(2):
                        dve.wait_ge(d_proj, 2 * t + s + 1)
                        for b in range(2):
                            dst = vaug[s][0:keys, b, :, 0:16]
                            src = bank[s][0][0:keys, b * P:(b + 1) * P].rearrange("p (h d) -> p h d", d=16)
                            if k == 0:
                                ins = v.tensor_tensor(dst, src, rows_sb[0:keys, BV4, :].rearrange("p (h d) -> p h d", d=16), ADD)
                            else:
                                ins = v.tensor_copy(dst, src)
                        ins.then_inc(d_v, 1)
                    for b in range(2):
                        def sc(s):
                            return wide[s][:, :, 0:4 * keys].rearrange("p c (h k) -> p c h k", h=4)
                        for s in range(2):
                            dve.wait_ge(d_scores, 4 * t + 2 * b + s + 1)
                            v.tensor_reduce(sm[s][:, 0:HP].rearrange("p (c h) -> p c h", c=2), sc(s), AX_X,
                                            MAX).then_inc(d_nmx, 1)
                        for s in range(2):
                            dve.wait_ge(d_nmx, 4 * t + 2 * b + s + 1)
                            for c in range(2):
                                ins = v.tensor_tensor(probs[s][:, 4 * c:4 * c + 4, 0:keys], sc(s)[:, c, :, :],
                                                      spread(sm[s][:, 4 * c:4 * c + 4], keys), SUB)
                            ins.then_inc(d_sub, 1)
                        def ov(s):
                            return wide[s][:, 0, 0:HP * 17].rearrange("p (h d) -> p h d", d=17)
                        for s in range(2):
                            dve.wait_ge(d_o, 4 * t + 2 * b + s + 1)
                            v.reciprocal(sm[s][:, 16:16 + HP], ov(s)[:, :, 16]).then_inc(d_rden, 1)
                        for s in range(2):
                            dve.wait_ge(d_rden, 4 * t + 2 * b + s + 1)
                            for h in range(2):
                                half = slice(h * S, (h + 1) * S)
                                ins = v.tensor_tensor(on4[s][half, 0:HP * HD].rearrange("p (h d) -> p h d", d=HD),
                                                      ov(s)[half, :, h * HD:(h + 1) * HD],
                                                      spread(sm[s][half, 16:16 + HP], HD), MUL)
                            ins.then_inc(d_on, 1)
                    for s in range(2):
                        tile = 2 * (t - k * PAIR_TURNS) + s
                        dve.wait_ge(d_y, 2 * t + s + 1)
                        dve.wait_ge(d_xb, 2 * t + s + 1)
                        v.tensor_tensor(xt(tile), bank[s][1][:, 0:C], xb[s][:, :], ADD).then_inc(d_upd, 1)
                    for s in range(2):
                        tile = 2 * (t - k * PAIR_TURNS) + s
                        dve.wait_ge(d_upd, 2 * t + s + 1)
                        v.bn_stats(stats[:, bass.ds(tile * 6, 6)], xt(tile))
                link(v.memset(st_a[:, 0:1], 0.0))
                variance(st, mean[:, :], TILES, *ONCE)
                dve.wait_ge(stat_rstd, 6 + k)

            with dve.Fori(0, GROUP_TURNS) as t:
                for s in range(2):
                    normalise(xn[s], (2 * t + s) * G, G, f_normed)
                for s in range(2):
                    dve.wait_ge(f_logits, 2 * t + s + 1)
                    v.tensor_scalar(rl_all[:, bass.ds((2 * t + s) * G * E, G * E)], bank[s][1][:, 0:G * E], 1.0, None, MUL).then_inc(f_logits_s, 1)
            dve.wait_ge(f_logits_s, GROUPS)

            def best(dst, kd, logits, m):
                link(v.tensor_reduce(m, logits, AX_X, MAX))
                link(v.tensor_tensor(dst, logits, spread(m, E), ALU.is_ge))
                link(v.tensor_tensor(dst, dst, iota_sb[:, :].unsqueeze(1).to_broadcast([P, TILES, E]), MUL))
                link(v.tensor_reduce(kd, dst, AX_X, MAX))
                link(v.tensor_tensor(dst, dst, spread(kd, E), ALU.is_equal))

            best(r_1, st_b[:, 0:TILES], r_l0, st_a[:, 0:TILES])
            v.tensor_tensor(r_l, r_l0, spread(st_a[:, 0:TILES], E), SUB).then_inc(f_vec, 2)
            link(v.scalar_tensor_tensor(r_3, r_1, NEG, r_l0, MUL, ADD))
            best(r_2, st_b[:, 0:TILES], r_3, st_c[:, 0:TILES])
            link(v.tensor_tensor(r_1, r_1, r_2, ADD))
            dve.wait_ge(f_exp, 1)
            link(v.tensor_reduce(st_a[:, 0:TILES], r_e, AX_X, ADD))
            link(v.reciprocal(st_b[:, 0:TILES], st_a[:, 0:TILES]))
            link(v.tensor_tensor(r_2, r_e, spread(st_b[:, 0:TILES], E), MUL))
            link(v.tensor_tensor(r_1, r_1, r_2, MUL))
            link(v.tensor_reduce(st_a[:, 0:TILES], r_1, AX_X, ADD))
            link(v.tensor_scalar(st_c[:, 0:TILES], st_a[:, 0:TILES], 1e-9, None, ADD))
            link(v.reciprocal(st_b[:, 0:TILES], st_c[:, 0:TILES]))
            link(v.tensor_tensor(r_3, r_1, spread(st_b[:, 0:TILES], E), MUL))

            with dve.Fori(0, GROUPS) as g:
                v.tensor_copy(wst[:, :], r_3f[:, bass.ds(g * G * E, G * E)]).then_inc(f_wst, 1)

                def accumulate(e):
                    dve.wait_ge(f_down, E * g + e + 1)
                    dve.wait_ge(f_acc, (E + 1) * g + e + 1)
                    for j in range(G):
                        ins = v.scalar_tensor_tensor(yacc[:, j, :], wide[0][:, e % 2, j * C:(j + 1) * C],
                                                     wst[:, j * E + e:j * E + e + 1], yacc[:, j, :], MUL, ADD)
                    ins.then_inc(f_acc, 1)

                for k in range(E * FC):
                    if k == 2:
                        dve.wait_ge(f_yb, g + 1)
                        v.tensor_tensor(yacc[:, :, :].rearrange("p j c -> p (j c)"), wide[1][:, 1, :], xt(g * G, G),
                                        ADD).then_inc(f_acc, 1)
                    dve.wait_ge(f_silu, E * FC * g + k + 1)
                    v.scalar_tensor_tensor(hf[k % 2], bank[k % 2][1][:, :], col(UP_B + k), sg[k % 2], ADD,
                                           MUL).then_inc(f_h, 1)
                    if k >= 2 and k % 2 == 0:
                        accumulate(k // 2 - 1)
                accumulate(E - 1)
                dve.wait_ge(f_acc, (E + 1) * g + E + 1)
                v.tensor_scalar(xt(g * G, G), yacc[:, :, :].rearrange("p j c -> p (j c)"), 1.0, None, MUL).then_inc(f_upd, 1)
                dve.wait_ge(f_upd, g + 1)

        @block.tensor
        def _(pe):
            mm, ident_ap = nc.tensor.matmul, id_sb[:, :]

            def turn_groups(t, normed, turned, banks):
                for s in range(2):
                    pe.wait_ge(normed, 2 * t + s + 1)
                    for j in range(G):
                        ins = nc.tensor.transpose(banks[s][:, j * P:(j + 1) * P], xn[s][:, j, :], ident_ap)
                    ins.then_inc(turned, 1)

            pe.wait_ge(loaded, LOADED)
            pe.wait_ge(loaded_later, LATER)
            pe.wait_ge(vec, 1)
            with pe.Fori(0, PAIR_TURNS) as t:
                for s in range(2):
                    pe.wait_ge(a_normed, 2 * t + s + 1)
                    T = bank[s][0]
                    nc.tensor.transpose(T[:, 0:P], xn[s][:, 0, :], ident_ap)
                    for b in range(2):
                        ins = nc.tensor.transpose(T[0:CC, (1 + b) * P:(2 + b) * P], xn[s][:, 1 + b, 0:CC], ident_ap)
                    ins.then_inc(a_turned, 1)
                for s in range(2):
                    pe.wait_ge(a_lnT, 2 * t + s + 1)
                    for b in range(2):
                        mm(wide[s][:, 0, b * 256:(b + 1) * 256], cnT[s][0:CC, b * M:(b + 1) * M], wkv0[:, :], start=True, stop=True)
                    mm(wide[s][:, 1, 0:256], lnT[s], wqkv0[:, 0:256], start=True, stop=True)
                    for b in range(2):
                        ins = mm(wide[s][0:S, 1, 256 + b * P:256 + (b + 1) * P], lnT[s][:, b * S:(b + 1) * S],
                                 wqkv0[:, 256:384], start=True, stop=True)
                    ins.then_inc(a_proj, 1)
                for s in range(2):
                    pe.wait_ge(a_qkn, 2 * t + s + 1)
                    for i in range(4):
                        ins = nc.tensor.transpose(bank[s][0][:, i * P:(i + 1) * P], qk0[s][:, i * P:(i + 1) * P], ident_ap)
                    ins.then_inc(a_qkT, 1)
                for s in range(2):
                    sc = [bank[s][1], wide[s][:, 0, :]]
                    pe.wait_ge(a_qTs, 2 * t + s + 1)
                    for h in range(2):
                        mm(sc[h][:, 0:M], sel2_sb[:, :], mst[s][:, :], start=True,
                           stop=False, skip_group_check=True)
                    for h in range(2):
                        d = slice(h * HD0, (h + 1) * HD0)
                        for b in range(2):
                            q = slice(b * S, (b + 1) * S)
                            mm(sc[h][q, 0:M], qT0[s][d, q], kT0[s][d, P + b * M:P + (b + 1) * M],
                               start=False, stop=True, skip_group_check=True)
                            ins = mm(sc[h][q, M:NK0], qT0[s][d, q], kT0[s][d, q],
                                     start=False, stop=True, skip_group_check=True)
                    ins.then_inc(a_scores, 1)
                for s in range(2):
                    pe.wait_ge(a_pn, 2 * t + s + 1)
                    T = bank[s][0]
                    for h in range(2):
                        nc.tensor.transpose(T[:, h * P:(h + 1) * P], p0[s][:, h, 0:M], ident_ap)
                        ins = nc.tensor.transpose(T[0:S, (2 + h) * P:(3 + h) * P], p0[s][:, h, M:NK0], ident_ap)
                    ins.then_inc(a_pT, 1)
                for s in range(2):
                    pe.wait_ge(a_pTs, 2 * t + s + 1)
                    for h in range(2):
                        d = slice(h * HD0, (h + 1) * HD0)
                        for b in range(2):
                            q = slice(b * S, (b + 1) * S)
                            o = wide[s][d, 0, q]
                            mm(o, vc[s][:, b * P + h * HD0:b * P + (h + 1) * HD0],
                               pT0[s][:, h * P + b * S:h * P + (b + 1) * S], start=True, stop=False)
                            ins = mm(o, vl[s][0:S, b * P + h * HD0:b * P + (h + 1) * HD0],
                                     pT0[s][0:S, (2 + h) * P + b * S:(2 + h) * P + (b + 1) * S], start=False, stop=True)
                    ins.then_inc(a_oT, 1)
                for s in range(2):
                    pe.wait_ge(a_oTs, 2 * t + s + 1)
                    mm(wide[s][:, 1, 0:C], oT0[s], wo0[:, :], start=True, stop=True).then_inc(a_y, 1)

            with pe.Fori(0, GROUP_TURNS) as t:
                turn_groups(t, b_normed, b_turned, [bank[0][0], bank[1][0]])
                for s in range(2):
                    pe.wait_ge(b_xT, 2 * t + s + 1)
                    mm(wide[s][:, 0, :], wqkv1[:, 0:P], xT[s][:, :], start=True, stop=True)
                    mm(wide[s][:, 1, :], wqkv1[:, P:2 * P], xT[s][:, :], start=True, stop=True).then_inc(b_qk, 1)
                    for j in range(G):
                        ins = mm(bank[s][0][:, j * P:(j + 1) * P], xT[s][:, j * P:(j + 1) * P], wqkv1[:, 2 * P:3 * P],
                                 start=True, stop=True)
                    ins.then_inc(b_v, 1)
                for s in range(2):
                    pe.wait_ge(b_q, 2 * t + s + 1)
                    pe.wait_ge(b_kv, 2 * t + s + 1)
                    for j in range(G):
                        for b in range(2):
                            q = slice(j * P + b * S, j * P + (b + 1) * S)
                            ins = mm(bank[s][1][b * S:(b + 1) * S, j * S:(j + 1) * S], bq[s][:, q], bk[s][:, q],
                                     start=True, stop=True)
                    ins.then_inc(b_scores, 1)
                for s in range(2):
                    pe.wait_ge(b_exp, 2 * t + s + 1)
                    for j in range(G):
                        ins = nc.tensor.transpose(wide[s][:, 1, j * P:(j + 1) * P], pbd[s][:, j * P:(j + 1) * P], ident_ap)
                    ins.then_inc(b_pT, 1)
                for s in range(2):
                    pe.wait_ge(b_pTs, 2 * t + s + 1)
                    for j in range(G):
                        ins = mm(bank[s][1][:, j * C:(j + 1) * C], bpT[s][:, j * P:(j + 1) * P], bv[s][:, j * P:(j + 1) * P],
                                 start=True, stop=True)
                    ins.then_inc(b_o, 1)

            with pe.Fori(0, GROUP_TURNS) as t:
                turn_groups(t, c_normed, c_turned, [bank[0][0], bank[1][0]])
            pe.wait_ge(c_zsum, 1)
            mm(bank[0][0][0:B, 0:E], zbn[:, :], wr2[:, :], start=True, stop=True).then_inc(c_logits, 1)
            pe.wait_ge(c_coef, 1)
            nc.tensor.transpose(bank[0][1][0:E, 0:B], coef[:, :], id_sb[0:B, 0:B]).then_inc(c_coefT, 1)
            pe.wait_ge(c_coef, 2)
            for c in range(CH0):
                ins = mm(bank[1][0][:, c * B:(c + 1) * B], esel_sb[:, c * P:(c + 1) * P], coefT[:, :], start=True, stop=True)
            ins.then_inc(c_spread, 1)
            pe.wait_ge(c_spread_s, 1)
            with pe.Fori(0, GROUP_TURNS) as t:
                for c in range(CH0):
                    for s in range(2):
                        if c >= 2:
                            pe.wait_ge(c_relu, 2 * (CH0 * t + c - 2) + s + 1)
                        mm(bank[s][c % 2][:, :], wdown2[:, c * P:(c + 1) * P], feat_T[:, bass.ds((2 * t + s) * GW, GW)],
                           start=True, stop=True).then_inc(c_h, 1)
                for s in range(2):
                    pe.wait_ge(c_hm, 2 * (CH0 * t + CH0 - 1) + s + 1)
                    pe.wait_ge(c_tok, 2 * t + s + 1)
                    for j in range(G):
                        y = wide[s][:, 0, j * C:(j + 1) * C]
                        for c in range(CH0):
                            mm(y, hr[s][:, c, j * P:(j + 1) * P], wup2[:, c, :], start=(c == 0), stop=False)
                        ins = mm(y, ctok[s][:, j * P:(j + 1) * P], bup2[:, :], start=False, stop=True)
                    ins.then_inc(c_y, 1)

            for k in range(2):
                keys = (M, KX)[k]
                wo = (wo4, wo5)[k]
                with pe.Fori(k * PAIR_TURNS, (k + 1) * PAIR_TURNS) as t:
                    for s in range(2):
                        pe.wait_ge(d_normed, 2 * t + s + 1)
                        nc.tensor.transpose(bank[s][0][:, 0:P], xn[s][:, 0, :], ident_ap).then_inc(d_turned, 1)
                    for s in range(2):
                        if k == 0:
                            pe.wait_ge(d_ctx[s], 16 * t + 16)
                            mm(bank[s][1][:, P:P + 2 * keys], wk4[:, :], ctxT_s[s][:, :], start=True, stop=True)
                            pe.wait_ge(d_xT, 2 * t + s + 1)
                            mm(bank[s][1][:, 0:P], wq4[:, :], xT[s][:, 0:P], start=True, stop=True)
                            for b in range(2):
                                ins = mm(bank[s][0][:, b * P:(b + 1) * P], ctxT_s[s][:, b * M:(b + 1) * M], wv4[:, :],
                                         start=True, stop=True)
                        else:
                            pe.wait_ge(d_xT, 2 * t + s + 1)
                            mm(bank[s][1][:, 0:P], wqkv5[:, 0:P], xg[s][:, :, 1:KX], start=True, stop=True)
                            mm(bank[s][1][:, P:P + 2 * keys], wqkv5[:, P:2 * P], xg[s][:, :, :], start=True, stop=True)
                            for b in range(2):
                                ins = mm(bank[s][0][0:keys, b * P:(b + 1) * P], xg[s][:, b, :], wqkv5[:, 2 * P:3 * P],
                                         start=True, stop=True)
                        ins.then_inc(d_proj, 1)
                    for b in range(2):
                        for s in range(2):
                            pe.wait_ge(d_qm, 4 * t + 2 * b + s + 1)
                            pe.wait_ge(d_qk, 4 * t + 2 * s + 2)
                            if k == 1:
                                for c in range(2):
                                    mm(wide[s][:, c, 0:4 * keys], qneg_sb[:, :], e64_sb[:, :], start=True, stop=False,
                                       skip_group_check=True)
                            for h in range(HP):
                                ins = mm(wide[s][:, h // 4, h % 4 * keys:(h % 4 + 1) * keys],
                                         big[s][:, b, 2 * h:2 * h + 2, :], kT4[s][:, b * keys:(b + 1) * keys],
                                         start=(k == 0), stop=True, skip_group_check=(k == 1))
                            ins.then_inc(d_scores, 1)
                        for s in range(2):
                            pe.wait_ge(d_exp, 4 * t + 2 * b + s + 1)
                            if b == 0:
                                pe.wait_ge(d_v, 2 * t + s + 1)
                            for h in range(HP):
                                ins = nc.tensor.transpose(bank[s][h // 4][0:keys, h % 4 * P:(h % 4 + 1) * P],
                                                          probs[s][:, h, 0:keys], ident_ap)
                                if h % 4 == 3:
                                    ins.then_inc(d_pT, 1)
                        for s in range(2):
                            pe.wait_ge(d_pTs, 8 * t + 4 * b + 2 * s + 2)
                            for h in range(HP):
                                ins = mm(wide[s][:, 0, h * 17:(h + 1) * 17], probsT[s][0:keys, h, :],
                                         vaug[s][0:keys, b, h, :], start=True, stop=True)
                            ins.then_inc(d_o, 1)
                        for s in range(2):
                            pe.wait_ge(d_on, 4 * t + 2 * b + s + 1)
                            nc.tensor.transpose(bank[s][0][:, 0:P], on4[s][:, :], ident_ap).then_inc(d_oT, 1)
                    for s in range(2):
                        pe.wait_ge(d_oTs, 4 * t + 2 + s + 1)
                        for b in range(2):
                            for h in range(2):
                                ins = mm(bank[s][1][b * S:(b + 1) * S, 0:C], oT4[s][:, b, h * S:(h + 1) * S], wo[:, h, :],
                                         start=(h == 0), stop=(h == 1))
                        ins.then_inc(d_y, 1)

            with pe.Fori(0, GROUP_TURNS) as t:
                turn_groups(t, f_normed, f_turned, [bank[0][0], bank[1][0]])
                for s in range(2):
                    pe.wait_ge(f_xT, 4 * t + 2 * s + 2)
                    for j in range(G):
                        ins = mm(bank[s][1][:, j * E:(j + 1) * E], xT[s][:, j * P:(j + 1) * P], wr6[:, :], start=True, stop=True)
                    ins.then_inc(f_logits, 1)
            pe.wait_ge(f_logits_s, GROUPS)

            with pe.Fori(0, GROUPS) as g:
                xg_T = feat_T[:, bass.ds(g * GW, GW)]

                def gate_up(k):
                    mm(bank[k % 2][0][:, :], wgate6[:, k, :], xg_T, start=True, stop=True)
                    mm(bank[k % 2][1][:, :], wup6[:, k, :], xg_T, start=True, stop=True).then_inc(f_gu, 1)

                def down(k):
                    e, f = k // FC, k % FC
                    pe.wait_ge(f_h, E * FC * g + k + 1)
                    for j in range(G):
                        ins = mm(wide[0][:, e % 2, j * C:(j + 1) * C], hf[k % 2][:, j * P:(j + 1) * P], wdown6[:, k, :],
                                 start=(f == 0 and j == 0), stop=(f == FC - 1), skip_group_check=True)
                    if f == FC - 1:
                        ins.then_inc(f_down, 1)

                for k in range(E * FC + 1):
                    if k < E * FC:
                        gate_up(k)
                    if k == 0:
                        pe.wait_ge(f_wst, g + 1)
                        for j in range(G):
                            ins = nc.tensor.transpose(wide[1][0:E, 0, j * P:(j + 1) * P], wst[:, j * E:(j + 1) * E], ident_ap)
                        ins.then_inc(f_wT, 1)
                    if k == 1:
                        pe.wait_ge(f_wTs, g + 1)
                        for j in range(G):
                            ins = mm(wide[1][:, 1, j * C:(j + 1) * C], wTs[:, j * P:(j + 1) * P], bdown6[:, :],
                                     start=True, stop=True)
                        ins.then_inc(f_yb, 1)
                    if k >= 1:
                        down(k - 1)


def kernel(**inputs):
    import numpy as np
    import concourse.bacc as bacc
    from concourse.bass_utils import run_bass_kernel_spmd as run

    i = {k: np.asarray(a) for k, a in inputs.items()}
    f32 = np.float32
    bf16 = mybir.dt.np(mybir.dt.bfloat16)

    def column(a):
        c = np.zeros((P, 1), f32)
        c[:a.shape[0], 0] = a
        return c

    vectors = [column(i["L0_xattn_" + n]) for n in ("ln_x_g", "ln_x_b", "ln_l_g", "ln_l_b")]
    vectors += [column(np.tile(i["L0_xattn_" + n], 2)) for n in ("qn_g", "kn_g")]
    vectors += [column(i["L0_ffn_" + n]) for n in ("ln_g", "ln_b", "bn_g", "bn_b", "bn_mean", "bn_var")]
    vectors += [column(i["L1_xattn_bq"]), column(i["L1_xattn_bk"]), column(i["L1_attn_global_token"].reshape(C))]
    vectors += [i["L0_ffn_b_down"].reshape(CH0, P).T, i["L1_ffn_gate_b"].reshape(E * FC, P).T,
                i["L1_ffn_up_b"].reshape(E * FC, P).T]
    row_vectors = np.stack([i["L0_xattn_bo"], i["L1_xattn_bv"], i["L1_xattn_bo"], i["L1_attn_proj_b"]])
    
    def heads(w):
        w = w.reshape(HP, 2, HD, C).transpose(0, 2, 1, 3).reshape(HP * HD, 2, C)
        return np.concatenate([w, np.zeros_like(w)])

    part = np.arange(P)
    sel2 = (part[None, :] // S == np.arange(2)[:, None]).astype(bf16)
    qneg = np.where(part % S == S - 1, 0.0, NEG).astype(bf16)[None, :]
    e64 = np.tile(np.arange(S + 1) == S, 4).astype(bf16)[None, :]
    arrays = {
        "x": i["x"].reshape(TILES, P, C).transpose(1, 0, 2),
        "ctx": i["ctx_768"].transpose(1, 0, 2),
        "ctxT": i["ctx_768"].transpose(2, 0, 1).reshape(CC, B * M),
        "mask": i["mask_BxS2_bk0"].reshape(TILES, 2, M).transpose(1, 0, 2).reshape(2, TILES * M),
        "cols": np.concatenate(vectors, axis=1),
        "rows": np.broadcast_to(row_vectors[None], (P, 4, C)),
        "br": np.broadcast_to(i["L0_ffn_br"][None], (B, E)),
        "iota8": np.broadcast_to(np.arange(E, 0, -1).astype(f32)[None], (P, E)),
        "ident": np.eye(P, dtype=f32),
        "headmask": (part[:, None] // HD == np.arange(2 * HP)[None, :]).astype(f32),
        "sel2": sel2, "qneg": qneg, "e64": e64,
        "esel": (np.arange(E * H0)[None, :] // H0 == np.arange(E)[:, None]).astype(f32),
        "w_kv0": i["L0_xattn_Wkv"].T,
        "w_qkv0": np.concatenate([i["L0_xattn_Wq"].T, i["L0_xattn_Wlkv"].T], axis=1),
        "w_o0": i["L0_xattn_Wo"].T,
        "w_qkv1": i["L0_attn_W_qkv"].T,
        "w_r2": i["L0_ffn_Wr"],
        "w_down2": i["L0_ffn_W_down"].transpose(1, 0, 2).reshape(C, E * H0),
        "w_up2": i["L0_ffn_W_up"].reshape(CH0, P, C).transpose(1, 0, 2),
        "b_up2": i["L0_ffn_b_up"],
        "w_q4": i["L1_xattn_Wq"], "w_k4": i["L1_xattn_Wk"], "w_v4": i["L1_xattn_Wv"], "w_o4": heads(i["L1_xattn_Wo"]),
        "w_qkv5": i["L1_attn_qkv_w"].T, "w_o5": heads(i["L1_attn_proj_w"].T),
        "w_r6": i["L1_ffn_router_w"].T,
        "w_gate6": i["L1_ffn_gate_w"].reshape(E, C, FC, P).transpose(1, 0, 2, 3).reshape(C, E * FC, P),
        "w_up6": i["L1_ffn_up_w"].reshape(E, C, FC, P).transpose(1, 0, 2, 3).reshape(C, E * FC, P),
        "w_down6": i["L1_ffn_down_w"].reshape(E * FC, P, C).transpose(1, 0, 2),
        "b_down6": i["L1_ffn_down_b"],
    }
    arrays = {k: np.ascontiguousarray(a) for k, a in arrays.items()}
    nc = bacc.Bacc("TRN2", target_bir_lowering=False, num_devices=1)
    args = [nc.dram_tensor(f"in_{k}", a.shape, mybir.dt.from_np(a.dtype), kind="ExternalInput").ap()
            for k, a in arrays.items()]
    out = nc.dram_tensor("out", (P, TILES, C), F32, kind="ExternalOutput").ap()
    perceiver_kernel(nc, *args, out)
    got = run(nc, [{f"in_{k}": a for k, a in arrays.items()}], core_ids=[0])
    return got.results[0]["out"].transpose(1, 0, 2).reshape(B, S, C)
```

```python
from contextlib import ExitStack

import concourse.bass as bass
from concourse import mybir

ALU = mybir.AluOpType
ACT = mybir.ActivationFunctionType
F32 = mybir.dt.float32
BF16 = mybir.dt.bfloat16
U8 = mybir.dt.uint8
AX_X = mybir.AxisListType.X

P = 128
B, S, C = 64, 64, 128
TILES = B * S // P
M, CC = 128, 96
G = 4
GW = G * P
GROUPS = TILES // G
EPS = 1e-5
RMS_EPS = 1e-8
NEG = -1e30
HD0 = 64
NK0 = M + S
HP, HD = 8, 8
SC0 = HD0 ** -0.5
SC1 = C ** -0.5
SC4 = 16 ** -0.5
SC5 = HD ** -0.5
E = 8
H0 = 64
CH0 = E * H0 // P
FC = 2
PAIR_TURNS = TILES // 2
GROUP_TURNS = GROUPS // 2

LNX_G, LNX_B, LNL_G, LNL_B, QN_G, KN_G, FLN_G, FLN_B, BN_G, BN_B, BN_M, BN_V, BQ4, BK4, GTOK = range(15)
BDOWN = 15
GATE_B = BDOWN + CH0
UP_B = GATE_B + E * FC
BV4H = UP_B + E * FC
NCOLS = BV4H + 2
BO0, BO4, BO5 = range(3)


def perceiver_kernel(nc, x, ctx, ctxT, mask, cols, rows, br, iota8, ident, headmask, sel2, qneg, e64, esel,
                     w_kv0, w_qkv0, w_o0, w_qkv1, w_r2, w_down2, w_up2, b_up2,
                     w_q4, w_k4, w_v4, w_o4, w_qkv5, w_o5, w_r6, w_gate6, w_up6, w_down6, b_down6, out):
    with ExitStack() as stack:
        def sb(name, shape, dt=F32):
            return stack.enter_context(nc.sbuf_tensor(name, shape, dt))

        def sem(name):
            return stack.enter_context(nc.semaphore(name))

        def two(name):
            return [sem(f"{name}_{s}") for s in range(2)]

        bank = [[stack.enter_context(nc.psum_tensor(f"bank{s}{i}", [P, 512], F32)) for i in range(2)] for s in range(2)]
        wide = [stack.enter_context(nc.psum_tensor(f"wide{s}", [P, 2, 512], F32)) for s in range(2)]

        x_sb = sb("x_sb", [P, TILES * C])
        ctx_sb = sb("ctx_sb", [P, B * CC])
        feat_T = sb("feat_T", [P, TILES * P])
        stats = sb("stats", [P, TILES * 6])
        cstats = sb("cstats", [P, B * 6])
        mean = sb("mean", [P, TILES])
        rstd = sb("rstd", [P, TILES])
        cmean = sb("cmean", [P, B])
        crstd = sb("crstd", [P, B])
        st_a = sb("st_a", [P, B])
        st_b = sb("st_b", [P, B])
        st_c = sb("st_c", [P, B])
        st_d = sb("st_d", [P, B])
        st_v = sb("st_v", [P, B])
        neg_half = sb("neg_half", [P, B])
        cols_sb = sb("cols_sb", [P, NCOLS])
        rows_sb = sb("rows_sb", [P, 3, C])
        br_sb = sb("br_sb", [B, E])
        iota_sb = sb("iota_sb", [P, E])
        id_sb = sb("id_sb", [P, P])
        hm_sb = sb("hm_sb", [P, 2 * HP])
        sel2_sb = sb("sel2_sb", [2, P], BF16)
        qneg_sb = sb("qneg_sb", [1, P], BF16)
        e64_sb = sb("e64_sb", [1, 4 * (S + 1)], BF16)
        esel_sb = sb("esel_sb", [E, E * H0])
        mask_sb = sb("mask_sb", [2, TILES * M], U8)
        mneg = sb("mneg", [2, TILES * M], BF16)
        wkv0 = sb("wkv0", [CC, 2 * C])
        wqkv0 = sb("wqkv0", [P, 3 * C])
        wo0 = sb("wo0", [P, C])
        wqkv1 = sb("wqkv1", [P, 3 * C])
        wr2 = sb("wr2", [P, E])
        wdown2 = sb("wdown2", [P, E * H0])
        wup2 = sb("wup2", [P, CH0, C])
        bup2 = sb("bup2", [E, C])
        wq4 = sb("wq4", [P, C])
        wk4 = sb("wk4", [CC, C])
        wv4 = sb("wv4", [CC, C])
        wo4 = sb("wo4", [P, 2, C])
        wqkv5 = sb("wqkv5", [P, 3 * C])
        wo5 = sb("wo5", [P, 2, C])
        wr6 = sb("wr6", [P, E])
        wgate6 = sb("wgate6", [P, E * FC, P])
        wup6 = sb("wup6", [P, E * FC, P])
        wdown6 = sb("wdown6", [P, E * FC, C])
        bdown6 = sb("bdown6", [E, C])
        gq0 = sb("gq0", [P, 1])
        bq4s = sb("bq4s", [P, 1])

        def col(i):
            return cols_sb[:, i:i + 1]

        def pairs(name, shape, dt=F32):
            return [sb(f"{name}{s}", shape, dt) for s in range(2)]

        xn = pairs("xn", [P, G, C])
        xT = pairs("xT", [P, GW])
        xb = pairs("xb", [P, C])
        probs = pairs("probs", [P, HP, P])
        probsT = pairs("probsT", [P, HP, P])
        big = pairs("big", [P, 2, 2 * HP, S])
        sm = pairs("sm", [P, 64])
        sm2 = pairs("sm2", [P, 64])
        sm3 = pairs("sm3", [P, 64])

        loaded = sem("loaded")
        consts = sem("consts")
        vec = sem("vec")
        stat_var = sem("stat_var")
        stat_rstd = sem("stat_rstd")
        x_done = sem("x_done")
        block = stack.enter_context(nc.Block())

        loads = [(x_sb[:, :].rearrange("p (t c) -> p t c", c=C), x), (ctx_sb[:, :].rearrange("p (b c) -> p b c", c=CC), ctx),
                 (cols_sb[:, :], cols), (rows_sb[:, :, :], rows), (br_sb[:, :], br), (iota_sb[:, :], iota8),
                 (id_sb[:, :], ident), (hm_sb[:, :], headmask), (sel2_sb[:, :], sel2), (qneg_sb[:, :], qneg),
                 (e64_sb[:, :], e64), (esel_sb[:, :], esel), (mask_sb[:, :], mask), (wkv0[:, :], w_kv0),
                 (wqkv0[:, :], w_qkv0), (wo0[:, :], w_o0)]
        later = [(wqkv1[:, :], w_qkv1), (wr2[:, :], w_r2), (wdown2[:, :], w_down2), (wup2[:, :, :], w_up2),
                 (bup2[:, :], b_up2), (wq4[:, :], w_q4), (wk4[:, :], w_k4), (wv4[:, :], w_v4), (wo4[:, :, :], w_o4),
                 (wqkv5[:, :], w_qkv5), (wo5[:, :, :], w_o5), (wr6[:, :], w_r6), (wgate6[:, :, :], w_gate6),
                 (wup6[:, :, :], w_up6), (wdown6[:, :, :], w_down6), (bdown6[:, :], b_down6)]
        LOADED = 16 * len(loads)
        loaded_later = sem("loaded_later")
        LATER = 16 * len(later)

        T1_ps, T2_ps, T3_ps, OY_ps = bank[0][0], bank[0][1], bank[1][0], bank[1][1]
        KV_ps, QL_ps = wide[0][:, 0, :].rearrange("p (b k) -> p b k", b=2), wide[0][:, 1, :]
        S0_ps = wide[1]
        lnT = [xT[s][:, 0:P] for s in range(2)]
        cnT = [xT[s][:, P:3 * P] for s in range(2)]
        qT0 = [xT[s][:, 3 * P:4 * P] for s in range(2)]
        flat = [[t[s][:, :, :].rearrange("p a b -> p (a b)") for s in range(2)] for t in (probs, probsT)]
        bigf = [big[s][:, :, :, :].rearrange("p a b c -> p (a b c)") for s in range(2)]
        p0 = [flat[0][s][:, 0:2 * NK0].rearrange("p (h k) -> p h k", h=2) for s in range(2)]
        kT0 = [flat[0][s][:, 512:896] for s in range(2)]
        oT0 = [flat[0][s][:, 896:1024] for s in range(2)]
        pT0 = [flat[1][s][:, 0:512] for s in range(2)]
        qk0 = [bigf[s][:, 0:512] for s in range(2)]
        sq = [bigf[s][:, 512:1024] for s in range(2)]
        kvc = [feat_T[:, i * 512:(i + 1) * 512].rearrange("p (b k) -> p b k", b=2) for i in range(4)]
        qkl = [feat_T[:, 2048 + i * 512:2048 + (i + 1) * 512] for i in range(4)]
        bq = [flat[0][s][:, 0:512] for s in range(2)]
        bk = [flat[0][s][:, 512:1024] for s in range(2)]
        bv = [flat[1][s][:, 0:512] for s in range(2)]
        bpT = [flat[1][s][:, 512:1024] for s in range(2)]
        pbd = [bigf[s][:, 0:512] for s in range(2)]
        bsub = [bigf[s][:, 512:768] for s in range(2)]
        zsum = sb("zsum", [P, B])
        zbn = sb("zbn", [P, B])
        rt = sb("rt", [P, 8])
        rt64 = sb("rt64", [B, 4])
        lg = sb("lg", [B, E])
        lg2 = sb("lg2", [B, E])
        ex = sb("ex", [B, E])
        pick = sb("pick", [B, E])
        coef = sb("coef", [B, E])
        coefT = sb("coefT", [E, B])
        cspr = sb("cspr", [P, CH0 * B])
        hr = [bigf[s].rearrange("p (c n) -> p c n", c=CH0) for s in range(2)]
        ctok = [flat[0][s][0:E, 0:GW] for s in range(2)]
        ctxT_s = pairs("ctxT_s", [CC, 2 * M])
        kT4 = pairs("kT4", [P, 2 * M])
        vaug = pairs("vaug", [P, 2, HP, 17])
        on4 = pairs("on4", [P, P])
        oT4 = pairs("oT4", [P, 2, P])
        ysb = pairs("ysb", [P, C])
        S_ps = wide
        T_ps = bank[0]
        A_ps, O_ps = bank[1]
        mst = pairs("mst", [2, M], BF16)
        xg = pairs("xg", [P, 2, S + 1])
        rl_all = sb("rl_all", [P, TILES * E])
        route = [sb(f"route{i}", [P, TILES * E]) for i in range(5)]
        r_l0 = rl_all[:, :].rearrange("p (t e) -> p t e", e=E)
        r_1, r_2, r_3, r_e, r_l = [r[:, :].rearrange("p (t e) -> p t e", e=E) for r in route]
        r_3f = route[2]
        wst = sb("wst", [P, G * E])
        wTs = flat[1][0][0:E, 0:GW]
        sg = [flat[0][0][:, 0:512], flat[0][0][:, 512:1024]]
        hf = [flat[0][1][:, 0:512], flat[0][1][:, 512:1024]]
        yacc = xn[0]

        a_raw, a_vals = sem("a_raw"), sem("a_vals")
        a_normed, a_turned, a_lnT, a_proj, a_sq = sem("a_normed"), sem("a_turned"), sem("a_lnT"), sem("a_proj"), sem("a_sq")
        a_ss, a_ssm, a_rk, a_qkn, a_qkT = sem("a_ss"), sem("a_ssm"), sem("a_rk"), sem("a_qkn"), sem("a_qkT")
        a_qTs, a_scores, a_nmx, a_exp = sem("a_qTs"), sem("a_scores"), sem("a_nmx"), sem("a_exp")
        a_rden, a_pn, a_pT, a_pTs = sem("a_rden"), sem("a_pn"), sem("a_pT"), sem("a_pTs")
        a_oT, a_oTs, a_y, a_xb, a_upd = sem("a_oT"), sem("a_oTs"), sem("a_y"), sem("a_xb"), sem("a_upd")
        b_normed, b_turned, b_xT, b_qk, b_v = sem("b_normed"), sem("b_turned"), sem("b_xT"), sem("b_qk"), sem("b_v")
        b_q, b_kv, b_scores, b_nmx, b_sub = sem("b_q"), sem("b_kv"), sem("b_scores"), sem("b_nmx"), sem("b_sub")
        b_exp, b_den, b_rden, b_pT, b_pTs, b_o, b_upd = (sem("b_exp"), sem("b_den"), sem("b_rden"), sem("b_pT"),
                                                         sem("b_pTs"), sem("b_o"), sem("b_upd"))
        b_zero = sem("b_zero")
        c_normed, c_turned, c_z = sem("c_normed"), sem("c_turned"), sem("c_z")
        c_zsum, c_route, c_logits, c_exp, c_coef = sem("c_zsum"), sem("c_route"), sem("c_logits"), sem("c_exp"), sem("c_coef")
        c_coefT, c_spread, c_spread_s = sem("c_coefT"), sem("c_spread"), sem("c_spread_s")
        c_tok, c_h, c_relu, c_hm, c_y, c_upd = sem("c_tok"), sem("c_h"), sem("c_relu"), sem("c_hm"), sem("c_y"), sem("c_upd")
        d_ctx, d_normed, d_turned, d_xT, d_proj, d_qk = (two("d_ctx"), sem("d_normed"), sem("d_turned"), sem("d_xT"),
                                                         sem("d_proj"), sem("d_qk"))
        d_v, d_qm, d_scores, d_nmx, d_sub, d_exp = (sem("d_v"), sem("d_qm"), sem("d_scores"), sem("d_nmx"),
                                                    sem("d_sub"), sem("d_exp"))
        d_pT, d_pTs, d_o, d_rden, d_on, d_oT, d_oTs = (sem("d_pT"), sem("d_pTs"), sem("d_o"), sem("d_rden"),
                                                       sem("d_on"), sem("d_oT"), sem("d_oTs"))
        d_y, d_xb, d_upd, d_ys, d_vp = sem("d_y"), sem("d_xb"), sem("d_upd"), sem("d_ys"), sem("d_vp")
        d_ones, d_gtok, d_bq = sem("d_ones"), sem("d_gtok"), sem("d_bq")
        f_normed, f_turned, f_xT, f_logits = sem("f_normed"), sem("f_turned"), sem("f_xT"), sem("f_logits")
        f_logits_s, f_vec, f_exp, f_w = sem("f_logits_s"), sem("f_vec"), sem("f_exp"), sem("f_w")
        f_wst, f_wT, f_wTs, f_yb, f_acc0 = sem("f_wst"), sem("f_wT"), sem("f_wTs"), sem("f_yb"), sem("f_acc0")
        f_gu, f_silu, f_h, f_down, f_acc, f_upd = (sem("f_gu"), sem("f_silu"), sem("f_h"), sem("f_down"), sem("f_acc"),
                                                   sem("f_upd"))
        stored = sem("stored")

        st = stats[:, :].rearrange("p (t k) -> p t k", k=6)
        cst = cstats[:, :].rearrange("p (t k) -> p t k", k=6)
        KX = S + 1

        def xt(tile, n=1):
            return x_sb[:, bass.ds(tile * C, n * C)]

        def spread(ap, n):
            return ap.unsqueeze(len(ap.shape)).to_broadcast(list(ap.shape) + [n])

        def live(c):
            return 0 <= c < B

        def live_tile(i):
            return 0 <= i < TILES

        def run_tiles(eng, slot):
            for c in range(-1, 5):
                slot(0, c)
            with eng.Fori(0, 6) as t:
                for c in range(5, 9):
                    slot(t, c)
            for c in range(29, TILES + 5):
                slot(0, c)

        def run_slots(eng, k, slot):
            first = k * (B // 4)
            for c in range(-3, 6):
                slot(first, c)
            with eng.Fori(first, first + 13) as t:
                for c in range(6, 10):
                    slot(t, c)
            for c in range(6 + 13 * 4, B + 6):
                slot(first, c)

        @block.sync
        def _(sp):
            for dst, src in loads:
                sp.dma_start(dst, src).then_inc(loaded, 16)
            for dst, src in later:
                sp.dma_start(dst, src).then_inc(loaded_later, 16)
            for s in range(2):
                sp.dma_start(ctxT_s[s][:, :], ctxT[:, s * 2 * M:(s + 1) * 2 * M]).then_inc(d_ctx[s], 16)
            with sp.Fori(1, PAIR_TURNS) as t:
                for s in range(2):
                    sp.wait_ge(d_vp, 2 * t + s - 1)
                    sp.dma_start(ctxT_s[s][:, :], ctxT[:, bass.ds((2 * t + s) * 2 * M, 2 * M)]).then_inc(d_ctx[s], 16)
            with sp.Fori(0, GROUPS) as g:
                sp.wait_ge(f_upd, g + 1)
                sp.dma_start(out[:, bass.ds(g * G, G), :],
                             xt(g * G, G).rearrange("p (t c) -> p t c", c=C)).then_inc(stored, 16)
            sp.wait_ge(stored, 16 * GROUPS)

        @block.gpsimd
        def _(pool):
            nc.gpsimd.memset(neg_half[:, :], -0.5).then_inc(consts, 1)
            pool.wait_ge(consts, 1)

            def power(n, dst, width):
                pool.wait_ge(stat_var, n)
                nc.gpsimd.tensor_tensor(dst, st_v[:, 0:width], neg_half[:, 0:width], ALU.pow).then_inc(stat_rstd, 1)

            pool.wait_ge(loaded_later, LATER)
            power(1, rstd[:, :], TILES)
            power(2, crstd[:, :], B)

            def pool_tile_slot(t, c):
                u = 4 * t + c
                if live_tile(c):
                    pool.wait_ge(a_normed, u + 1)
                    nc.gpsimd.tensor_tensor(xt(u), xt(u), rows_sb[:, BO0, :], ALU.add).then_inc(a_xb, 1)
                    pool.wait_ge(a_raw, u + 1)
                    nc.gpsimd.tensor_tensor(sq[c % 2][:, 0:256], qkl[c % 4][:, 0:256], qkl[c % 4][:, 0:256], ALU.mult)
                    pool.wait_ge(a_vals, u + 1)
                    nc.gpsimd.tensor_tensor(sq[c % 2][:, 256:512].rearrange("p (b k) -> p b k", b=2),
                                            kvc[c % 4][:, :, 0:P], kvc[c % 4][:, :, 0:P], ALU.mult).then_inc(a_sq, 1)
                    pool.wait_ge(a_ssm, u + 1)
                    nc.gpsimd.tensor_tensor(sm[c % 2][:, 16:24], sm[c % 2][:, 8:16], neg_half[:, 0:8],
                                            ALU.pow).then_inc(a_rk, 1)

            run_tiles(pool, pool_tile_slot)
            power(3, rstd[:, :], TILES)
            for s in range(2):
                nc.gpsimd.memset(pbd[s], 0.0).then_inc(b_zero, 1)
            power(4, rstd[:, :], TILES)
            pool.wait_ge(c_route, 1)
            nc.gpsimd.tensor_tensor(rt[:, 1:2], rt[:, 0:1], neg_half[:, 0:1], ALU.pow).then_inc(c_exp, 1)
            pool.wait_ge(c_spread_s, 1)
            with pool.Fori(0, GROUP_TURNS) as t:
                for s in range(2):
                    g = 2 * t + s
                    pool.wait_ge(c_h, 2 * CH0 * t + s + 1)
                    nc.gpsimd.tensor_copy(ctok[s].rearrange("p (b q) -> p b q", q=S),
                                          spread(coefT[:, bass.ds(g * 2 * G, 2 * G)], S)).then_inc(c_tok, 1)

            for k, bo, n in ((0, BO4, 5), (1, BO5, 6)):
                power(n, rstd[:, :], TILES)
                if k == 0:
                    for s in range(2):
                        nc.gpsimd.memset(vaug[s][:, :, :, 16:17], 1.0).then_inc(d_ones, 1)
                        nc.gpsimd.memset(on4[s][:, HP * HD:P], 0.0).then_inc(d_ones, 1)

                def pool_slot(t, c):
                    u, b, here = 4 * t + c, c % 2, 2 * t + c // 2
                    par = (c // 2 + 1) % 2
                    if b == 0 and live(c - 6):
                        pool.wait_ge(d_ys, 2 * t + (c - 6) // 2 + 1)
                        pool.wait_ge(d_xb, 2 * t + (c - 6) // 2 + 1)
                        tile = 2 * t + (c - 6) // 2 - k * TILES
                        nc.gpsimd.tensor_tensor(xt(tile), xt(tile), ysb[(c - 6) // 2 % 2][:, :], ALU.add).then_inc(d_upd, 1)
                    if live_tile(c // 2 + 1):
                        pool.wait_ge(d_qk, 2 * here + 3)
                        if live(c - 2):
                            pool.wait_ge(d_scores, u - 1)
                        nc.gpsimd.tensor_tensor(
                            big[par][:, b, :, :],
                            xT[par][:, 256 + b * S:256 + (b + 1) * S].unsqueeze(1).to_broadcast([P, 2 * HP, S]),
                            spread(hm_sb[:, :], S), ALU.mult).then_inc(d_qm, 1)
                    if b == 1 and live_tile(c // 2 + 2):
                        pool.wait_ge(d_normed, here + 3)
                        tile = here + 2 - k * TILES
                        nc.gpsimd.tensor_tensor(xt(tile), xt(tile), rows_sb[:, bo, :], ALU.add).then_inc(d_xb, 1)

                run_slots(pool, k, pool_slot)
            power(7, rstd[:, :], TILES)

        @block.scalar
        def _(act):
            ID, EXP = ACT.Identity, ACT.Exp
            act.wait_ge(loaded, LOADED)
            act.wait_ge(loaded_later, LATER)
            act.wait_ge(vec, 2)
            def act_tile_slot(t, c):
                u, s = 4 * t + c, c % 2
                if live_tile(c):
                    act.wait_ge(a_turned, u + 1)
                    nc.scalar.activation(lnT[s], T1_ps[:, 0:P], ID, bias=col(LNL_B), scale=col(LNL_G))
                    nc.scalar.activation(cnT[s][0:CC, :], T1_ps[0:CC, P:3 * P], ID, bias=cols_sb[0:CC, LNX_B:LNX_B + 1],
                                         scale=cols_sb[0:CC, LNX_G:LNX_G + 1]).then_inc(a_lnT, 1)
                if live_tile(c - 4):
                    act.wait_ge(a_pT, u - 3)
                    nc.scalar.activation(pT0[s][:, 0:2 * P], T3_ps[:, 0:2 * P], ID)
                    nc.scalar.activation(pT0[s][0:S, 2 * P:4 * P], T3_ps[0:S, 2 * P:4 * P], ID).then_inc(a_pTs, 1)
                if live_tile(c - 3):
                    act.wait_ge(a_nmx, u - 2)
                    q = (c - 3) % 2
                    for h in range(2):
                        ins = nc.scalar.activation(p0[q][:, h, :], S0_ps[:, h, 0:NK0], EXP,
                                                   bias=sm[q][:, 24 + h:25 + h], scale=1.0,
                                                   accum_out=sm[q][:, 26 + h:27 + h])
                    ins.then_inc(a_exp, 1)
                if live_tile(c - 2):
                    act.wait_ge(a_qkT, u - 1)
                    nc.scalar.activation(qT0[s], T2_ps[:, 0:P], ID, scale=gq0[:, 0:1])
                    nc.scalar.activation(kT0[s], T2_ps[:, P:4 * P], ID).then_inc(a_qTs, 1)
                if live_tile(c - 4):
                    act.wait_ge(a_oT, u - 3)
                    nc.scalar.activation(oT0[s], OY_ps[:, 0:P], ID).then_inc(a_oTs, 1)
                if live_tile(c):
                    act.wait_ge(a_proj, u + 1)
                    nc.scalar.activation(kvc[c % 4], KV_ps, ID).then_inc(a_vals, 1)

            run_tiles(act, act_tile_slot)

            act.wait_ge(b_zero, 2)
            with act.Fori(0, GROUP_TURNS) as t:
                for s in range(2):
                    act.wait_ge(b_turned, 2 * t + s + 1)
                    nc.scalar.activation(xT[s][:, :], bank[s][0][:, :], ID).then_inc(b_xT, 1)
                for s in range(2):
                    act.wait_ge(b_qk, 2 * t + s + 1)
                    nc.scalar.activation(bq[s], wide[s][:, 0, :], ID, scale=SC1).then_inc(b_q, 1)
                for s in range(2):
                    act.wait_ge(b_sub, 2 * t + s + 1)
                    for b in range(2):
                        half = slice(b * S, (b + 1) * S)
                        ins = nc.scalar.activation(pbd[s].rearrange("p (j k) -> p j k", k=P)[half, :, half],
                                                   bsub[s].rearrange("p (j k) -> p j k", k=S)[half, :, :], EXP)
                    ins.then_inc(b_exp, 1)
                for s in range(2):
                    act.wait_ge(b_pT, 2 * t + s + 1)
                    nc.scalar.activation(bpT[s], wide[s][:, 1, :], ID).then_inc(b_pTs, 1)

            with act.Fori(0, GROUP_TURNS) as t:
                for s in range(2):
                    act.wait_ge(c_turned, 2 * t + s + 1)
                    nc.scalar.activation(feat_T[:, bass.ds((2 * t + s) * GW, GW)], bank[s][0][:, :], ID,
                                         bias=col(FLN_B), scale=col(FLN_G)).then_inc(c_z, 1)
            act.wait_ge(c_route, 2)
            nc.scalar.activation(ex[:, :], lg2[:, :], EXP, accum_out=rt64[:, 2:3]).then_inc(c_exp, 1)
            with act.Fori(0, GROUP_TURNS) as t:
                for c in range(CH0):
                    for s in range(2):
                        act.wait_ge(c_h, 2 * (CH0 * t + c) + s + 1)
                        nc.scalar.activation(hr[s][:, c, :], bank[s][c % 2][:, :], ACT.Relu,
                                             bias=col(BDOWN + c)).then_inc(c_relu, 1)

            act.wait_ge(d_bq, 1)
            act.wait_ge(d_gtok, 2)
            act.wait_ge(d_ones, 4)
            for k in range(2):
                keys = (M, KX)[k]

                def act_slot(t, c):
                    u, b, here = 4 * t + c, c % 2, 2 * t + c // 2
                    par = (c // 2 + 1) % 2
                    if b == 0 and live_tile(c // 2):
                        act.wait_ge(d_vp, here + 1)
                        nc.scalar.activation(vaug[1 - par][0:keys, :, :, 0:16],
                                             A_ps[0:keys, 0:2 * P].rearrange("p (b h d) -> p b h d", b=2, d=16),
                                             ID).then_inc(d_v, 1)
                    if b == 1 and live_tile(c // 2 + 1):
                        act.wait_ge(d_proj, here + 2)
                        qT, kT = xT[par][:, 256:384], kT4[par][:, 0:2 * keys]
                        if k == 0:
                            nc.scalar.activation(qT, A_ps[:, 0:P], ID, bias=bq4s[:, 0:1], scale=SC4).then_inc(d_qk, 1)
                            nc.scalar.activation(kT, A_ps[:, P:P + 2 * keys], ID, bias=col(BK4)).then_inc(d_qk, 1)
                        else:
                            nc.scalar.activation(qT, A_ps[:, 0:P], ID, scale=SC5).then_inc(d_qk, 1)
                            nc.scalar.activation(kT, A_ps[:, P:P + 2 * keys], ID).then_inc(d_qk, 1)
                    if live(c - 1):
                        act.wait_ge(d_sub, u)
                        nc.scalar.activation(probs[1 - b][:, :, 0:keys], probs[1 - b][:, :, 0:keys], EXP).then_inc(d_exp, 1)
                    if live(c - 3):
                        act.wait_ge(d_oT, u - 2)
                        dst = oT4[(c - 3) // 2 % 2]
                        if k == 0:
                            for h in range(2):
                                ins = nc.scalar.activation(dst[:, 1 - b, h * S:(h + 1) * S], A_ps[:, 384 + h * S:384 + (h + 1) * S],
                                                           ID, bias=col(BV4H + h))
                        else:
                            ins = nc.scalar.activation(dst[:, 1 - b, :], A_ps[:, 384:512], ID)
                        ins.then_inc(d_oTs, 1)
                    for half in range(2):
                        if live(c - 1):
                            act.wait_ge(d_pT, 2 * u - 1 + half)
                            nc.scalar.activation(probsT[1 - b][0:keys, 4 * half:4 * half + 4, :],
                                                 T_ps[half][0:keys, :].rearrange("p (h q) -> p h q", q=P),
                                                 ID).then_inc(d_pTs, 1)
                        if half == 0 and b == 0 and live_tile(c // 2 + 1):
                            act.wait_ge(d_turned, here + 2)
                            if k == 0:
                                nc.scalar.activation(xT[par][:, 0:P], A_ps[:, 0:P], ID).then_inc(d_xT, 1)
                            else:
                                nc.scalar.activation(xg[par][:, :, 1:KX], A_ps[:, 0:P].rearrange("p (b q) -> p b q", b=2),
                                                     ID).then_inc(d_xT, 1)
                        if half == 0 and b == 1 and live(c - 5):
                            act.wait_ge(d_y, (c - 5) // 2 + 2 * t + 1)
                            if live(c - 9):
                                act.wait_ge(d_upd, (c - 9) // 2 + 2 * t + 1)
                            nc.scalar.activation(ysb[(c - 5) // 2 % 2][:, :], A_ps[:, 256:256 + C], ID).then_inc(d_ys, 1)

                run_slots(act, k, act_slot)
            with act.Fori(0, GROUP_TURNS) as t:
                for s in range(2):
                    act.wait_ge(f_turned, 2 * t + s + 1)
                    nc.scalar.activation(xT[s][:, :], bank[s][0][:, :], ID).then_inc(f_xT, 1)
                    nc.scalar.activation(feat_T[:, bass.ds((2 * t + s) * GW, GW)], bank[s][0][:, :],
                                         ID).then_inc(f_xT, 1)
            act.wait_ge(f_vec, 2)
            nc.scalar.activation(r_e, r_l, EXP).then_inc(f_exp, 1)
            with act.Fori(0, GROUPS) as g:
                act.wait_ge(f_wT, g + 1)
                nc.scalar.activation(wTs, wide[1][0:E, 0, :], ID).then_inc(f_wTs, 1)
                for k in range(E * FC):
                    act.wait_ge(f_gu, E * FC * g + k + 1)
                    nc.scalar.activation(sg[k % 2], bank[k % 2][0][:, :], ACT.Silu,
                                         bias=col(GATE_B + k)).then_inc(f_silu, 1)

        @block.vector
        def _(dve):
            SUB, MUL, ADD, MAX = ALU.subtract, ALU.mult, ALU.add, ALU.max
            v = nc.vector
            done = [0]

            def link(ins):
                done[0] += 1
                ins.then_inc(vec, 1)
                dve.wait_ge(vec, done[0])

            def variance(src, mean_dst, n, a, b):
                link(v.tensor_tensor(st_a[:, 0:n], src[:, :, 1], src[:, :, 4], ADD))
                link(v.tensor_scalar(mean_dst, st_a[:, 0:n], 0.5, None, MUL))
                link(v.tensor_tensor(st_b[:, 0:n], src[:, :, 1], src[:, :, 4], SUB))
                link(v.tensor_tensor(st_c[:, 0:n], src[:, :, 2], src[:, :, 5], ADD))
                link(v.scalar_tensor_tensor(st_d[:, 0:n], st_b[:, 0:n], 0.25, st_b[:, 0:n], MUL, MUL))
                width = C if n == TILES else CC
                link(v.scalar_tensor_tensor(st_a[:, 0:n], st_c[:, 0:n], 1.0 / width, st_d[:, 0:n], MUL, ADD))
                done[0] += 1
                v.tensor_scalar(st_v[:, 0:n], st_a[:, 0:n], a, b, MUL, ADD).then_inc(vec, 1)
                dve.wait_ge(vec, done[0])
                v.tensor_scalar(st_a[:, 0:1], st_v[:, 0:1], 1.0, None, MUL).then_inc(stat_var, 1)

            TWICE = (1.0 + EPS, EPS * EPS)
            ONCE = (1.0, EPS)

            def normalise(dst, tile, n, normed):
                for j in range(n):
                    ins = v.tensor_scalar(dst[:, j, :], xt(tile + j), mean[:, bass.ds(tile + j, 1)],
                                          rstd[:, bass.ds(tile + j, 1)], SUB, MUL)
                ins.then_inc(normed, 1)

            dve.wait_ge(loaded, LOADED)
            dve.wait_ge(loaded_later, LATER)
            link(v.tensor_scalar(mneg[:, :], mask_sb[:, :], -1.0, -NEG, ADD, MUL))
            done[0] += 1
            v.scalar_tensor_tensor(gq0[:, :], col(QN_G), SC0, col(KN_G), MUL, MUL).then_inc(vec, 1)
            dve.wait_ge(vec, done[0])
            v.tensor_scalar(bq4s[:, :], col(BQ4), SC4, None, MUL).then_inc(d_bq, 1)
            for s in range(2):
                v.tensor_copy(xg[s][:, :, 0:1], spread(col(GTOK), 2).rearrange("p a b -> p b a")).then_inc(d_gtok, 1)
            for i in range(TILES):
                link(v.bn_stats(st[:, i, :], xt(i)))
            variance(st, mean[:, :], TILES, *TWICE)
            for i in range(B):
                link(v.bn_stats(cst[:, i, :], ctx_sb[:, i * CC:(i + 1) * CC]))
            dve.wait_ge(stat_rstd, 1)
            variance(cst, cmean[:, :], B, *ONCE)
            dve.wait_ge(stat_rstd, 2)

            def dve_tile_slot(t, c):
                u, s = 4 * t + c, c % 2
                if live_tile(c - 3):
                    dve.wait_ge(a_scores, u - 2)
                    q = 1 - s
                    v.tensor_reduce(sm[q][:, 24:26], S0_ps[:, :, 0:NK0], AX_X, MAX, negate=True).then_inc(a_nmx, 1)
                if live_tile(c + 1):
                    tile, q = u + 1, 1 - s
                    if live_tile(c - 1):
                        dve.wait_ge(a_turned, u)
                    for b in range(2):
                        v.tensor_scalar(xn[q][:, 1 + b, 0:CC], ctx_sb[:, bass.ds((2 * tile + b) * CC, CC)],
                                        cmean[:, bass.ds(2 * tile + b, 1)], crstd[:, bass.ds(2 * tile + b, 1)], SUB, MUL)
                    normalise(xn[q], tile, 1, a_normed)
                if live_tile(c - 3):
                    q = 1 - s
                    dve.wait_ge(a_exp, u - 2)
                    v.reciprocal(sm[q][:, 28:30], sm[q][:, 26:28]).then_inc(a_rden, 1)
                    dve.wait_ge(a_rden, u - 2)
                    for h in range(2):
                        ins = v.tensor_scalar(p0[q][:, h, :], p0[q][:, h, :], sm[q][:, 28 + h:29 + h], None, MUL)
                    ins.then_inc(a_pn, 1)
                if live_tile(c):
                    dve.wait_ge(a_proj, u + 1)
                    v.tensor_copy(qkl[c % 4][:, 0:256], QL_ps[:, 0:256])
                    v.tensor_copy(qkl[c % 4][0:S, 256:512], QL_ps[0:S, 256:512]).then_inc(a_raw, 1)
                if live_tile(c - 4):
                    dve.wait_ge(a_y, u - 3)
                    dve.wait_ge(a_xb, u - 3)
                    v.tensor_tensor(xt(u - 4), OY_ps[:, P:2 * P], xt(u - 4), ADD).then_inc(a_upd, 1)
                if live_tile(c - 1):
                    q = 1 - s
                    dve.wait_ge(a_rk, u)
                    if live_tile(c - 3):
                        dve.wait_ge(a_qkT, u - 2)
                    v.tensor_tensor(qk0[q][:, 0:256].rearrange("p (h d) -> p h d", d=HD0),
                                    qkl[(c - 1) % 4][:, 0:256].rearrange("p (h d) -> p h d", d=HD0),
                                    spread(sm[q][:, 16:20], HD0), MUL)
                    v.tensor_tensor(qk0[q][:, 256:512].rearrange("p (b h d) -> p b h d", b=2, d=HD0),
                                    kvc[(c - 1) % 4][:, :, 0:P].rearrange("p b (h d) -> p b h d", d=HD0),
                                    spread(sm[q][:, 20:24].rearrange("p (b h) -> p b h", b=2), HD0), MUL).then_inc(a_qkn, 1)
                if live_tile(c - 4):
                    dve.wait_ge(a_upd, u - 3)
                    v.bn_stats(stats[:, bass.ds((u - 4) * 6, 6)], xt(u - 4))
                if live_tile(c):
                    dve.wait_ge(a_sq, u + 1)
                    v.tensor_reduce(sm[s][:, 0:8], sq[s].rearrange("p (h d) -> p h d", d=HD0), AX_X, ADD).then_inc(a_ss, 1)
                    dve.wait_ge(a_ss, u + 1)
                    v.tensor_scalar(sm[s][:, 8:16], sm[s][:, 0:8], 1.0 / HD0, RMS_EPS * RMS_EPS, MUL, MAX).then_inc(a_ssm, 1)

            run_tiles(dve, dve_tile_slot)
            link(v.memset(st_a[:, 0:1], 0.0))
            variance(st, mean[:, :], TILES, *ONCE)
            dve.wait_ge(stat_rstd, 3)

            with dve.Fori(0, GROUP_TURNS) as t:
                for s in range(2):
                    normalise(xn[s], (2 * t + s) * G, G, b_normed)
                for s in range(2):
                    dve.wait_ge(b_qk, 2 * t + s + 1)
                    v.tensor_copy(bk[s], wide[s][:, 1, :])
                    dve.wait_ge(b_v, 2 * t + s + 1)
                    v.tensor_copy(bv[s], bank[s][0][:, :]).then_inc(b_kv, 1)
                for s in range(2):
                    sc = bank[s][1][:, 0:G * S].rearrange("p (j k) -> p j k", k=S)
                    dve.wait_ge(b_scores, 2 * t + s + 1)
                    v.tensor_reduce(sm[s][:, 0:G], sc, AX_X, MAX).then_inc(b_nmx, 1)
                for s in range(2):
                    sc = bank[s][1][:, 0:G * S].rearrange("p (j k) -> p j k", k=S)
                    dve.wait_ge(b_nmx, 2 * t + s + 1)
                    v.tensor_tensor(bsub[s].rearrange("p (j k) -> p j k", k=S), sc, spread(sm[s][:, 0:G], S),
                                    SUB).then_inc(b_sub, 1)
                for s in range(2):
                    dve.wait_ge(b_exp, 2 * t + s + 1)
                    v.tensor_reduce(sm[s][:, 4:4 + G], pbd[s].rearrange("p (j k) -> p j k", k=P), AX_X,
                                    ADD).then_inc(b_den, 1)
                for s in range(2):
                    dve.wait_ge(b_den, 2 * t + s + 1)
                    v.reciprocal(sm[s][:, 8:8 + G], sm[s][:, 4:4 + G]).then_inc(b_rden, 1)
                for s in range(2):
                    g = 2 * t + s
                    dve.wait_ge(b_rden, 2 * t + s + 1)
                    dve.wait_ge(b_o, 2 * t + s + 1)
                    for j in range(G):
                        ins = v.scalar_tensor_tensor(xt(g * G + j), bank[s][1][:, j * C:(j + 1) * C],
                                                     sm[s][:, 8 + j:9 + j], xt(g * G + j), MUL, ADD)
                    ins.then_inc(b_upd, 1)
                for s in range(2):
                    g = 2 * t + s
                    dve.wait_ge(b_upd, 2 * t + s + 1)
                    for j in range(G):
                        v.bn_stats(stats[:, bass.ds((g * G + j) * 6, 6)], xt(g * G + j))
            link(v.memset(st_a[:, 0:1], 0.0))
            variance(st, mean[:, :], TILES, *TWICE)
            dve.wait_ge(stat_rstd, 4)

            with dve.Fori(0, GROUP_TURNS) as t:
                for s in range(2):
                    normalise(xn[s], (2 * t + s) * G, G, c_normed)
                for s in range(2):
                    g = 2 * t + s
                    dve.wait_ge(c_z, 2 * t + s + 1)
                    v.tensor_reduce(zsum[:, bass.ds(g * 2 * G, 2 * G)],
                                    feat_T[:, bass.ds(g * GW, GW)].rearrange("p (b q) -> p b q", q=S), AX_X, ADD)
            v.tensor_scalar(rt[:, 0:1], col(BN_V), EPS, None, ADD).then_inc(c_route, 1)
            dve.wait_ge(c_exp, 1)
            link(v.tensor_scalar(rt[:, 2:3], col(BN_G), rt[:, 1:2], None, MUL))
            link(v.scalar_tensor_tensor(rt[:, 3:4], col(BN_M), rt[:, 2:3], col(BN_B), MUL, SUB))
            link(v.tensor_scalar(rt[:, 4:5], rt[:, 2:3], 1.0 / S, None, MUL))
            v.tensor_scalar(zbn[:, :], zsum[:, :], rt[:, 4:5], rt[:, 3:4], MUL, SUB).then_inc(c_zsum, 1)
            dve.wait_ge(c_logits, 1)
            link(v.tensor_tensor(lg[:, :], bank[0][0][0:B, 0:E], br_sb[:, :], ADD))
            link(v.tensor_reduce(rt64[:, 0:1], lg[:, :], AX_X, MAX))
            v.tensor_scalar(lg2[:, :], lg[:, :], rt64[:, 0:1], None, SUB).then_inc(c_route, 1)
            link(v.tensor_scalar(pick[:, :], lg[:, :], rt64[:, 0:1], None, ALU.is_ge))
            link(v.tensor_tensor(pick[:, :], pick[:, :], iota_sb[0:B, :], MUL))
            link(v.tensor_reduce(rt64[:, 1:2], pick[:, :], AX_X, MAX))
            dve.wait_ge(c_exp, 2)
            link(v.reciprocal(rt64[:, 3:4], rt64[:, 2:3]))
            v.tensor_scalar(coef[:, :], pick[:, :], rt64[:, 1:2], rt64[:, 3:4], ALU.is_equal, MUL).then_inc(c_coef, 1)
            dve.wait_ge(c_coefT, 1)
            v.tensor_copy(coefT[:, :], bank[0][1][0:E, 0:B]).then_inc(c_coef, 1)
            dve.wait_ge(c_spread, 1)
            v.tensor_copy(cspr[:, :], bank[1][0][:, 0:CH0 * B]).then_inc(c_spread_s, 1)
            dve.wait_ge(c_spread_s, 1)
            with dve.Fori(0, GROUP_TURNS) as t:
                for c in range(CH0):
                    for s in range(2):
                        g = 2 * t + s
                        dve.wait_ge(c_relu, 2 * (CH0 * t + c) + s + 1)
                        v.tensor_tensor(hr[s][:, c, :].rearrange("p (b q) -> p b q", q=S),
                                        hr[s][:, c, :].rearrange("p (b q) -> p b q", q=S),
                                        spread(cspr[:, bass.ds(c * B + g * 2 * G, 2 * G)], S), MUL).then_inc(c_hm, 1)
                for s in range(2):
                    g = 2 * t + s
                    dve.wait_ge(c_y, 2 * t + s + 1)
                    v.tensor_tensor(xt(g * G, G), wide[s][:, 0, :], xt(g * G, G), ADD).then_inc(c_upd, 1)
                for s in range(2):
                    g = 2 * t + s
                    dve.wait_ge(c_upd, 2 * t + s + 1)
                    for j in range(G):
                        v.bn_stats(stats[:, bass.ds((g * G + j) * 6, 6)], xt(g * G + j))
            link(v.memset(st_a[:, 0:1], 0.0))
            variance(st, mean[:, :], TILES, *ONCE)
            dve.wait_ge(stat_rstd, 5)

            dve.wait_ge(d_ones, 4)
            for k in range(2):
                keys = (M, KX)[k]

                def dve_slot(t, c):
                    u, b, here = 4 * t + c, c % 2, 2 * t + c // 2
                    sc = S_ps[b][:, :, 0:4 * keys].rearrange("p c (h k) -> p c h k", h=4)
                    if live(c):
                        dve.wait_ge(d_scores, u + 1)
                        v.tensor_reduce(sm[b][:, 0:HP].rearrange("p (c h) -> p c h", c=2), sc, AX_X, MAX).then_inc(d_nmx, 1)
                        dve.wait_ge(d_nmx, u + 1)
                        for h in range(2):
                            ins = v.tensor_tensor(probs[b][:, 4 * h:4 * h + 4, 0:keys], sc[:, h, :, :],
                                                  spread(sm[b][:, 4 * h:4 * h + 4], keys), SUB)
                        ins.then_inc(d_sub, 1)
                    if b == 1 and live_tile(c // 2 + 2):
                        if c // 2 + 2 >= 1:
                            dve.wait_ge(d_turned, here + 2)
                        normalise(xn[0], here + 2 - k * TILES, 1, d_normed)
                    if live(c - 2):
                        ov = O_ps[:, 0:HP * 17].rearrange("p (h d) -> p h d", d=17)
                        dve.wait_ge(d_o, u - 1)
                        v.reciprocal(sm[b][:, 16:16 + HP], ov[:, :, 16]).then_inc(d_rden, 1)
                        dve.wait_ge(d_rden, u - 1)
                        for h in range(2):
                            half = slice(h * S, (h + 1) * S)
                            ins = v.tensor_tensor(on4[b][half, 0:HP * HD].rearrange("p (h d) -> p h d", d=HD),
                                                  ov[half, :, h * HD:(h + 1) * HD],
                                                  spread(sm[b][half, 16:16 + HP], HD), MUL)
                        ins.then_inc(d_on, 1)
                    if b == 1 and live_tile((c - 7) // 2):
                        dve.wait_ge(d_upd, 2 * t + (c - 7) // 2 + 1)
                        tile = 2 * t + (c - 7) // 2 - k * TILES
                        v.bn_stats(stats[:, bass.ds(tile * 6, 6)], xt(tile))

                run_slots(dve, k, dve_slot)
                link(v.memset(st_a[:, 0:1], 0.0))
                variance(st, mean[:, :], TILES, *ONCE)
                dve.wait_ge(stat_rstd, 6 + k)
            with dve.Fori(0, GROUP_TURNS) as t:
                for s in range(2):
                    normalise(xn[s], (2 * t + s) * G, G, f_normed)
                for s in range(2):
                    dve.wait_ge(f_logits, 2 * t + s + 1)
                    v.tensor_scalar(rl_all[:, bass.ds((2 * t + s) * G * E, G * E)], bank[s][1][:, 0:G * E], 1.0, None, MUL).then_inc(f_logits_s, 1)
            dve.wait_ge(f_logits_s, GROUPS)

            def best(dst, kd, logits, m):
                link(v.tensor_reduce(m, logits, AX_X, MAX))
                link(v.tensor_tensor(dst, logits, spread(m, E), ALU.is_ge))
                link(v.tensor_tensor(dst, dst, iota_sb[:, :].unsqueeze(1).to_broadcast([P, TILES, E]), MUL))
                link(v.tensor_reduce(kd, dst, AX_X, MAX))
                link(v.tensor_tensor(dst, dst, spread(kd, E), ALU.is_equal))

            best(r_1, st_b[:, 0:TILES], r_l0, st_a[:, 0:TILES])
            v.tensor_tensor(r_l, r_l0, spread(st_a[:, 0:TILES], E), SUB).then_inc(f_vec, 2)
            link(v.scalar_tensor_tensor(r_3, r_1, NEG, r_l0, MUL, ADD))
            best(r_2, st_b[:, 0:TILES], r_3, st_c[:, 0:TILES])
            link(v.tensor_tensor(r_1, r_1, r_2, ADD))
            dve.wait_ge(f_exp, 1)
            link(v.tensor_reduce(st_a[:, 0:TILES], r_e, AX_X, ADD))
            link(v.reciprocal(st_b[:, 0:TILES], st_a[:, 0:TILES]))
            link(v.tensor_tensor(r_2, r_e, spread(st_b[:, 0:TILES], E), MUL))
            link(v.tensor_tensor(r_1, r_1, r_2, MUL))
            link(v.tensor_reduce(st_a[:, 0:TILES], r_1, AX_X, ADD))
            link(v.tensor_scalar(st_c[:, 0:TILES], st_a[:, 0:TILES], 1e-9, None, ADD))
            link(v.reciprocal(st_b[:, 0:TILES], st_c[:, 0:TILES]))
            link(v.tensor_tensor(r_3, r_1, spread(st_b[:, 0:TILES], E), MUL))

            with dve.Fori(0, GROUPS) as g:
                v.tensor_copy(wst[:, :], r_3f[:, bass.ds(g * G * E, G * E)]).then_inc(f_wst, 1)

                def accumulate(e):
                    dve.wait_ge(f_down, E * g + e + 1)
                    dve.wait_ge(f_acc, (E + 1) * g + e + 1)
                    for j in range(G):
                        ins = v.scalar_tensor_tensor(yacc[:, j, :], wide[0][:, e % 2, j * C:(j + 1) * C],
                                                     wst[:, j * E + e:j * E + e + 1], yacc[:, j, :], MUL, ADD)
                    ins.then_inc(f_acc, 1)

                for k in range(E * FC):
                    if k == 2:
                        dve.wait_ge(f_yb, g + 1)
                        v.tensor_tensor(yacc[:, :, :].rearrange("p j c -> p (j c)"), wide[1][:, 1, :], xt(g * G, G),
                                        ADD).then_inc(f_acc, 1)
                    dve.wait_ge(f_silu, E * FC * g + k + 1)
                    v.scalar_tensor_tensor(hf[k % 2], bank[k % 2][1][:, :], col(UP_B + k), sg[k % 2], ADD,
                                           MUL).then_inc(f_h, 1)
                    if k >= 2 and k % 2 == 0:
                        accumulate(k // 2 - 1)
                accumulate(E - 1)
                dve.wait_ge(f_acc, (E + 1) * g + E + 1)
                v.tensor_scalar(xt(g * G, G), yacc[:, :, :].rearrange("p j c -> p (j c)"), 1.0, None, MUL).then_inc(f_upd, 1)
                dve.wait_ge(f_upd, g + 1)

        @block.tensor
        def _(pe):
            mm, ident_ap = nc.tensor.matmul, id_sb[:, :]

            def turn_groups(t, normed, turned, banks):
                for s in range(2):
                    pe.wait_ge(normed, 2 * t + s + 1)
                    for j in range(G):
                        ins = nc.tensor.transpose(banks[s][:, j * P:(j + 1) * P], xn[s][:, j, :], ident_ap)
                    ins.then_inc(turned, 1)

            pe.wait_ge(loaded, LOADED)
            pe.wait_ge(loaded_later, LATER)
            pe.wait_ge(vec, 1)
            def pe_tile_slot(t, c):
                u, s = 4 * t + c, c % 2
                if live_tile(c):
                    pe.wait_ge(a_normed, u + 1)
                    if live_tile(c - 1):
                        pe.wait_ge(a_lnT, u)
                    nc.tensor.transpose(T1_ps[:, 0:P], xn[s][:, 0, :], ident_ap)
                    for b in range(2):
                        ins = nc.tensor.transpose(T1_ps[0:CC, (1 + b) * P:(2 + b) * P], xn[s][:, 1 + b, 0:CC], ident_ap)
                    ins.then_inc(a_turned, 1)
                if live_tile(c - 4):
                    pe.wait_ge(a_pn, u - 3)
                    for h in range(2):
                        nc.tensor.transpose(T3_ps[:, h * P:(h + 1) * P], p0[s][:, h, 0:M], ident_ap)
                        ins = nc.tensor.transpose(T3_ps[0:S, (2 + h) * P:(3 + h) * P], p0[s][:, h, M:NK0], ident_ap)
                    ins.then_inc(a_pT, 1)
                if live_tile(c - 3):
                    q = 1 - s
                    pe.wait_ge(a_qTs, u - 2)
                    if live_tile(c - 4):
                        pe.wait_ge(a_exp, u - 3)
                    for h in range(2):
                        mm(S0_ps[:, h, 0:M], sel2_sb[:, :], mneg[:, bass.ds((u - 3) * M, M)], start=True,
                           stop=False, skip_group_check=True)
                    for h in range(2):
                        d = slice(h * HD0, (h + 1) * HD0)
                        for b in range(2):
                            tok = slice(b * S, (b + 1) * S)
                            mm(S0_ps[tok, h, 0:M], qT0[q][d, tok], kT0[q][d, P + b * M:P + (b + 1) * M],
                               start=False, stop=True, skip_group_check=True)
                            ins = mm(S0_ps[tok, h, M:NK0], qT0[q][d, tok], kT0[q][d, tok],
                                     start=False, stop=True, skip_group_check=True)
                    ins.then_inc(a_scores, 1)
                if live_tile(c - 2):
                    pe.wait_ge(a_qkn, u - 1)
                    if live_tile(c - 3):
                        pe.wait_ge(a_qTs, u - 2)
                    for i in range(4):
                        ins = nc.tensor.transpose(T2_ps[:, i * P:(i + 1) * P], qk0[s][:, i * P:(i + 1) * P], ident_ap)
                    ins.then_inc(a_qkT, 1)
                if live_tile(c - 4):
                    pe.wait_ge(a_pTs, u - 3)
                    pe.wait_ge(a_vals, u - 3)
                    if live_tile(c - 5):
                        pe.wait_ge(a_upd, u - 4)
                    for h in range(2):
                        d = slice(h * HD0, (h + 1) * HD0)
                        for b in range(2):
                            tok = slice(b * S, (b + 1) * S)
                            mm(OY_ps[d, tok], kvc[c % 4][:, b, P + h * HD0:P + (h + 1) * HD0],
                               pT0[s][:, h * P + b * S:h * P + (b + 1) * S], start=True, stop=False)
                            ins = mm(OY_ps[d, tok], qkl[c % 4][0:S, 256 + b * P + h * HD0:256 + b * P + (h + 1) * HD0],
                                     pT0[s][0:S, (2 + h) * P + b * S:(2 + h) * P + (b + 1) * S], start=False, stop=True)
                    ins.then_inc(a_oT, 1)
                if live_tile(c):
                    pe.wait_ge(a_lnT, u + 1)
                    if live_tile(c - 1):
                        pe.wait_ge(a_raw, u)
                        pe.wait_ge(a_vals, u)
                    for b in range(2):
                        mm(KV_ps[:, b, :], cnT[s][0:CC, b * M:(b + 1) * M], wkv0[:, :], start=True, stop=True)
                    mm(QL_ps[:, 0:256], lnT[s], wqkv0[:, 0:256], start=True, stop=True)
                    for b in range(2):
                        ins = mm(QL_ps[0:S, 256 + b * P:256 + (b + 1) * P], lnT[s][:, b * S:(b + 1) * S],
                                 wqkv0[:, 256:384], start=True, stop=True)
                    ins.then_inc(a_proj, 1)
                if live_tile(c - 4):
                    pe.wait_ge(a_oTs, u - 3)
                    mm(OY_ps[:, P:2 * P], oT0[s], wo0[:, :], start=True, stop=True).then_inc(a_y, 1)

            run_tiles(pe, pe_tile_slot)

            with pe.Fori(0, GROUP_TURNS) as t:
                turn_groups(t, b_normed, b_turned, [bank[0][0], bank[1][0]])
                for s in range(2):
                    pe.wait_ge(b_xT, 2 * t + s + 1)
                    mm(wide[s][:, 0, :], wqkv1[:, 0:P], xT[s][:, :], start=True, stop=True)
                    mm(wide[s][:, 1, :], wqkv1[:, P:2 * P], xT[s][:, :], start=True, stop=True).then_inc(b_qk, 1)
                    for j in range(G):
                        ins = mm(bank[s][0][:, j * P:(j + 1) * P], xT[s][:, j * P:(j + 1) * P], wqkv1[:, 2 * P:3 * P],
                                 start=True, stop=True)
                    ins.then_inc(b_v, 1)
                for s in range(2):
                    pe.wait_ge(b_q, 2 * t + s + 1)
                    pe.wait_ge(b_kv, 2 * t + s + 1)
                    for j in range(G):
                        for b in range(2):
                            q = slice(j * P + b * S, j * P + (b + 1) * S)
                            ins = mm(bank[s][1][b * S:(b + 1) * S, j * S:(j + 1) * S], bq[s][:, q], bk[s][:, q],
                                     start=True, stop=True)
                    ins.then_inc(b_scores, 1)
                for s in range(2):
                    pe.wait_ge(b_exp, 2 * t + s + 1)
                    for j in range(G):
                        ins = nc.tensor.transpose(wide[s][:, 1, j * P:(j + 1) * P], pbd[s][:, j * P:(j + 1) * P], ident_ap)
                    ins.then_inc(b_pT, 1)
                for s in range(2):
                    pe.wait_ge(b_pTs, 2 * t + s + 1)
                    for j in range(G):
                        ins = mm(bank[s][1][:, j * C:(j + 1) * C], bpT[s][:, j * P:(j + 1) * P], bv[s][:, j * P:(j + 1) * P],
                                 start=True, stop=True)
                    ins.then_inc(b_o, 1)

            with pe.Fori(0, GROUP_TURNS) as t:
                turn_groups(t, c_normed, c_turned, [bank[0][0], bank[1][0]])
            pe.wait_ge(c_zsum, 1)
            mm(bank[0][0][0:B, 0:E], zbn[:, :], wr2[:, :], start=True, stop=True).then_inc(c_logits, 1)
            pe.wait_ge(c_coef, 1)
            nc.tensor.transpose(bank[0][1][0:E, 0:B], coef[:, :], id_sb[0:B, 0:B]).then_inc(c_coefT, 1)
            pe.wait_ge(c_coef, 2)
            for c in range(CH0):
                ins = mm(bank[1][0][:, c * B:(c + 1) * B], esel_sb[:, c * P:(c + 1) * P], coefT[:, :], start=True, stop=True)
            ins.then_inc(c_spread, 1)
            pe.wait_ge(c_spread_s, 1)
            with pe.Fori(0, GROUP_TURNS) as t:
                for c in range(CH0):
                    for s in range(2):
                        if c >= 2:
                            pe.wait_ge(c_relu, 2 * (CH0 * t + c - 2) + s + 1)
                        mm(bank[s][c % 2][:, :], wdown2[:, c * P:(c + 1) * P], feat_T[:, bass.ds((2 * t + s) * GW, GW)],
                           start=True, stop=True).then_inc(c_h, 1)
                for s in range(2):
                    pe.wait_ge(c_hm, 2 * (CH0 * t + CH0 - 1) + s + 1)
                    pe.wait_ge(c_tok, 2 * t + s + 1)
                    for j in range(G):
                        y = wide[s][:, 0, j * C:(j + 1) * C]
                        for c in range(CH0):
                            mm(y, hr[s][:, c, j * P:(j + 1) * P], wup2[:, c, :], start=(c == 0), stop=False)
                        ins = mm(y, ctok[s][:, j * P:(j + 1) * P], bup2[:, :], start=False, stop=True)
                    ins.then_inc(c_y, 1)

            for k in range(2):
                keys, wo = (M, KX)[k], (wo4, wo5)[k]

                def pe_slot(t, c):
                    u, b, here = 4 * t + c, c % 2, 2 * t + c // 2
                    par = (c // 2 + 1) % 2
                    if live(c):
                        pe.wait_ge(d_qm, u + 1)
                        pe.wait_ge(d_qk, 2 * here + 2)
                        if live(c - 2):
                            pe.wait_ge(d_sub, u - 1)
                        if k == 1:
                            for h in range(2):
                                mm(S_ps[b][:, h, 0:4 * keys], qneg_sb[:, :], e64_sb[:, :], start=True, stop=False,
                                   skip_group_check=True)
                        for h in range(HP):
                            ins = mm(S_ps[b][:, h // 4, h % 4 * keys:(h % 4 + 1) * keys],
                                     big[c // 2 % 2][:, b, 2 * h:2 * h + 2, :],
                                     kT4[c // 2 % 2][:, b * keys:(b + 1) * keys],
                                     start=(k == 0), stop=True, skip_group_check=(k == 1))
                        ins.then_inc(d_scores, 1)
                    if live(c - 3):
                        pe.wait_ge(d_on, u - 2)
                        if b == 0 and live_tile(c // 2):
                            pe.wait_ge(d_v, here + 1)
                        elif b == 1 and live_tile(c // 2 + 1):
                            pe.wait_ge(d_qk, 2 * here + 4)
                        elif b == 0 and live(c - 6):
                            pe.wait_ge(d_ys, (c - 6) // 2 + 2 * t + 1)
                        elif live(c - 4):
                            pe.wait_ge(d_oTs, u - 3)
                        nc.tensor.transpose(A_ps[:, 384:512], on4[1 - b][:, :], ident_ap).then_inc(d_oT, 1)
                    if live(c - 2):
                        pe.wait_ge(d_pTs, 2 * u - 2)
                        pe.wait_ge(d_v, here)
                        if live(c - 3):
                            pe.wait_ge(d_on, u - 2)
                    if live(c - 1):
                        pe.wait_ge(d_exp, u)
                    for h in range(HP):
                        if live(c - 1):
                            ins = nc.tensor.transpose(T_ps[h // 4][0:keys, h % 4 * P:(h % 4 + 1) * P],
                                                      probs[1 - b][:, h, 0:keys], ident_ap)
                            if h % 4 == 3:
                                ins.then_inc(d_pT, 1)
                        if live(c - 2):
                            ins = mm(O_ps[:, h * 17:(h + 1) * 17], probsT[b][0:keys, h, :],
                                     vaug[(c - 2) // 2 % 2][0:keys, b, h, :], start=True, stop=True)
                            if h == HP - 1:
                                ins.then_inc(d_o, 1)
                        if h == 3 and b == 0 and live_tile(c // 2 + 1):
                            pe.wait_ge(d_normed, here + 2)
                            if live(c - 3):
                                pe.wait_ge(d_oTs, u - 2)
                            elif live_tile(c // 2):
                                pe.wait_ge(d_v, here + 1)
                            nc.tensor.transpose(A_ps[:, 0:P], xn[0][:, 0, :], ident_ap).then_inc(d_turned, 1)
                        if h == 3 and b == 1 and live(c - 5):
                            pe.wait_ge(d_oTs, u - 2 if live(c - 3) else u - 3)
                            for n in range(2):
                                for i in range(2):
                                    ins = mm(A_ps[n * S:(n + 1) * S, 256:256 + C],
                                             oT4[(c - 5) // 2 % 2][:, n, i * S:(i + 1) * S], wo[:, i, :],
                                             start=(i == 0), stop=(i == 1))
                            ins.then_inc(d_y, 1)
                    if b == 0 and live_tile(c // 2 + 1):
                        if k == 0:
                            pe.wait_ge(d_ctx[par], 16 * (t + (c // 2 + 1) // 2 + 1))
                        pe.wait_ge(d_xT, here + 2)
                        if k == 0:
                            mm(A_ps[:, P:P + 2 * keys], wk4[:, :], ctxT_s[par][:, :], start=True, stop=True)
                            ins = mm(A_ps[:, 0:P], wq4[:, :], xT[par][:, 0:P], start=True, stop=True)
                        else:
                            mm(A_ps[:, 0:P], wqkv5[:, 0:P], xg[par][:, :, 1:KX], start=True, stop=True)
                            ins = mm(A_ps[:, P:P + 2 * keys], wqkv5[:, P:2 * P], xg[par][:, :, :], start=True, stop=True)
                        ins.then_inc(d_proj, 1)
                    if b == 1 and live_tile(c // 2 + 1):
                        if live(c - 5):
                            pe.wait_ge(d_ys, (c - 5) // 2 + 2 * t + 1)
                        elif live(c - 3):
                            pe.wait_ge(d_oTs, u - 2)
                        pe.wait_ge(d_qk, 2 * here + 4)
                        for n in range(2):
                            lhs = ctxT_s[par][:, n * M:(n + 1) * M] if k == 0 else xg[par][:, n, :]
                            ins = mm(A_ps[0:keys, n * P:(n + 1) * P], lhs, wv4[:, :] if k == 0 else wqkv5[:, 2 * P:3 * P],
                                     start=True, stop=True)
                        ins.then_inc(d_vp, 1)

                run_slots(pe, k, pe_slot)
            with pe.Fori(0, GROUP_TURNS) as t:
                turn_groups(t, f_normed, f_turned, [bank[0][0], bank[1][0]])
                for s in range(2):
                    pe.wait_ge(f_xT, 4 * t + 2 * s + 2)
                    for j in range(G):
                        ins = mm(bank[s][1][:, j * E:(j + 1) * E], xT[s][:, j * P:(j + 1) * P], wr6[:, :], start=True, stop=True)
                    ins.then_inc(f_logits, 1)
            pe.wait_ge(f_logits_s, GROUPS)

            with pe.Fori(0, GROUPS) as g:
                xg_T = feat_T[:, bass.ds(g * GW, GW)]

                def gate_up(k):
                    mm(bank[k % 2][0][:, :], wgate6[:, k, :], xg_T, start=True, stop=True)
                    mm(bank[k % 2][1][:, :], wup6[:, k, :], xg_T, start=True, stop=True).then_inc(f_gu, 1)

                def down(k):
                    e, f = k // FC, k % FC
                    pe.wait_ge(f_h, E * FC * g + k + 1)
                    for j in range(G):
                        ins = mm(wide[0][:, e % 2, j * C:(j + 1) * C], hf[k % 2][:, j * P:(j + 1) * P], wdown6[:, k, :],
                                 start=(f == 0 and j == 0), stop=(f == FC - 1), skip_group_check=True)
                    if f == FC - 1:
                        ins.then_inc(f_down, 1)

                for k in range(E * FC + 1):
                    if k < E * FC:
                        gate_up(k)
                    if k == 0:
                        pe.wait_ge(f_wst, g + 1)
                        for j in range(G):
                            ins = nc.tensor.transpose(wide[1][0:E, 0, j * P:(j + 1) * P], wst[:, j * E:(j + 1) * E], ident_ap)
                        ins.then_inc(f_wT, 1)
                    if k == 1:
                        pe.wait_ge(f_wTs, g + 1)
                        for j in range(G):
                            ins = mm(wide[1][:, 1, j * C:(j + 1) * C], wTs[:, j * P:(j + 1) * P], bdown6[:, :],
                                     start=True, stop=True)
                        ins.then_inc(f_yb, 1)
                    if k >= 1:
                        down(k - 1)


def kernel(**inputs):
    import numpy as np
    import concourse.bacc as bacc
    from concourse.bass_utils import run_bass_kernel_spmd as run

    i = {k: np.asarray(a) for k, a in inputs.items()}
    f32 = np.float32
    bf16 = mybir.dt.np(mybir.dt.bfloat16)

    def column(a):
        c = np.zeros((P, 1), f32)
        c[:a.shape[0], 0] = a
        return c

    vectors = [column(i["L0_xattn_" + n]) for n in ("ln_x_g", "ln_x_b", "ln_l_g", "ln_l_b")]
    vectors += [column(np.tile(i["L0_xattn_" + n], 2)) for n in ("qn_g", "kn_g")]
    vectors += [column(i["L0_ffn_" + n]) for n in ("ln_g", "ln_b", "bn_g", "bn_b", "bn_mean", "bn_var")]
    vectors += [column(i["L1_xattn_bq"]), column(i["L1_xattn_bk"]), column(i["L1_attn_global_token"].reshape(C))]
    vectors += [i["L0_ffn_b_down"].reshape(CH0, P).T, i["L1_ffn_gate_b"].reshape(E * FC, P).T,
                i["L1_ffn_up_b"].reshape(E * FC, P).T]
    vectors += [column(i["L1_xattn_bv"].reshape(HP, 2, HD)[:, h].reshape(HP * HD)) for h in range(2)]
    row_vectors = np.stack([i["L0_xattn_bo"], i["L1_xattn_bo"], i["L1_attn_proj_b"]])
    
    def heads(w):
        w = w.reshape(HP, 2, HD, C).transpose(0, 2, 1, 3).reshape(HP * HD, 2, C)
        return np.concatenate([w, np.zeros_like(w)])

    part = np.arange(P)
    sel2 = (part[None, :] // S == np.arange(2)[:, None]).astype(bf16)
    qneg = np.where(part % S == S - 1, 0.0, NEG).astype(bf16)[None, :]
    e64 = np.tile(np.arange(S + 1) == S, 4).astype(bf16)[None, :]
    arrays = {
        "x": i["x"].reshape(TILES, P, C).transpose(1, 0, 2),
        "ctx": i["ctx_768"].transpose(1, 0, 2),
        "ctxT": i["ctx_768"].transpose(2, 0, 1).reshape(CC, B * M),
        "mask": i["mask_BxS2_bk0"].reshape(TILES, 2, M).transpose(1, 0, 2).reshape(2, TILES * M),
        "cols": np.concatenate(vectors, axis=1),
        "rows": np.broadcast_to(row_vectors[None], (P, 3, C)),
        "br": np.broadcast_to(i["L0_ffn_br"][None], (B, E)),
        "iota8": np.broadcast_to(np.arange(E, 0, -1).astype(f32)[None], (P, E)),
        "ident": np.eye(P, dtype=f32),
        "headmask": (part[:, None] // HD == np.arange(2 * HP)[None, :]).astype(f32),
        "sel2": sel2, "qneg": qneg, "e64": e64,
        "esel": (np.arange(E * H0)[None, :] // H0 == np.arange(E)[:, None]).astype(f32),
        "w_kv0": i["L0_xattn_Wkv"].T,
        "w_qkv0": np.concatenate([i["L0_xattn_Wq"].T, i["L0_xattn_Wlkv"].T], axis=1),
        "w_o0": i["L0_xattn_Wo"].T,
        "w_qkv1": i["L0_attn_W_qkv"].T,
        "w_r2": i["L0_ffn_Wr"],
        "w_down2": i["L0_ffn_W_down"].transpose(1, 0, 2).reshape(C, E * H0),
        "w_up2": i["L0_ffn_W_up"].reshape(CH0, P, C).transpose(1, 0, 2),
        "b_up2": i["L0_ffn_b_up"],
        "w_q4": i["L1_xattn_Wq"], "w_k4": i["L1_xattn_Wk"], "w_v4": i["L1_xattn_Wv"], "w_o4": heads(i["L1_xattn_Wo"]),
        "w_qkv5": i["L1_attn_qkv_w"].T, "w_o5": heads(i["L1_attn_proj_w"].T),
        "w_r6": i["L1_ffn_router_w"].T,
        "w_gate6": i["L1_ffn_gate_w"].reshape(E, C, FC, P).transpose(1, 0, 2, 3).reshape(C, E * FC, P),
        "w_up6": i["L1_ffn_up_w"].reshape(E, C, FC, P).transpose(1, 0, 2, 3).reshape(C, E * FC, P),
        "w_down6": i["L1_ffn_down_w"].reshape(E * FC, P, C).transpose(1, 0, 2),
        "b_down6": i["L1_ffn_down_b"],
    }
    arrays = {k: np.ascontiguousarray(a) for k, a in arrays.items()}
    nc = bacc.Bacc("TRN2", target_bir_lowering=False, num_devices=1)
    args = [nc.dram_tensor(f"in_{k}", a.shape, mybir.dt.from_np(a.dtype), kind="ExternalInput").ap()
            for k, a in arrays.items()]
    out = nc.dram_tensor("out", (P, TILES, C), F32, kind="ExternalOutput").ap()
    perceiver_kernel(nc, *args, out)
    got = run(nc, [{f"in_{k}": a for k, a in arrays.items()}], core_ids=[0])
    return got.results[0]["out"].transpose(1, 0, 2).reshape(B, S, C)
```

```python
from contextlib import ExitStack

import concourse.bass as bass
from concourse import mybir

ALU = mybir.AluOpType
ACT = mybir.ActivationFunctionType
F32 = mybir.dt.float32
F32R = mybir.dt.float32r
BF16 = mybir.dt.bfloat16
U8 = mybir.dt.uint8
AX_X = mybir.AxisListType.X

P = 128
B, S, C = 64, 64, 128
TILES = B * S // P
M, CC = 128, 96
G = 4
GW = G * P
GROUPS = TILES // G
EPS = 1e-5
RMS_EPS = 1e-8
NEG = -1e30
HD0 = 64
NK0 = M + S
HP, HD = 8, 8
SC0 = HD0 ** -0.5
SC1 = C ** -0.5
SC4 = 16 ** -0.5
SC5 = HD ** -0.5
E = 8
H0 = 64
CH0 = E * H0 // P
FC = 2
CHUNKS = 4
CT = TILES // CHUNKS
EARLY = TILES - CT
PAIR_TURNS = TILES // 2
GROUP_TURNS = GROUPS // 2

LNX_G, LNX_B, LNL_G, LNL_B, QN_G, KN_G, FLN_G, FLN_B, BN_G, BN_B, BN_M, BN_V, BQ4, BK4, GTOK = range(15)
BDOWN = 15
GATE_B = BDOWN + CH0
UP_B = GATE_B + E * FC
BV4H = UP_B + E * FC
NCOLS = BV4H + 2
BO0, BO4, BO5 = range(3)


def perceiver_kernel(nc, x, ctx, ctxT, mask, cols, rows, br, iota8, ident, headmask, sel2, qneg, e64, esel,
                     w_kv0, w_qkv0, w_o0, w_qkv1, w_r2, w_down2, w_up2, b_up2,
                     w_q4, w_k4, w_v4, w_o4, w_qkv5, w_o5, w_r6, w_gate6, w_up6, w_down6, b_down6, out):
    with ExitStack() as stack:
        def sb(name, shape, dt=F32):
            return stack.enter_context(nc.sbuf_tensor(name, shape, dt))

        def sem(name):
            return stack.enter_context(nc.semaphore(name))

        bank = [[stack.enter_context(nc.psum_tensor(f"bank{s}{i}", [P, 512], F32)) for i in range(2)] for s in range(2)]
        wide = [stack.enter_context(nc.psum_tensor(f"wide{s}", [P, 2, 512], F32)) for s in range(2)]

        with ExitStack() as before6:
            wgu6, ctx_sb, feat_T = [before6.enter_context(nc.sbuf_tensor(name, [P, width], F32)) for name, width in
                                    (("wgu6", 2 * E * FC * P), ("ctx_sb", B * CC), ("feat_T", TILES * P))]
        w_lo = sb("w_lo", [P, 2 * E * FC * P], F32R)
        w_hi = sb("w_hi", [P, 2 * E * FC * P], F32R)
        feat_hi = sb("feat_hi", [P, TILES * P], F32R)
        feat_lo = sb("feat_lo", [P, TILES * P], F32R)
        x_sb = sb("x_sb", [P, TILES * C])
        stats = sb("stats", [P, TILES * 6])
        cstats = sb("cstats", [P, B * 6])
        mean = sb("mean", [P, TILES])
        rstd = sb("rstd", [P, TILES])
        cmean = sb("cmean", [P, B])
        crstd = sb("crstd", [P, B])
        st_a = sb("st_a", [P, B])
        st_b = sb("st_b", [P, B])
        st_c = sb("st_c", [P, B])
        st_d = sb("st_d", [P, B])
        st_v = sb("st_v", [P, TILES])
        cst_v = sb("cst_v", [P, B])
        neg_half = sb("neg_half", [P, B])
        cols_sb = sb("cols_sb", [P, NCOLS])
        rows_sb = sb("rows_sb", [P, 3, C])
        br_sb = sb("br_sb", [B, E])
        iota_sb = sb("iota_sb", [P, E])
        id_sb = sb("id_sb", [P, P])
        hm_sb = sb("hm_sb", [P, 2 * HP])
        sel2_sb = sb("sel2_sb", [2, P], BF16)
        qneg_sb = sb("qneg_sb", [1, P], BF16)
        e64_sb = sb("e64_sb", [1, 4 * (S + 1)], BF16)
        esel_sb = sb("esel_sb", [E, E * H0])
        mask_sb = sb("mask_sb", [2, TILES * M], U8)
        mneg = sb("mneg", [2, TILES * M], BF16)
        wkv0 = sb("wkv0", [CC, 2 * C])
        wqkv0 = sb("wqkv0", [P, 3 * C])
        wo0 = sb("wo0", [P, C])
        wqkv1 = sb("wqkv1", [P, 3 * C])
        wr2 = sb("wr2", [P, E])
        wdown2 = sb("wdown2", [P, E * H0])
        wup2 = sb("wup2", [P, CH0, C])
        bup2 = sb("bup2", [E, C])
        wq4 = sb("wq4", [P, C])
        wk4 = sb("wk4", [CC, C])
        wv4 = sb("wv4", [CC, C])
        wo4 = sb("wo4", [P, 2, C])
        wqkv5 = sb("wqkv5", [P, 3 * C])
        wo5 = sb("wo5", [P, 2, C])
        wr6 = sb("wr6", [P, E])
        wdown6 = sb("wdown6", [P, E * FC, C])
        bdown6 = sb("bdown6", [E, C])
        gq0 = sb("gq0", [P, 1])
        bq4s = sb("bq4s", [P, 1])

        def col(i):
            return cols_sb[:, i:i + 1]

        def pairs(name, shape, dt=F32):
            return [sb(f"{name}{s}", shape, dt) for s in range(2)]

        xn = pairs("xn", [P, G, C])
        xT = pairs("xT", [P, GW])
        probs = pairs("probs", [P, HP, P])
        probsT = pairs("probsT", [P, HP, P])
        big = pairs("big", [P, 2, 2 * HP, S])
        sm = pairs("sm", [P, 64])

        loaded = sem("loaded")
        consts = sem("consts")
        vec = sem("vec")
        mask_ready, scale_ready = sem("mask_ready"), sem("scale_ready")
        chunk_loaded = [sem(f"chunk_loaded_{i}") for i in range(CHUNKS)]
        stat_var = sem("stat_var")
        stat_rstd = sem("stat_rstd")
        block = stack.enter_context(nc.Block())

        chunks = [(x_sb[:, i * CT * C:(i + 1) * CT * C].rearrange("p (t c) -> p t c", c=C), x[:, i * CT:(i + 1) * CT, :],
                   ctx_sb[:, i * 2 * CT * CC:(i + 1) * 2 * CT * CC].rearrange("p (b c) -> p b c", c=CC),
                   ctx[:, i * 2 * CT:(i + 1) * 2 * CT, :]) for i in range(CHUNKS)]
        loads = [(cols_sb[:, :], cols), (id_sb[:, :], ident), (wkv0[:, :], w_kv0), (wqkv0[:, :], w_qkv0),
                 (rows_sb[:, :, :], rows), (mask_sb[:, :], mask), (sel2_sb[:, :], sel2), (wo0[:, :], w_o0)]
        later = [(wqkv1[:, :], w_qkv1), (wr2[:, :], w_r2), (br_sb[:, :], br), (iota_sb[:, :], iota8),
                 (hm_sb[:, :], headmask), (qneg_sb[:, :], qneg), (e64_sb[:, :], e64), (esel_sb[:, :], esel),
                 (wdown2[:, :], w_down2), (wup2[:, :, :], w_up2),
                 (bup2[:, :], b_up2), (wq4[:, :], w_q4), (wk4[:, :], w_k4), (wv4[:, :], w_v4), (wo4[:, :, :], w_o4),
                 (wqkv5[:, :], w_qkv5),
                 (wo5[:, :, :], w_o5), (wr6[:, :], w_r6),
                 (wgu6[:, 0:E * FC * P].rearrange("p (a b) -> p a b", b=P), w_gate6),
                 (wgu6[:, E * FC * P:2 * E * FC * P].rearrange("p (a b) -> p a b", b=P), w_up6),
                 (wdown6[:, :, :], w_down6), (bdown6[:, :], b_down6)]
        LOADED = 16 * len(loads)
        loaded_later = sem("loaded_later")
        LATER = 16 * len(later)

        T1_ps, T2_ps, T3_ps, OY_ps = bank[0][0], bank[0][1], bank[1][0], bank[1][1]
        KV_ps, QL_ps = wide[0][:, 0, :].rearrange("p (b k) -> p b k", b=2), wide[0][:, 1, :]
        S0_ps = wide[1]
        lnT = [xT[s][:, 0:P] for s in range(2)]
        cnT = [xT[s][:, P:3 * P] for s in range(2)]
        qT0 = [xT[s][:, 3 * P:4 * P] for s in range(2)]
        flat = [[t[s][:, :, :].rearrange("p a b -> p (a b)") for s in range(2)] for t in (probs, probsT)]
        bigf = [big[s][:, :, :, :].rearrange("p a b c -> p (a b c)") for s in range(2)]
        p0 = [flat[0][s][:, 0:2 * NK0].rearrange("p (h k) -> p h k", h=2) for s in range(2)]
        kT0 = [flat[0][s][:, 512:896] for s in range(2)]
        oT0 = [flat[0][s][:, 896:1024] for s in range(2)]
        pT0 = [flat[1][s][:, 0:512] for s in range(2)]
        qk0 = [bigf[s][:, 0:512] for s in range(2)]
        sq = [bigf[s][:, 512:1024] for s in range(2)]
        kvc = [feat_T[:, i * 512:(i + 1) * 512].rearrange("p (b k) -> p b k", b=2) for i in range(4)]
        qkl = [feat_T[:, 2048 + i * 512:2048 + (i + 1) * 512] for i in range(4)]
        bq = [flat[0][s][:, 0:512] for s in range(2)]
        bk = [flat[0][s][:, 512:1024] for s in range(2)]
        bv = [flat[1][s][:, 0:512] for s in range(2)]
        bpT = [flat[1][s][:, 512:1024] for s in range(2)]
        pbd = [bigf[s][:, 0:512] for s in range(2)]
        bsub = [bigf[s][:, 512:768] for s in range(2)]
        bT_ps, bV_ps, bS_ps, bP_ps = bank[0][0], bank[0][1], bank[1][0], bank[1][1]
        bQ_ps, bK_ps, bO_ps = wide[0][:, 0, :], wide[0][:, 1, :], wide[1][:, 0, :]
        zsum = sb("zsum", [P, B])
        zbn = sb("zbn", [P, B])
        rt = sb("rt", [P, 8])
        rt64 = sb("rt64", [B, 4])
        lg = sb("lg", [B, E])
        lg2 = sb("lg2", [B, E])
        ex = sb("ex", [B, E])
        pick = sb("pick", [B, E])
        coef = sb("coef", [B, E])
        coefT = sb("coefT", [E, B])
        cspr = sb("cspr", [P, CH0 * B])
        hr = [bigf[s].rearrange("p (c n) -> p c n", c=CH0) for s in range(2)]
        ctok = [flat[0][s][0:E, 0:GW] for s in range(2)]
        ctxT_s = pairs("ctxT_s", [CC, 2 * M])
        kT4 = pairs("kT4", [P, 2 * M])
        vaug = pairs("vaug", [P, 2, HP, 17])
        on4 = pairs("on4", [P, P])
        oT4 = pairs("oT4", [P, 2, P])
        ysb = pairs("ysb", [P, C])
        S_ps = wide
        T_ps = bank[0]
        A_ps, O_ps = bank[1]
        xg = pairs("xg", [P, 2, S + 1])
        rl_all = sb("rl_all", [P, TILES * E])
        route = [sb(f"route{i}", [P, TILES * E]) for i in range(5)]
        r_l0 = rl_all[:, :].rearrange("p (t e) -> p t e", e=E)
        r_1, r_2, r_3, r_e, r_l = [r[:, :].rearrange("p (t e) -> p t e", e=E) for r in route]
        r_3f = route[2]
        wst = sb("wst", [P, G * E])
        wTs = flat[1][0][0:E, 0:GW]
        sg = [flat[0][0][:, 0:512], flat[0][0][:, 512:1024]]
        hf = [flat[0][1][:, 0:512], flat[0][1][:, 512:1024]]

        a_raw, a_vals = sem("a_raw"), sem("a_vals")
        a_normed, a_turned, a_lnT, a_proj, a_sq = sem("a_normed"), sem("a_turned"), sem("a_lnT"), sem("a_proj"), sem("a_sq")
        a_ss, a_ssm, a_rk, a_qkn, a_qkT = sem("a_ss"), sem("a_ssm"), sem("a_rk"), sem("a_qkn"), sem("a_qkT")
        a_qTs, a_scores, a_nmx, a_exp = sem("a_qTs"), sem("a_scores"), sem("a_nmx"), sem("a_exp")
        a_rden, a_pn, a_pT, a_pTs = sem("a_rden"), sem("a_pn"), sem("a_pT"), sem("a_pTs")
        a_oT, a_oTs, a_y, a_xb, a_upd = sem("a_oT"), sem("a_oTs"), sem("a_y"), sem("a_xb"), sem("a_upd")
        b_normed, b_turned, b_xT, b_qk, b_v = sem("b_normed"), sem("b_turned"), sem("b_xT"), sem("b_qk"), sem("b_v")
        b_q, b_k, b_vs, b_scores, b_nmx, b_sub = sem("b_q"), sem("b_k"), sem("b_vs"), sem("b_scores"), sem("b_nmx"), sem("b_sub")
        b_exp, b_den, b_rden, b_pT, b_pTs, b_o, b_upd = (sem("b_exp"), sem("b_den"), sem("b_rden"), sem("b_pT"),
                                                         sem("b_pTs"), sem("b_o"), sem("b_upd"))
        b_zero = sem("b_zero")
        c_normed, c_turned, c_z = sem("c_normed"), sem("c_turned"), sem("c_z")
        c_zsum, c_route, c_logits, c_exp, c_coef = sem("c_zsum"), sem("c_route"), sem("c_logits"), sem("c_exp"), sem("c_coef")
        c_coefT, c_spread, c_spread_s = sem("c_coefT"), sem("c_spread"), sem("c_spread_s")
        c_tok, c_h, c_relu, c_hm, c_y, c_upd = sem("c_tok"), sem("c_h"), sem("c_relu"), sem("c_hm"), sem("c_y"), sem("c_upd")
        d_ctx, d_normed, d_turned, d_xT, d_proj, d_qk = ([sem("d_ctx_0"), sem("d_ctx_1")], sem("d_normed"), sem("d_turned"), sem("d_xT"),
                                                         sem("d_proj"), sem("d_qk"))
        d_v, d_qm, d_scores, d_nmx, d_sub, d_exp = (sem("d_v"), sem("d_qm"), sem("d_scores"), sem("d_nmx"),
                                                    sem("d_sub"), sem("d_exp"))
        d_pT, d_pTs, d_o, d_rden, d_on, d_oT, d_oTs = (sem("d_pT"), sem("d_pTs"), sem("d_o"), sem("d_rden"),
                                                       sem("d_on"), sem("d_oT"), sem("d_oTs"))
        d_y, d_xb, d_upd, d_ys, d_vp = sem("d_y"), sem("d_xb"), sem("d_upd"), sem("d_ys"), sem("d_vp")
        d_ones, d_gtok, d_bq = sem("d_ones"), sem("d_gtok"), sem("d_bq")
        f_whi, f_parts, f_lo = sem("f_whi"), sem("f_parts"), sem("f_lo")
        f_normed, f_turned, f_xT, f_logits = sem("f_normed"), sem("f_turned"), sem("f_xT"), sem("f_logits")
        f_logits_s, f_vec, f_exp = sem("f_logits_s"), sem("f_vec"), sem("f_exp")
        f_wst, f_wT, f_wTs, f_yb = sem("f_wst"), sem("f_wT"), sem("f_wTs"), sem("f_yb")
        f_gu, f_silu, f_h, f_down, f_acc = sem("f_gu"), sem("f_silu"), sem("f_h"), sem("f_down"), sem("f_acc")
        stored = sem("stored")

        st = stats[:, :].rearrange("p (t k) -> p t k", k=6)
        cst = cstats[:, :].rearrange("p (t k) -> p t k", k=6)
        KX = S + 1
        KEYS = (M, KX)

        def xt(tile, n=1):
            return x_sb[:, bass.ds(tile * C, n * C)]

        def spread(ap, n):
            return ap.unsqueeze(len(ap.shape)).to_broadcast(list(ap.shape) + [n])

        UNITS = 2 * B
        RAMP, TURNS = 10, 12
        STAT_EARLY, STAT_LAST = RAMP + 4 * TURNS, B + 8

        def live(c):
            return 0 <= c < UNITS

        def live_pair(i):
            return 0 <= i < UNITS // 2

        def live_tile(i):
            return 0 <= i < TILES

        def nothing(c):
            pass

        def run_tiles(eng, slot, before=nothing):
            for c in range(-1, 5):
                before(c)
                slot(0, c)
            before(5)
            with eng.Fori(0, 6) as t:
                for c in range(5, 9):
                    slot(t, c)
            before(29)
            for c in range(29, TILES + 6):
                slot(0, c)

        def run_slots(eng, slot, before=nothing):
            for k in range(2):
                first = k * (B // 4)
                for c in range(-3 if k == 0 else RAMP + 4 * TURNS, k * B + RAMP):
                    before(c)
                    slot(0, c, None)
                before(k * B + RAMP)
                with eng.Fori(first, first + TURNS) as t:
                    for c in range(RAMP, RAMP + 4):
                        slot(t, c, k)
            for c in range(B + RAMP + 4 * TURNS, UNITS + 6):
                before(c)
                slot(0, c, None)

        def which(k, c):
            return c // B if k is None else k

        def live_group(c):
            return 0 <= c < GROUPS

        def run_groups(eng, slot, before=nothing):
            for c in range(-1, 2):
                before(c)
                slot(0, c)
            before(2)
            with eng.Fori(0, 2) as t:
                for c in range(2, 4):
                    slot(t, c)
            for c in range(6, GROUPS + 2):
                before(c)
                slot(0, c)

        def stat_chunk(i):
            return 2 * i + 1

        def stat_early(stage):
            return 2 * CHUNKS + 2 * stage + 1

        @block.sync
        def _(sp):
            for i, (x_dst, x_src, c_dst, c_src) in enumerate(chunks):
                sp.dma_start(x_dst, x_src).then_inc(chunk_loaded[i], 16)
                sp.dma_start(c_dst, c_src).then_inc(chunk_loaded[i], 16)
                if i == 0:
                    for dst, src in loads:
                        sp.dma_start(dst, src).then_inc(loaded, 16)
            for dst, src in later:
                sp.dma_start(dst, src).then_inc(loaded_later, 16)
            for s in range(2):
                sp.dma_start(ctxT_s[s][:, :], ctxT[:, s * 2 * M:(s + 1) * 2 * M]).then_inc(d_ctx[s], 16)
            with sp.Fori(1, PAIR_TURNS) as t:
                for s in range(2):
                    sp.wait_ge(d_vp, 2 * t + s - 1)
                    sp.dma_start(ctxT_s[s][:, :], ctxT[:, bass.ds((2 * t + s) * 2 * M, 2 * M)]).then_inc(d_ctx[s], 16)
            with sp.Fori(0, GROUPS) as g:
                sp.wait_ge(f_acc, (E + 1) * (g + 1))
                sp.dma_start(out[:, bass.ds(g * G, G), :],
                             xt(g * G, G).rearrange("p (t c) -> p t c", c=C)).then_inc(stored, 16)
            sp.wait_ge(stored, 16 * GROUPS)

        @block.gpsimd
        def _(pool):
            nc.gpsimd.memset(neg_half[:, :], -0.5).then_inc(consts, 1)
            pool.wait_ge(consts, 1)

            def power(n, dst, var):
                pool.wait_ge(stat_var, n)
                nc.gpsimd.tensor_tensor(dst, var, neg_half[:, 0:var.shape[1]], ALU.pow).then_inc(stat_rstd, 1)

            def power_chunk(i):
                power(stat_chunk(i), rstd[:, i * CT:(i + 1) * CT], st_v[:, i * CT:(i + 1) * CT])
                power(stat_chunk(i) + 1, crstd[:, 2 * i * CT:2 * (i + 1) * CT], cst_v[:, 2 * i * CT:2 * (i + 1) * CT])

            def power_early(stage):
                power(stat_early(stage), rstd[:, 0:EARLY], st_v[:, 0:EARLY])

            def power_last(stage):
                power(stat_early(stage) + 1, rstd[:, EARLY:TILES], st_v[:, EARLY:TILES])

            pool.wait_ge(loaded, LOADED)
            power_chunk(0)

            def pool_tile_slot(t, c):
                u = 4 * t + c
                if live_tile(c):
                    pool.wait_ge(a_normed, u + 1)
                    nc.gpsimd.tensor_tensor(xt(u), xt(u), rows_sb[:, BO0, :], ALU.add).then_inc(a_xb, 1)
                    pool.wait_ge(a_raw, u + 1)
                    nc.gpsimd.tensor_tensor(sq[c % 2][:, 0:256], qkl[c % 4][:, 0:256], qkl[c % 4][:, 0:256], ALU.mult)
                    pool.wait_ge(a_vals, u + 1)
                    nc.gpsimd.tensor_tensor(sq[c % 2][:, 256:512].rearrange("p (b k) -> p b k", b=2),
                                            kvc[c % 4][:, :, 0:P], kvc[c % 4][:, :, 0:P], ALU.mult).then_inc(a_sq, 1)
                    pool.wait_ge(a_ssm, u + 1)
                    nc.gpsimd.tensor_tensor(sm[c % 2][:, 16:24], sm[c % 2][:, 8:16], neg_half[:, 0:8],
                                            ALU.pow).then_inc(a_rk, 1)

            def pool_tile_besides(c):
                if 0 <= c < CHUNKS - 1:
                    power_chunk(c + 1)
                if c == 29:
                    power_early(0)

            run_tiles(pool, pool_tile_slot, pool_tile_besides)
            pool.wait_ge(loaded_later, LATER)
            power_last(0)
            for s in range(2):
                nc.gpsimd.memset(pbd[s], 0.0).then_inc(b_zero, 1)
            pool.wait_ge(a_normed, TILES)
            for i in range(2):
                half = slice(i * E * FC * P, (i + 1) * E * FC * P)
                nc.gpsimd.tensor_copy(w_hi[:, half], wgu6[:, half]).then_inc(f_whi, 1)
                pool.wait_ge(f_whi, i + 1)
                nc.gpsimd.tensor_tensor(w_lo[:, half], wgu6[:, half], w_hi[:, half].bitcast(F32),
                                        ALU.subtract).then_inc(f_parts, 1)
            power_early(1)
            power_last(1)
            pool.wait_ge(c_route, 1)
            nc.gpsimd.tensor_tensor(rt[:, 1:2], rt[:, 0:1], neg_half[:, 0:1], ALU.pow).then_inc(c_exp, 1)
            pool.wait_ge(c_spread_s, 1)
            with pool.Fori(0, GROUP_TURNS) as t:
                for s in range(2):
                    g = 2 * t + s
                    pool.wait_ge(c_h, 2 * CH0 * t + s + 1)
                    nc.gpsimd.tensor_copy(ctok[s].rearrange("p (b q) -> p b q", q=S),
                                          spread(coefT[:, bass.ds(g * 2 * G, 2 * G)], S)).then_inc(c_tok, 1)

            power_early(2)
            power_last(2)
            for s in range(2):
                nc.gpsimd.memset(vaug[s][:, :, :, 16:17], 1.0).then_inc(d_ones, 1)
                nc.gpsimd.memset(on4[s][:, HP * HD:P], 0.0).then_inc(d_ones, 1)

            def pool_slot(t, c, k):
                u, b, here = 4 * t + c, c % 2, 2 * t + c // 2
                par = (c // 2 + 1) % 2
                if b == 0 and live(c - 6):
                    pool.wait_ge(d_ys, 2 * t + (c - 6) // 2 + 1)
                    pool.wait_ge(d_xb, 2 * t + (c - 6) // 2 + 1)
                    tile = 2 * t + (c - 6) // 2 - which(k, c - 6) * TILES
                    nc.gpsimd.tensor_tensor(xt(tile), xt(tile), ysb[(c - 6) // 2 % 2][:, :], ALU.add).then_inc(d_upd, 1)
                if live_pair(c // 2 + 1):
                    pool.wait_ge(d_qk, 2 * here + 3)
                    if live(c - 2):
                        pool.wait_ge(d_scores, u - 1)
                    nc.gpsimd.tensor_tensor(
                        big[par][:, b, :, :],
                        xT[par][:, 256 + b * S:256 + (b + 1) * S].unsqueeze(1).to_broadcast([P, 2 * HP, S]),
                        spread(hm_sb[:, :], S), ALU.mult).then_inc(d_qm, 1)
                if b == 1 and live_pair(c // 2 + 2):
                    pool.wait_ge(d_normed, here + 3)
                    at = which(k, c + 3)
                    tile = here + 2 - at * TILES
                    nc.gpsimd.tensor_tensor(xt(tile), xt(tile), rows_sb[:, (BO4, BO5)[at], :], ALU.add).then_inc(d_xb, 1)

            def pool_besides(c):
                if c == STAT_EARLY:
                    power_early(3)
                if c == STAT_LAST:
                    power_last(3)
                if c == B + STAT_EARLY:
                    power_early(4)

            run_slots(pool, pool_slot, pool_besides)
            power_last(4)

        @block.scalar
        def _(act):
            ID, EXP = ACT.Identity, ACT.Exp
            act.wait_ge(loaded, LOADED)
            act.wait_ge(scale_ready, 1)
            def act_tile_slot(t, c):
                u, s = 4 * t + c, c % 2
                if live_tile(c):
                    act.wait_ge(a_turned, u + 1)
                    nc.scalar.activation(lnT[s], T1_ps[:, 0:P], ID, bias=col(LNL_B), scale=col(LNL_G))
                    nc.scalar.activation(cnT[s][0:CC, :], T1_ps[0:CC, P:3 * P], ID, bias=cols_sb[0:CC, LNX_B:LNX_B + 1],
                                         scale=cols_sb[0:CC, LNX_G:LNX_G + 1]).then_inc(a_lnT, 1)
                if live_tile(c - 4):
                    act.wait_ge(a_pT, u - 3)
                    nc.scalar.activation(pT0[s][:, 0:2 * P], T3_ps[:, 0:2 * P], ID)
                    nc.scalar.activation(pT0[s][0:S, 2 * P:4 * P], T3_ps[0:S, 2 * P:4 * P], ID).then_inc(a_pTs, 1)
                if live_tile(c - 3):
                    act.wait_ge(a_nmx, u - 2)
                    q = (c - 3) % 2
                    for h in range(2):
                        ins = nc.scalar.activation(p0[q][:, h, :], S0_ps[:, h, 0:NK0], EXP,
                                                   bias=sm[q][:, 24 + h:25 + h], scale=1.0,
                                                   accum_out=sm[q][:, 26 + h:27 + h])
                    ins.then_inc(a_exp, 1)
                if live_tile(c - 2):
                    act.wait_ge(a_qkT, u - 1)
                    nc.scalar.activation(qT0[s], T2_ps[:, 0:P], ID, scale=gq0[:, 0:1])
                    nc.scalar.activation(kT0[s], T2_ps[:, P:4 * P], ID).then_inc(a_qTs, 1)
                if live_tile(c - 4):
                    act.wait_ge(a_oT, u - 3)
                    nc.scalar.activation(oT0[s], OY_ps[:, 0:P], ID).then_inc(a_oTs, 1)
                if live_tile(c):
                    act.wait_ge(a_proj, u + 1)
                    nc.scalar.activation(kvc[c % 4], KV_ps, ID).then_inc(a_vals, 1)

            run_tiles(act, act_tile_slot)

            act.wait_ge(b_zero, 2)

            def act_group_slot(t, c):
                u, s = 2 * t + c, c % 2
                if live_group(c - 2):
                    act.wait_ge(b_pT, u - 1)
                    nc.scalar.activation(bpT[s], bP_ps[:, :], ID).then_inc(b_pTs, 1)
                if live_group(c):
                    act.wait_ge(b_turned, u + 1)
                    nc.scalar.activation(xT[s][:, :], bT_ps[:, :], ID).then_inc(b_xT, 1)
                if live_group(c - 1):
                    act.wait_ge(b_sub, u)
                    q = 1 - s
                    for b in range(2):
                        half = slice(b * S, (b + 1) * S)
                        ins = nc.scalar.activation(pbd[q].rearrange("p (j k) -> p j k", k=P)[half, :, half],
                                                   bsub[q].rearrange("p (j k) -> p j k", k=S)[half, :, :], EXP)
                    ins.then_inc(b_exp, 1)
                if live_group(c):
                    act.wait_ge(b_qk, u + 1)
                    nc.scalar.activation(bq[s], bQ_ps, ID, scale=SC1).then_inc(b_q, 1)
                    act.wait_ge(b_v, u + 1)
                    nc.scalar.activation(bv[s], bV_ps[:, :], ID).then_inc(b_vs, 1)

            run_groups(act, act_group_slot)

            def act_z_slot(t, c):
                u, s = 2 * t + c, c % 2
                if live_group(c):
                    act.wait_ge(c_turned, u + 1)
                    nc.scalar.activation(feat_T[:, bass.ds(u * GW, GW)], bank[s][0][:, :], ID,
                                         bias=col(FLN_B), scale=col(FLN_G)).then_inc(c_z, 1)

            run_groups(act, act_z_slot)
            act.wait_ge(c_route, 2)
            nc.scalar.activation(ex[:, :], lg2[:, :], EXP, accum_out=rt64[:, 2:3]).then_inc(c_exp, 1)
            with act.Fori(0, GROUP_TURNS) as t:
                for c in range(CH0):
                    for s in range(2):
                        act.wait_ge(c_h, 2 * (CH0 * t + c) + s + 1)
                        nc.scalar.activation(hr[s][:, c, :], bank[s][c % 2][:, :], ACT.Relu,
                                             bias=col(BDOWN + c)).then_inc(c_relu, 1)

            act.wait_ge(d_bq, 1)
            act.wait_ge(d_gtok, 2)
            act.wait_ge(d_ones, 4)
            def act_slot(t, c, k):
                u, b, here = 4 * t + c, c % 2, 2 * t + c // 2
                par = (c // 2 + 1) % 2
                if b == 0 and live_pair(c // 2):
                    keys = KEYS[which(k, c)]
                    act.wait_ge(d_vp, here + 1)
                    nc.scalar.activation(vaug[1 - par][0:keys, :, :, 0:16],
                                         A_ps[0:keys, 0:2 * P].rearrange("p (b h d) -> p b h d", b=2, d=16),
                                         ID).then_inc(d_v, 1)
                if b == 1 and live_pair(c // 2 + 1):
                    at = which(k, c + 1)
                    keys = KEYS[at]
                    act.wait_ge(d_proj, here + 2)
                    qT, kT = xT[par][:, 256:384], kT4[par][:, 0:2 * keys]
                    if at == 0:
                        nc.scalar.activation(qT, A_ps[:, 0:P], ID, bias=bq4s[:, 0:1], scale=SC4).then_inc(d_qk, 1)
                        nc.scalar.activation(kT, A_ps[:, P:P + 2 * keys], ID, bias=col(BK4)).then_inc(d_qk, 1)
                    else:
                        nc.scalar.activation(qT, A_ps[:, 0:P], ID, scale=SC5).then_inc(d_qk, 1)
                        nc.scalar.activation(kT, A_ps[:, P:P + 2 * keys], ID).then_inc(d_qk, 1)
                if live(c - 1):
                    act.wait_ge(d_sub, u)
                    keys = KEYS[which(k, c - 1)]
                    nc.scalar.activation(probs[1 - b][:, :, 0:keys], probs[1 - b][:, :, 0:keys], EXP).then_inc(d_exp, 1)
                if live(c - 3):
                    act.wait_ge(d_oT, u - 2)
                    dst = oT4[(c - 3) // 2 % 2]
                    if which(k, c - 3) == 0:
                        for h in range(2):
                            ins = nc.scalar.activation(dst[:, h, (1 - b) * S:(2 - b) * S], A_ps[:, 384 + h * S:384 + (h + 1) * S],
                                                       ID, bias=col(BV4H + h))
                    else:
                        ins = nc.scalar.activation(dst[:, :, (1 - b) * S:(2 - b) * S],
                                                       A_ps[:, 384:512].rearrange("p (h q) -> p h q", h=2), ID)
                    ins.then_inc(d_oTs, 1)
                for half in range(2):
                    if live(c - 1):
                        act.wait_ge(d_pT, 2 * u - 1 + half)
                        keys = KEYS[which(k, c - 1)]
                        nc.scalar.activation(probsT[1 - b][0:keys, 4 * half:4 * half + 4, :],
                                             T_ps[half][0:keys, :].rearrange("p (h q) -> p h q", q=P),
                                             ID).then_inc(d_pTs, 1)
                    if half == 0 and b == 0 and live_pair(c // 2 + 1):
                        act.wait_ge(d_turned, here + 2)
                        if which(k, c + 2) == 0:
                            nc.scalar.activation(xT[par][:, 0:P], A_ps[:, 0:P], ID).then_inc(d_xT, 1)
                        else:
                            nc.scalar.activation(xg[par][:, :, 1:KX], A_ps[:, 0:P].rearrange("p (b q) -> p b q", b=2),
                                                 ID).then_inc(d_xT, 1)
                    if half == 0 and b == 1 and live(c - 5):
                        act.wait_ge(d_y, (c - 5) // 2 + 2 * t + 1)
                        if live(c - 9):
                            act.wait_ge(d_upd, (c - 9) // 2 + 2 * t + 1)
                        nc.scalar.activation(ysb[(c - 5) // 2 % 2][:, :], A_ps[:, 256:256 + C], ID).then_inc(d_ys, 1)

            run_slots(act, act_slot)
            def act_router_slot(t, c):
                u, s = 2 * t + c, c % 2
                if live_group(c):
                    act.wait_ge(f_turned, u + 1)
                    nc.scalar.activation(xT[s][:, :], bank[s][0][:, :], ID).then_inc(f_xT, 1)
                    nc.scalar.activation(feat_hi[:, bass.ds(u * GW, GW)], bank[s][0][:, :], ID).then_inc(f_xT, 1)

            run_groups(act, act_router_slot)
            act.wait_ge(f_vec, 2)
            nc.scalar.activation(r_e, r_l, EXP).then_inc(f_exp, 1)

            def weights_out(g):
                act.wait_ge(f_wT, g + 1)
                nc.scalar.activation(wTs, wide[1][0:E, 0, :], ID).then_inc(f_wTs, 1)

            def gates(g, last=False):
                for k in range(E * FC):
                    if k == 12 and not last:
                        weights_out(g + 1)
                    act.wait_ge(f_gu, E * FC * g + k + 1)
                    nc.scalar.activation(sg[k % 2], bank[k % 2][0][:, :], ACT.Silu,
                                         bias=col(GATE_B + k)).then_inc(f_silu, 1)

            weights_out(0)
            with act.Fori(0, GROUPS - 1) as g:
                gates(g)
            gates(GROUPS - 1, last=True)

        @block.vector
        def _(dve):
            SUB, MUL, ADD, MAX = ALU.subtract, ALU.mult, ALU.add, ALU.max
            v = nc.vector
            done, variances = [0], [0]

            def link(ins):
                done[0] += 1
                ins.then_inc(vec, 1)
                dve.wait_ge(vec, done[0])

            def variance(src, mean_dst, scaled, lo, hi, width, a, b):
                src, mean_dst, scaled = src[:, lo:hi, :], mean_dst[:, lo:hi], scaled[:, lo:hi]
                a_, b_, c_, d_ = [st[:, lo:hi] for st in (st_a, st_b, st_c, st_d)]
                link(v.memset(a_, 0.0))
                v.tensor_tensor(a_, src[:, :, 1], src[:, :, 4], ADD)
                v.tensor_tensor(b_, src[:, :, 1], src[:, :, 4], SUB)
                link(v.tensor_tensor(c_, src[:, :, 2], src[:, :, 5], ADD))
                v.tensor_scalar(mean_dst, a_, 0.5, None, MUL)
                link(v.scalar_tensor_tensor(d_, b_, 0.25, b_, MUL, MUL))
                link(v.scalar_tensor_tensor(a_, c_, 1.0 / width, d_, MUL, ADD))
                v.tensor_scalar(scaled, a_, a, b, MUL, ADD).then_inc(stat_var, 1)
                variances[0] += 1
                dve.wait_ge(stat_var, variances[0])

            def variance_early(scale):
                variance(st, mean, st_v, 0, EARLY, C, *scale)

            def variance_last(scale):
                variance(st, mean, st_v, EARLY, TILES, C, *scale)

            def chunk_stats(i):
                dve.wait_ge(chunk_loaded[i], 32)
                for j in range(i * CT, (i + 1) * CT):
                    v.bn_stats(st[:, j, :], xt(j))
                variance(st, mean, st_v, i * CT, (i + 1) * CT, C, *TWICE)
                for j in range(2 * i * CT, 2 * (i + 1) * CT):
                    v.bn_stats(cst[:, j, :], ctx_sb[:, j * CC:(j + 1) * CC])
                variance(cst, cmean, cst_v, 2 * i * CT, 2 * (i + 1) * CT, CC, *ONCE)

            TWICE = (1.0 + EPS, EPS * EPS)
            ONCE = (1.0, EPS)

            def normalise(dst, tile, n, normed):
                for j in range(n):
                    ins = v.tensor_scalar(dst[:, j, :], xt(tile + j), mean[:, bass.ds(tile + j, 1)],
                                          rstd[:, bass.ds(tile + j, 1)], SUB, MUL)
                ins.then_inc(normed, 1)

            chunk_stats(0)
            dve.wait_ge(loaded, LOADED)
            v.scalar_tensor_tensor(gq0[:, :], col(QN_G), SC0, col(KN_G), MUL, MUL).then_inc(scale_ready, 1)
            dve.wait_ge(stat_rstd, stat_chunk(0) + 1)

            def dve_tile_slot(t, c):
                u, s = 4 * t + c, c % 2
                if live_tile(c - 5):
                    dve.wait_ge(a_y, u - 4)
                    dve.wait_ge(a_xb, u - 4)
                    v.tensor_tensor(xt(u - 5), OY_ps[:, P:2 * P], xt(u - 5), ADD).then_inc(a_upd, 1)
                if live_tile(c - 3):
                    dve.wait_ge(a_scores, u - 2)
                    q = 1 - s
                    v.tensor_reduce(sm[q][:, 24:26], S0_ps[:, :, 0:NK0], AX_X, MAX, negate=True).then_inc(a_nmx, 1)
                if live_tile(c - 1):
                    q = 1 - s
                    dve.wait_ge(a_sq, u)
                    v.tensor_reduce(sm[q][:, 0:8], sq[q].rearrange("p (h d) -> p h d", d=HD0), AX_X, ADD).then_inc(a_ss, 1)
                    dve.wait_ge(a_ss, u)
                    v.tensor_scalar(sm[q][:, 8:16], sm[q][:, 0:8], 1.0 / HD0, RMS_EPS * RMS_EPS, MUL, MAX).then_inc(a_ssm, 1)
                if live_tile(c + 1):
                    tile, q = u + 1, 1 - s
                    if live_tile(c - 1):
                        dve.wait_ge(a_turned, u)
                    for b in range(2):
                        v.tensor_scalar(xn[q][:, 1 + b, 0:CC], ctx_sb[:, bass.ds((2 * tile + b) * CC, CC)],
                                        cmean[:, bass.ds(2 * tile + b, 1)], crstd[:, bass.ds(2 * tile + b, 1)], SUB, MUL)
                    normalise(xn[q], tile, 1, a_normed)
                if live_tile(c - 3):
                    q = 1 - s
                    dve.wait_ge(a_exp, u - 2)
                    v.reciprocal(sm[q][:, 28:30], sm[q][:, 26:28]).then_inc(a_rden, 1)
                    dve.wait_ge(a_rden, u - 2)
                    for h in range(2):
                        ins = v.tensor_scalar(p0[q][:, h, :], p0[q][:, h, :], sm[q][:, 28 + h:29 + h], None, MUL)
                    ins.then_inc(a_pn, 1)
                if live_tile(c):
                    dve.wait_ge(a_proj, u + 1)
                    v.tensor_copy(qkl[c % 4][:, 0:256], QL_ps[:, 0:256])
                    v.tensor_copy(qkl[c % 4][0:S, 256:512], QL_ps[0:S, 256:512]).then_inc(a_raw, 1)
                if live_tile(c - 1):
                    q = 1 - s
                    dve.wait_ge(a_rk, u)
                    if live_tile(c - 3):
                        dve.wait_ge(a_qkT, u - 2)
                    v.tensor_tensor(qk0[q][:, 0:256].rearrange("p (h d) -> p h d", d=HD0),
                                    qkl[(c - 1) % 4][:, 0:256].rearrange("p (h d) -> p h d", d=HD0),
                                    spread(sm[q][:, 16:20], HD0), MUL)
                    v.tensor_tensor(qk0[q][:, 256:512].rearrange("p (b h d) -> p b h d", b=2, d=HD0),
                                    kvc[(c - 1) % 4][:, :, 0:P].rearrange("p b (h d) -> p b h d", d=HD0),
                                    spread(sm[q][:, 20:24].rearrange("p (b h) -> p b h", b=2), HD0), MUL).then_inc(a_qkn, 1)
                if live_tile(c - 5):
                    dve.wait_ge(a_upd, u - 4)
                    v.bn_stats(stats[:, bass.ds((u - 5) * 6, 6)], xt(u - 5))

            def dve_tile_besides(c):
                if c == 0:
                    v.tensor_scalar(mneg[:, :], mask_sb[:, :], -1.0, -NEG, ADD, MUL).then_inc(mask_ready, 1)
                    v.tensor_scalar(bq4s[:, :], col(BQ4), SC4, None, MUL).then_inc(d_bq, 1)
                    for s in range(2):
                        v.tensor_copy(xg[s][:, :, 0:1], spread(col(GTOK), 2).rearrange("p a b -> p b a")).then_inc(d_gtok, 1)
                if 0 <= c < CHUNKS - 1:
                    chunk_stats(c + 1)
                if c == 5:
                    dve.wait_ge(stat_rstd, stat_chunk(CHUNKS - 1) + 1)
                if c == 29:
                    variance_early(ONCE)

            run_tiles(dve, dve_tile_slot, dve_tile_besides)
            variance_last(ONCE)
            dve.wait_ge(loaded_later, LATER)
            dve.wait_ge(stat_rstd, stat_early(0))

            def dve_group_slot(t, c):
                u, s = 2 * t + c, c % 2
                if live_group(c - 1):
                    q = 1 - s
                    sc = bS_ps[:, 0:G * S].rearrange("p (j k) -> p j k", k=S)
                    dve.wait_ge(b_scores, u)
                    v.tensor_reduce(sm[q][:, 0:G], sc, AX_X, MAX).then_inc(b_nmx, 1)
                    dve.wait_ge(b_nmx, u)
                    v.tensor_tensor(bsub[q].rearrange("p (j k) -> p j k", k=S), sc, spread(sm[q][:, 0:G], S),
                                    SUB).then_inc(b_sub, 1)
                if live_group(c + 1):
                    if live_group(c - 1):
                        dve.wait_ge(b_turned, u)
                    normalise(xn[1 - s], (u + 1) * G, G, b_normed)
                if live_group(c - 2):
                    dve.wait_ge(b_o, u - 1)
                    for j in range(G):
                        ins = v.scalar_tensor_tensor(xt((u - 2) * G + j), bO_ps[:, j * C:(j + 1) * C],
                                                     sm[s][:, 8 + j:9 + j], xt((u - 2) * G + j), MUL, ADD)
                    ins.then_inc(b_upd, 1)
                if live_group(c):
                    dve.wait_ge(b_qk, u + 1)
                    v.tensor_copy(bk[s], bK_ps).then_inc(b_k, 1)
                if live_group(c - 1):
                    q = 1 - s
                    dve.wait_ge(b_exp, u)
                    v.tensor_reduce(sm[q][:, 4:4 + G], pbd[q].rearrange("p (j k) -> p j k", k=P), AX_X,
                                    ADD).then_inc(b_den, 1)
                    dve.wait_ge(b_den, u)
                    v.reciprocal(sm[q][:, 8:8 + G], sm[q][:, 4:4 + G]).then_inc(b_rden, 1)
                if live_group(c - 2):
                    dve.wait_ge(b_upd, u - 1)
                    for j in range(G):
                        v.bn_stats(stats[:, bass.ds(((u - 2) * G + j) * 6, 6)], xt((u - 2) * G + j))
                if live_group(c - 1):
                    dve.wait_ge(b_rden, u)

            def dve_group_besides(c):
                if c == 2:
                    dve.wait_ge(stat_rstd, stat_early(0) + 1)
                if c == EARLY // G + 2:
                    variance_early(TWICE)

            run_groups(dve, dve_group_slot, dve_group_besides)
            variance_last(TWICE)
            dve.wait_ge(stat_rstd, stat_early(1))

            def dve_z_slot(t, c):
                u, s = 2 * t + c, c % 2
                if live_group(c + 1):
                    if live_group(c - 1):
                        dve.wait_ge(c_turned, u)
                    normalise(xn[1 - s], (u + 1) * G, G, c_normed)
                if live_group(c - 1):
                    dve.wait_ge(c_z, u)
                    v.tensor_reduce(zsum[:, bass.ds((u - 1) * 2 * G, 2 * G)],
                                    feat_T[:, bass.ds((u - 1) * GW, GW)].rearrange("p (b q) -> p b q", q=S), AX_X, ADD)

            def dve_z_besides(c):
                if c == 2:
                    dve.wait_ge(stat_rstd, stat_early(1) + 1)

            run_groups(dve, dve_z_slot, dve_z_besides)
            v.tensor_scalar(rt[:, 0:1], col(BN_V), EPS, None, ADD).then_inc(c_route, 1)
            dve.wait_ge(c_exp, 1)
            link(v.tensor_scalar(rt[:, 2:3], col(BN_G), rt[:, 1:2], None, MUL))
            link(v.scalar_tensor_tensor(rt[:, 3:4], col(BN_M), rt[:, 2:3], col(BN_B), MUL, SUB))
            link(v.tensor_scalar(rt[:, 4:5], rt[:, 2:3], 1.0 / S, None, MUL))
            v.tensor_scalar(zbn[:, :], zsum[:, :], rt[:, 4:5], rt[:, 3:4], MUL, SUB).then_inc(c_zsum, 1)
            dve.wait_ge(c_logits, 1)
            link(v.tensor_tensor(lg[:, :], bank[0][0][0:B, 0:E], br_sb[:, :], ADD))
            link(v.tensor_reduce(rt64[:, 0:1], lg[:, :], AX_X, MAX))
            v.tensor_scalar(lg2[:, :], lg[:, :], rt64[:, 0:1], None, SUB).then_inc(c_route, 1)
            link(v.tensor_scalar(pick[:, :], lg[:, :], rt64[:, 0:1], None, ALU.is_ge))
            link(v.tensor_tensor(pick[:, :], pick[:, :], iota_sb[0:B, :], MUL))
            link(v.tensor_reduce(rt64[:, 1:2], pick[:, :], AX_X, MAX))
            dve.wait_ge(c_exp, 2)
            link(v.reciprocal(rt64[:, 3:4], rt64[:, 2:3]))
            v.tensor_scalar(coef[:, :], pick[:, :], rt64[:, 1:2], rt64[:, 3:4], ALU.is_equal, MUL).then_inc(c_coef, 1)
            dve.wait_ge(c_coefT, 1)
            v.tensor_copy(coefT[:, :], bank[0][1][0:E, 0:B]).then_inc(c_coef, 1)
            dve.wait_ge(c_spread, 1)
            v.tensor_copy(cspr[:, :], bank[1][0][:, 0:CH0 * B]).then_inc(c_spread_s, 1)
            dve.wait_ge(c_spread_s, 1)

            def experts(t):
                for c in range(CH0):
                    for s in range(2):
                        g = 2 * t + s
                        dve.wait_ge(c_relu, 2 * (CH0 * t + c) + s + 1)
                        v.tensor_tensor(hr[s][:, c, :].rearrange("p (b q) -> p b q", q=S),
                                        hr[s][:, c, :].rearrange("p (b q) -> p b q", q=S),
                                        spread(cspr[:, bass.ds(c * B + g * 2 * G, 2 * G)], S), MUL).then_inc(c_hm, 1)
                for s in range(2):
                    g = 2 * t + s
                    dve.wait_ge(c_y, 2 * t + s + 1)
                    v.tensor_tensor(xt(g * G, G), wide[s][:, 0, :], xt(g * G, G), ADD).then_inc(c_upd, 1)
                for s in range(2):
                    g = 2 * t + s
                    dve.wait_ge(c_upd, 2 * t + s + 1)
                    for j in range(G):
                        v.bn_stats(stats[:, bass.ds((g * G + j) * 6, 6)], xt(g * G + j))

            with dve.Fori(0, GROUP_TURNS - 1) as t:
                experts(t)
            variance_early(ONCE)
            experts(GROUP_TURNS - 1)
            variance_last(ONCE)
            dve.wait_ge(stat_rstd, stat_early(2))

            dve.wait_ge(d_ones, 4)
            def dve_slot(t, c, k):
                u, b, here = 4 * t + c, c % 2, 2 * t + c // 2
                if live(c):
                    keys = KEYS[which(k, c)]
                    sc = S_ps[b][:, :, 0:4 * keys].rearrange("p c (h k) -> p c h k", h=4)
                    dve.wait_ge(d_scores, u + 1)
                    v.tensor_reduce(sm[b][:, 0:HP].rearrange("p (c h) -> p c h", c=2), sc, AX_X, MAX).then_inc(d_nmx, 1)
                    dve.wait_ge(d_nmx, u + 1)
                    for h in range(2):
                        ins = v.tensor_tensor(probs[b][:, 4 * h:4 * h + 4, 0:keys], sc[:, h, :, :],
                                              spread(sm[b][:, 4 * h:4 * h + 4], keys), SUB)
                    ins.then_inc(d_sub, 1)
                if b == 1 and live_pair(c // 2 + 2):
                    if c // 2 + 2 >= 1:
                        dve.wait_ge(d_turned, here + 2)
                    normalise(xn[0], here + 2 - which(k, c + 3) * TILES, 1, d_normed)
                if live(c - 2):
                    ov = O_ps[:, 0:HP * 17].rearrange("p (h d) -> p h d", d=17)
                    dve.wait_ge(d_o, u - 1)
                    v.reciprocal(sm[b][:, 16:16 + HP], ov[:, :, 16]).then_inc(d_rden, 1)
                    dve.wait_ge(d_rden, u - 1)
                    for h in range(2):
                        half = slice(h * S, (h + 1) * S)
                        ins = v.tensor_tensor(on4[b][half, 0:HP * HD].rearrange("p (h d) -> p h d", d=HD),
                                              ov[half, :, h * HD:(h + 1) * HD],
                                              spread(sm[b][half, 16:16 + HP], HD), MUL)
                    ins.then_inc(d_on, 1)
                if b == 1 and live_pair((c - 7) // 2):
                    dve.wait_ge(d_upd, 2 * t + (c - 7) // 2 + 1)
                    tile = 2 * t + (c - 7) // 2 - which(k, c - 7) * TILES
                    v.bn_stats(stats[:, bass.ds(tile * 6, 6)], xt(tile))

            def dve_besides(c):
                if c == RAMP:
                    dve.wait_ge(stat_rstd, stat_early(2) + 1)
                if c in (STAT_EARLY, B + STAT_EARLY):
                    variance_early(ONCE)
                if c == B - 3:
                    dve.wait_ge(stat_rstd, stat_early(3))
                if c == STAT_LAST:
                    variance_last(ONCE)
                if c == B + RAMP:
                    dve.wait_ge(stat_rstd, stat_early(3) + 1)

            run_slots(dve, dve_slot, dve_besides)
            variance_last(ONCE)
            dve.wait_ge(stat_rstd, stat_early(4))
            def dve_router_slot(t, c):
                u, s = 2 * t + c, c % 2
                if live_group(c + 1):
                    if live_group(c - 1):
                        dve.wait_ge(f_turned, u)
                    normalise(xn[1 - s], (u + 1) * G, G, f_normed)
                if live_group(c - 1):
                    dve.wait_ge(f_xT, 2 * u)
                    v.tensor_tensor(feat_lo[:, bass.ds((u - 1) * GW, GW)], xT[1 - s][:, :],
                                    feat_hi[:, bass.ds((u - 1) * GW, GW)].bitcast(F32), SUB).then_inc(f_lo, 1)
                    dve.wait_ge(f_logits, u)
                    v.tensor_scalar(rl_all[:, bass.ds((u - 1) * G * E, G * E)], bank[1 - s][1][:, 0:G * E], 1.0, None,
                                    MUL).then_inc(f_logits_s, 1)

            def dve_router_besides(c):
                if c == 2:
                    dve.wait_ge(stat_rstd, stat_early(4) + 1)

            run_groups(dve, dve_router_slot, dve_router_besides)
            dve.wait_ge(f_logits_s, GROUPS)

            def best(dst, kd, logits, m):
                link(v.tensor_reduce(m, logits, AX_X, MAX))
                link(v.tensor_tensor(dst, logits, spread(m, E), ALU.is_ge))
                link(v.tensor_tensor(dst, dst, iota_sb[:, :].unsqueeze(1).to_broadcast([P, TILES, E]), MUL))
                link(v.tensor_reduce(kd, dst, AX_X, MAX))
                link(v.tensor_tensor(dst, dst, spread(kd, E), ALU.is_equal))

            best(r_1, st_b[:, 0:TILES], r_l0, st_a[:, 0:TILES])
            v.tensor_tensor(r_l, r_l0, spread(st_a[:, 0:TILES], E), SUB).then_inc(f_vec, 2)
            link(v.scalar_tensor_tensor(r_3, r_1, NEG, r_l0, MUL, ADD))
            best(r_2, st_b[:, 0:TILES], r_3, st_c[:, 0:TILES])
            link(v.tensor_tensor(r_1, r_1, r_2, ADD))
            dve.wait_ge(f_exp, 1)
            link(v.tensor_reduce(st_a[:, 0:TILES], r_e, AX_X, ADD))
            link(v.reciprocal(st_b[:, 0:TILES], st_a[:, 0:TILES]))
            link(v.tensor_tensor(r_2, r_e, spread(st_b[:, 0:TILES], E), MUL))
            link(v.tensor_tensor(r_1, r_1, r_2, MUL))
            link(v.tensor_reduce(st_a[:, 0:TILES], r_1, AX_X, ADD))
            link(v.tensor_scalar(st_c[:, 0:TILES], st_a[:, 0:TILES], 1e-9, None, ADD))
            link(v.reciprocal(st_b[:, 0:TILES], st_c[:, 0:TILES]))
            link(v.tensor_tensor(r_3, r_1, spread(st_b[:, 0:TILES], E), MUL))

            def group_weights(g):
                v.tensor_scalar(wst[:, :], r_3f[:, bass.ds(g * G * E, G * E)], 1.0, None, MUL).then_inc(f_wst, 1)

            def hidden(g, k):
                dve.wait_ge(f_silu, E * FC * g + k + 1)
                v.scalar_tensor_tensor(hf[k % 2], bank[k % 2][1][:, :], col(UP_B + k), sg[k % 2], ADD, MUL).then_inc(f_h, 1)

            def accumulate(g, e):
                dve.wait_ge(f_down, E * g + e + 1)
                dve.wait_ge(f_acc, (E + 1) * g + e + 1)
                for j in range(G):
                    ins = v.scalar_tensor_tensor(xt(g * G + j), wide[0][:, e % 2, j * C:(j + 1) * C],
                                                 r_3f[:, bass.ds((g * G + j) * E + e, 1)], xt(g * G + j), MUL, ADD)
                ins.then_inc(f_acc, 1)

            def experts6(g, last=False):
                for k in range(1, E * FC + 1):
                    if k == 2:
                        dve.wait_ge(f_yb, g + 1)
                        v.tensor_tensor(xt(g * G, G), wide[1][:, 1, :], xt(g * G, G), ADD).then_inc(f_acc, 1)
                    if k == 8 and not last:
                        group_weights(g + 1)
                    if k < E * FC:
                        hidden(g, k)
                    elif not last:
                        hidden(g + 1, 0)
                    if k % 2 == 0:
                        accumulate(g, k // 2 - 1)

            group_weights(0)
            hidden(0, 0)
            with dve.Fori(0, GROUPS - 1) as g:
                experts6(g)
            experts6(GROUPS - 1, last=True)

        @block.tensor
        def _(pe):
            mm, ident_ap = nc.tensor.matmul, id_sb[:, :]

            def turn_group(t, c, normed, turned):
                u, s = 2 * t + c, c % 2
                pe.wait_ge(normed, u + 1)
                for j in range(G):
                    ins = nc.tensor.transpose(bank[s][0][:, j * P:(j + 1) * P], xn[s][:, j, :], ident_ap)
                ins.then_inc(turned, 1)

            pe.wait_ge(loaded, LOADED)
            def pe_tile_slot(t, c):
                u, s = 4 * t + c, c % 2
                if live_tile(c):
                    pe.wait_ge(a_normed, u + 1)
                    if live_tile(c - 1):
                        pe.wait_ge(a_lnT, u)
                    nc.tensor.transpose(T1_ps[:, 0:P], xn[s][:, 0, :], ident_ap)
                    for b in range(2):
                        ins = nc.tensor.transpose(T1_ps[0:CC, (1 + b) * P:(2 + b) * P], xn[s][:, 1 + b, 0:CC], ident_ap)
                    ins.then_inc(a_turned, 1)
                if live_tile(c - 4):
                    pe.wait_ge(a_pn, u - 3)
                    for h in range(2):
                        nc.tensor.transpose(T3_ps[:, h * P:(h + 1) * P], p0[s][:, h, 0:M], ident_ap)
                        ins = nc.tensor.transpose(T3_ps[0:S, (2 + h) * P:(3 + h) * P], p0[s][:, h, M:NK0], ident_ap)
                    ins.then_inc(a_pT, 1)
                if live_tile(c - 5):
                    pe.wait_ge(a_oTs, u - 4)
                    mm(OY_ps[:, P:2 * P], oT0[1 - s], wo0[:, :], start=True, stop=True).then_inc(a_y, 1)
                if live_tile(c - 3):
                    q = 1 - s
                    pe.wait_ge(a_qTs, u - 2)
                    if live_tile(c - 4):
                        pe.wait_ge(a_exp, u - 3)
                    for h in range(2):
                        mm(S0_ps[:, h, 0:M], sel2_sb[:, :], mneg[:, bass.ds((u - 3) * M, M)], start=True,
                           stop=False, skip_group_check=True)
                    for h in range(2):
                        d = slice(h * HD0, (h + 1) * HD0)
                        for b in range(2):
                            tok = slice(b * S, (b + 1) * S)
                            mm(S0_ps[tok, h, 0:M], qT0[q][d, tok], kT0[q][d, P + b * M:P + (b + 1) * M],
                               start=False, stop=True, skip_group_check=True)
                            ins = mm(S0_ps[tok, h, M:NK0], qT0[q][d, tok], kT0[q][d, tok],
                                     start=False, stop=True, skip_group_check=True)
                    ins.then_inc(a_scores, 1)
                if live_tile(c - 2):
                    pe.wait_ge(a_qkn, u - 1)
                    if live_tile(c - 3):
                        pe.wait_ge(a_qTs, u - 2)
                    for i in range(4):
                        ins = nc.tensor.transpose(T2_ps[:, i * P:(i + 1) * P], qk0[s][:, i * P:(i + 1) * P], ident_ap)
                    ins.then_inc(a_qkT, 1)
                if live_tile(c - 4):
                    pe.wait_ge(a_pTs, u - 3)
                    pe.wait_ge(a_vals, u - 3)
                    if live_tile(c - 5):
                        pe.wait_ge(a_upd, u - 4)
                    for h in range(2):
                        d = slice(h * HD0, (h + 1) * HD0)
                        for b in range(2):
                            tok = slice(b * S, (b + 1) * S)
                            mm(OY_ps[d, tok], kvc[c % 4][:, b, P + h * HD0:P + (h + 1) * HD0],
                               pT0[s][:, h * P + b * S:h * P + (b + 1) * S], start=True, stop=False)
                            ins = mm(OY_ps[d, tok], qkl[c % 4][0:S, 256 + b * P + h * HD0:256 + b * P + (h + 1) * HD0],
                                     pT0[s][0:S, (2 + h) * P + b * S:(2 + h) * P + (b + 1) * S], start=False, stop=True)
                    ins.then_inc(a_oT, 1)
                if live_tile(c):
                    pe.wait_ge(a_lnT, u + 1)
                    if live_tile(c - 1):
                        pe.wait_ge(a_raw, u)
                        pe.wait_ge(a_vals, u)
                    for b in range(2):
                        mm(KV_ps[:, b, :], cnT[s][0:CC, b * M:(b + 1) * M], wkv0[:, :], start=True, stop=True)
                    mm(QL_ps[:, 0:256], lnT[s], wqkv0[:, 0:256], start=True, stop=True)
                    for b in range(2):
                        ins = mm(QL_ps[0:S, 256 + b * P:256 + (b + 1) * P], lnT[s][:, b * S:(b + 1) * S],
                                 wqkv0[:, 256:384], start=True, stop=True)
                    ins.then_inc(a_proj, 1)

            def pe_tile_besides(c):
                if c == 3:
                    pe.wait_ge(mask_ready, 1)

            run_tiles(pe, pe_tile_slot, pe_tile_besides)
            pe.wait_ge(loaded_later, LATER)

            def pe_group_slot(t, c):
                u, s = 2 * t + c, c % 2
                if live_group(c):
                    pe.wait_ge(b_normed, u + 1)
                    if live_group(c - 1):
                        pe.wait_ge(b_xT, u)
                    for j in range(G):
                        ins = nc.tensor.transpose(bT_ps[:, j * P:(j + 1) * P], xn[s][:, j, :], ident_ap)
                    ins.then_inc(b_turned, 1)
                if live_group(c - 2):
                    pe.wait_ge(b_exp, u - 1)
                    for j in range(G):
                        ins = nc.tensor.transpose(bP_ps[:, j * P:(j + 1) * P], pbd[s][:, j * P:(j + 1) * P], ident_ap)
                    ins.then_inc(b_pT, 1)
                if live_group(c - 1):
                    q = 1 - s
                    pe.wait_ge(b_q, u)
                    pe.wait_ge(b_k, u)
                    if live_group(c - 2):
                        pe.wait_ge(b_sub, u - 1)
                    for j in range(G):
                        for b in range(2):
                            tok = slice(j * P + b * S, j * P + (b + 1) * S)
                            ins = mm(bS_ps[b * S:(b + 1) * S, j * S:(j + 1) * S], bq[q][:, tok], bk[q][:, tok],
                                     start=True, stop=True)
                    ins.then_inc(b_scores, 1)
                if live_group(c - 2):
                    pe.wait_ge(b_pTs, u - 1)
                    if live_group(c - 3):
                        pe.wait_ge(b_upd, u - 2)
                    for j in range(G):
                        ins = mm(bO_ps[:, j * C:(j + 1) * C], bpT[s][:, j * P:(j + 1) * P], bv[s][:, j * P:(j + 1) * P],
                                 start=True, stop=True)
                    ins.then_inc(b_o, 1)
                if live_group(c):
                    pe.wait_ge(b_xT, u + 1)
                    mm(bQ_ps, wqkv1[:, 0:P], xT[s][:, :], start=True, stop=True)
                    mm(bK_ps, wqkv1[:, P:2 * P], xT[s][:, :], start=True, stop=True).then_inc(b_qk, 1)
                    if live_group(c - 1):
                        pe.wait_ge(b_vs, u)
                    for j in range(G):
                        ins = mm(bV_ps[:, j * P:(j + 1) * P], xT[s][:, j * P:(j + 1) * P], wqkv1[:, 2 * P:3 * P],
                                 start=True, stop=True)
                    ins.then_inc(b_v, 1)

            run_groups(pe, pe_group_slot)

            def pe_z_slot(t, c):
                if live_group(c):
                    if live_group(c - 2):
                        pe.wait_ge(c_z, 2 * t + c - 1)
                    turn_group(t, c, c_normed, c_turned)

            run_groups(pe, pe_z_slot)
            pe.wait_ge(c_zsum, 1)
            mm(bank[0][0][0:B, 0:E], zbn[:, :], wr2[:, :], start=True, stop=True).then_inc(c_logits, 1)
            pe.wait_ge(c_coef, 1)
            nc.tensor.transpose(bank[0][1][0:E, 0:B], coef[:, :], id_sb[0:B, 0:B]).then_inc(c_coefT, 1)
            pe.wait_ge(c_coef, 2)
            for c in range(CH0):
                ins = mm(bank[1][0][:, c * B:(c + 1) * B], esel_sb[:, c * P:(c + 1) * P], coefT[:, :], start=True, stop=True)
            ins.then_inc(c_spread, 1)
            pe.wait_ge(c_spread_s, 1)
            with pe.Fori(0, GROUP_TURNS) as t:
                for c in range(CH0):
                    for s in range(2):
                        if c >= 2:
                            pe.wait_ge(c_relu, 2 * (CH0 * t + c - 2) + s + 1)
                        mm(bank[s][c % 2][:, :], wdown2[:, c * P:(c + 1) * P], feat_T[:, bass.ds((2 * t + s) * GW, GW)],
                           start=True, stop=True).then_inc(c_h, 1)
                for s in range(2):
                    pe.wait_ge(c_hm, 2 * (CH0 * t + CH0 - 1) + s + 1)
                    pe.wait_ge(c_tok, 2 * t + s + 1)
                    for j in range(G):
                        y = wide[s][:, 0, j * C:(j + 1) * C]
                        for c in range(CH0):
                            mm(y, hr[s][:, c, j * P:(j + 1) * P], wup2[:, c, :], start=(c == 0), stop=False)
                        ins = mm(y, ctok[s][:, j * P:(j + 1) * P], bup2[:, :], start=False, stop=True)
                    ins.then_inc(c_y, 1)

            def pe_slot(t, c, k):
                u, b, here = 4 * t + c, c % 2, 2 * t + c // 2
                par = (c // 2 + 1) % 2
                if live(c):
                    at = which(k, c)
                    keys = KEYS[at]
                    pe.wait_ge(d_qm, u + 1)
                    pe.wait_ge(d_qk, 2 * here + 2)
                    if live(c - 2):
                        pe.wait_ge(d_sub, u - 1)
                    if at == 1:
                        for h in range(2):
                            mm(S_ps[b][:, h, 0:4 * keys], qneg_sb[:, :], e64_sb[:, :], start=True, stop=False,
                               skip_group_check=True)
                    for h in range(HP):
                        ins = mm(S_ps[b][:, h // 4, h % 4 * keys:(h % 4 + 1) * keys],
                                 big[c // 2 % 2][:, b, 2 * h:2 * h + 2, :],
                                 kT4[c // 2 % 2][:, b * keys:(b + 1) * keys],
                                 start=(at == 0), stop=True, skip_group_check=(at == 1))
                    ins.then_inc(d_scores, 1)
                if live(c - 3):
                    pe.wait_ge(d_on, u - 2)
                    if b == 0 and live_pair(c // 2):
                        pe.wait_ge(d_v, here + 1)
                    elif b == 1 and live_pair(c // 2 + 1):
                        pe.wait_ge(d_qk, 2 * here + 4)
                    elif b == 0 and live(c - 6):
                        pe.wait_ge(d_ys, (c - 6) // 2 + 2 * t + 1)
                    elif live(c - 4):
                        pe.wait_ge(d_oTs, u - 3)
                    nc.tensor.transpose(A_ps[:, 384:512], on4[1 - b][:, :], ident_ap).then_inc(d_oT, 1)
                if live(c - 2):
                    pe.wait_ge(d_pTs, 2 * u - 2)
                    pe.wait_ge(d_v, here)
                    if live(c - 3):
                        pe.wait_ge(d_on, u - 2)
                if live(c - 1):
                    pe.wait_ge(d_exp, u)
                for h in range(HP):
                    if live(c - 1):
                        keys = KEYS[which(k, c - 1)]
                        ins = nc.tensor.transpose(T_ps[h // 4][0:keys, h % 4 * P:(h % 4 + 1) * P],
                                                  probs[1 - b][:, h, 0:keys], ident_ap)
                        if h % 4 == 3:
                            ins.then_inc(d_pT, 1)
                    if live(c - 2):
                        keys = KEYS[which(k, c - 2)]
                        ins = mm(O_ps[:, h * 17:(h + 1) * 17], probsT[b][0:keys, h, :],
                                 vaug[(c - 2) // 2 % 2][0:keys, b, h, :], start=True, stop=True)
                        if h == HP - 1:
                            ins.then_inc(d_o, 1)
                    if h == 3 and b == 0 and live_pair(c // 2 + 1):
                        pe.wait_ge(d_normed, here + 2)
                        if live(c - 3):
                            pe.wait_ge(d_oTs, u - 2)
                        elif live_pair(c // 2):
                            pe.wait_ge(d_v, here + 1)
                        nc.tensor.transpose(A_ps[:, 0:P], xn[0][:, 0, :], ident_ap).then_inc(d_turned, 1)
                    if h == 3 and b == 1 and live(c - 5):
                        wo = (wo4, wo5)[which(k, c - 5)]
                        pe.wait_ge(d_oTs, u - 2 if live(c - 3) else u - 3)
                        for i in range(2):
                            ins = mm(A_ps[:, 256:256 + C], oT4[(c - 5) // 2 % 2][:, i, :], wo[:, i, :],
                                     start=(i == 0), stop=(i == 1))
                        ins.then_inc(d_y, 1)
                if b == 0 and live_pair(c // 2 + 1):
                    at = which(k, c + 2)
                    keys = KEYS[at]
                    if at == 0:
                        pe.wait_ge(d_ctx[par], 16 * (t + (c // 2 + 1) // 2 + 1))
                    pe.wait_ge(d_xT, here + 2)
                    if at == 0:
                        mm(A_ps[:, P:P + 2 * keys], wk4[:, :], ctxT_s[par][:, :], start=True, stop=True)
                        ins = mm(A_ps[:, 0:P], wq4[:, :], xT[par][:, 0:P], start=True, stop=True)
                    else:
                        mm(A_ps[:, 0:P], wqkv5[:, 0:P], xg[par][:, :, 1:KX], start=True, stop=True)
                        ins = mm(A_ps[:, P:P + 2 * keys], wqkv5[:, P:2 * P], xg[par][:, :, :], start=True, stop=True)
                    ins.then_inc(d_proj, 1)
                if b == 1 and live_pair(c // 2 + 1):
                    at = which(k, c + 1)
                    keys = KEYS[at]
                    if live(c - 5):
                        pe.wait_ge(d_ys, (c - 5) // 2 + 2 * t + 1)
                    elif live(c - 3):
                        pe.wait_ge(d_oTs, u - 2)
                    pe.wait_ge(d_qk, 2 * here + 4)
                    for n in range(2):
                        lhs = ctxT_s[par][:, n * M:(n + 1) * M] if at == 0 else xg[par][:, n, :]
                        ins = mm(A_ps[0:keys, n * P:(n + 1) * P], lhs, wv4[:, :] if at == 0 else wqkv5[:, 2 * P:3 * P],
                                 start=True, stop=True)
                    ins.then_inc(d_vp, 1)

            def keep_clock(n):
                for _ in range(n):
                    nc.tensor.transpose(T_ps[1][:, 0:P], ident_ap, ident_ap)

            def pe_besides(c):
                if c == -2:
                    keep_clock(40)
                if c == 0:
                    keep_clock(16)

            run_slots(pe, pe_slot, pe_besides)
            def pe_router_slot(t, c):
                u, q = 2 * t + c, (c - 1) % 2
                if live_group(c):
                    if live_group(c - 2):
                        pe.wait_ge(f_xT, 2 * u - 2)
                        pe.wait_ge(f_lo, u - 1)
                    turn_group(t, c, f_normed, f_turned)
                if live_group(c - 1):
                    pe.wait_ge(f_xT, 2 * u)
                    if live_group(c - 3):
                        pe.wait_ge(f_logits_s, u - 2)
                    for j in range(G):
                        ins = mm(bank[q][1][:, j * E:(j + 1) * E], xT[q][:, j * P:(j + 1) * P], wr6[:, :], start=True, stop=True)
                    ins.then_inc(f_logits, 1)

            run_groups(pe, pe_router_slot)
            pe.wait_ge(f_logits_s, GROUPS)


            def gate_up(g, k):
                hi, lo = feat_hi[:, bass.ds(g * GW, GW)], feat_lo[:, bass.ds(g * GW, GW)]
                for i in range(2):
                    chunk = slice((i * E * FC + k) * P, (i * E * FC + k + 1) * P)
                    mm(bank[k % 2][i][:, :], w_hi[:, chunk], hi, start=True, stop=False)
                    mm(bank[k % 2][i][:, :], w_hi[:, chunk], lo, start=False, stop=False)
                    ins = mm(bank[k % 2][i][:, :], w_lo[:, chunk], hi, start=False, stop=True)
                ins.then_inc(f_gu, 1)

            def down(g, k):
                e, f = k // FC, k % FC
                pe.wait_ge(f_h, E * FC * g + k + 1)
                for j in range(G):
                    ins = mm(wide[0][:, e % 2, j * C:(j + 1) * C], hf[k % 2][:, j * P:(j + 1) * P], wdown6[:, k, :],
                             start=(f == 0 and j == 0), stop=(f == FC - 1), skip_group_check=True)
                if f == FC - 1:
                    ins.then_inc(f_down, 1)

            def weights_turned(g):
                pe.wait_ge(f_wst, g + 1)
                for j in range(G):
                    ins = nc.tensor.transpose(wide[1][0:E, 0, j * P:(j + 1) * P], wst[:, j * E:(j + 1) * E], ident_ap)
                ins.then_inc(f_wT, 1)

            def down_biases(g):
                pe.wait_ge(f_wTs, g + 1)
                for j in range(G):
                    ins = mm(wide[1][:, 1, j * C:(j + 1) * C], wTs[:, j * P:(j + 1) * P], bdown6[:, :],
                             start=True, stop=True)
                ins.then_inc(f_yb, 1)

            def group_products(g, last=False):
                for k in range(E * FC):
                    if k + 1 < E * FC:
                        gate_up(g, k + 1)
                    elif not last:
                        gate_up(g + 1, 0)
                    down(g, k)
                    if k == 10 and not last:
                        weights_turned(g + 1)
                    if k == 13 and not last:
                        down_biases(g + 1)

            pe.wait_ge(f_parts, 2)
            pe.wait_ge(f_lo, GROUPS)
            gate_up(0, 0)
            weights_turned(0)
            down_biases(0)
            with pe.Fori(0, GROUPS - 1) as g:
                group_products(g)
            group_products(GROUPS - 1, last=True)


def kernel(**inputs):
    import numpy as np
    import concourse.bacc as bacc
    from concourse.bass_utils import run_bass_kernel_spmd as run

    i = {k: np.asarray(a) for k, a in inputs.items()}
    f32 = np.float32
    bf16 = mybir.dt.np(mybir.dt.bfloat16)

    def column(a):
        c = np.zeros((P, 1), f32)
        c[:a.shape[0], 0] = a
        return c

    vectors = [column(i["L0_xattn_" + n]) for n in ("ln_x_g", "ln_x_b", "ln_l_g", "ln_l_b")]
    vectors += [column(np.tile(i["L0_xattn_" + n], 2)) for n in ("qn_g", "kn_g")]
    vectors += [column(i["L0_ffn_" + n]) for n in ("ln_g", "ln_b", "bn_g", "bn_b", "bn_mean", "bn_var")]
    vectors += [column(i["L1_xattn_bq"]), column(i["L1_xattn_bk"]), column(i["L1_attn_global_token"].reshape(C))]
    vectors += [i["L0_ffn_b_down"].reshape(CH0, P).T, i["L1_ffn_gate_b"].reshape(E * FC, P).T,
                i["L1_ffn_up_b"].reshape(E * FC, P).T]
    vectors += [column(i["L1_xattn_bv"].reshape(HP, 2, HD)[:, h].reshape(HP * HD)) for h in range(2)]
    row_vectors = np.stack([i["L0_xattn_bo"], i["L1_xattn_bo"], i["L1_attn_proj_b"]])
    
    def heads(w):
        w = w.reshape(HP, 2, HD, C).transpose(0, 2, 1, 3).reshape(HP * HD, 2, C)
        return np.concatenate([w, np.zeros_like(w)])

    part = np.arange(P)
    sel2 = (part[None, :] // S == np.arange(2)[:, None]).astype(bf16)
    qneg = np.where(part % S == S - 1, 0.0, NEG).astype(bf16)[None, :]
    e64 = np.tile(np.arange(S + 1) == S, 4).astype(bf16)[None, :]
    arrays = {
        "x": i["x"].reshape(TILES, P, C).transpose(1, 0, 2),
        "ctx": i["ctx_768"].transpose(1, 0, 2),
        "ctxT": i["ctx_768"].transpose(2, 0, 1).reshape(CC, B * M),
        "mask": i["mask_BxS2_bk0"].reshape(TILES, 2, M).transpose(1, 0, 2).reshape(2, TILES * M),
        "cols": np.concatenate(vectors, axis=1),
        "rows": np.broadcast_to(row_vectors[None], (P, 3, C)),
        "br": np.broadcast_to(i["L0_ffn_br"][None], (B, E)),
        "iota8": np.broadcast_to(np.arange(E, 0, -1).astype(f32)[None], (P, E)),
        "ident": np.eye(P, dtype=f32),
        "headmask": (part[:, None] // HD == np.arange(2 * HP)[None, :]).astype(f32),
        "sel2": sel2, "qneg": qneg, "e64": e64,
        "esel": (np.arange(E * H0)[None, :] // H0 == np.arange(E)[:, None]).astype(f32),
        "w_kv0": i["L0_xattn_Wkv"].T,
        "w_qkv0": np.concatenate([i["L0_xattn_Wq"].T, i["L0_xattn_Wlkv"].T], axis=1),
        "w_o0": i["L0_xattn_Wo"].T,
        "w_qkv1": i["L0_attn_W_qkv"].T,
        "w_r2": i["L0_ffn_Wr"],
        "w_down2": i["L0_ffn_W_down"].transpose(1, 0, 2).reshape(C, E * H0),
        "w_up2": i["L0_ffn_W_up"].reshape(CH0, P, C).transpose(1, 0, 2),
        "b_up2": i["L0_ffn_b_up"],
        "w_q4": i["L1_xattn_Wq"], "w_k4": i["L1_xattn_Wk"], "w_v4": i["L1_xattn_Wv"], "w_o4": heads(i["L1_xattn_Wo"]),
        "w_qkv5": i["L1_attn_qkv_w"].T, "w_o5": heads(i["L1_attn_proj_w"].T),
        "w_r6": i["L1_ffn_router_w"].T,
        "w_gate6": i["L1_ffn_gate_w"].reshape(E, C, FC, P).transpose(1, 0, 2, 3).reshape(C, E * FC, P),
        "w_up6": i["L1_ffn_up_w"].reshape(E, C, FC, P).transpose(1, 0, 2, 3).reshape(C, E * FC, P),
        "w_down6": i["L1_ffn_down_w"].reshape(E * FC, P, C).transpose(1, 0, 2),
        "b_down6": i["L1_ffn_down_b"],
    }
    arrays = {k: np.ascontiguousarray(a) for k, a in arrays.items()}
    nc = bacc.Bacc("TRN2", target_bir_lowering=False, num_devices=1)
    args = [nc.dram_tensor(f"in_{k}", a.shape, mybir.dt.from_np(a.dtype), kind="ExternalInput").ap()
            for k, a in arrays.items()]
    out = nc.dram_tensor("out", (P, TILES, C), F32, kind="ExternalOutput").ap()
    perceiver_kernel(nc, *args, out)
    got = run(nc, [{f"in_{k}": a for k, a in arrays.items()}], core_ids=[0])
    return got.results[0]["out"].transpose(1, 0, 2).reshape(B, S, C)
```
